# Optimizing a Trainium2 kernel written in Bass

```python
import numpy as np
import jax
import jax.numpy as jnp

def _softmax(x, axis=-1):
    return jax.nn.softmax(x, axis=axis)

def _gelu(x):
    return jax.nn.gelu(x, approximate=True)

def _silu(x):
    return jax.nn.silu(x)

def _sigmoid(x):
    return jax.nn.sigmoid(x)

def _layernorm(x, axis=-1, eps=1e-05):
    m = jnp.mean(x, axis=axis, keepdims=True)
    v = jnp.var(x, axis=axis, keepdims=True)
    return (x - m) / jnp.sqrt(v + eps)

def _scatter_add(tgt, idx, src, axis=0):
    return tgt.at[idx].add(src)

def _segment_sum(src, seg, n):
    return jax.ops.segment_sum(src, seg, n)
kernel_name = 'mk_seq_preln_d1_jaxref_r8_046dd5'

def setup_inputs(seed: int=0):
    np.random.seed(seed)
    _w = jnp.asarray

    def _L0_attn_setup():
        import jax, jax.numpy as jnp
        import numpy as np
        NH = 16
        D = 128
        C = 64
        EPS = 1e-12

        def _l2norm(x):
            n = jnp.linalg.norm(x, axis=-1, keepdims=True)
            return x / jnp.maximum(n, EPS)
        key = jax.random.key(seed)
        ks = jax.random.split(key, 12)
        B, L, H = (4, 512, 256)
        std = 0.02
        f32 = jnp.float32
        inp = {'hidden_states': jax.random.normal(ks[0], (B, L, H), f32), 'q_w': jax.random.normal(ks[1], (NH * D, H), f32) * std, 'q_b': jnp.zeros((NH * D,), f32), 'k_w': jax.random.normal(ks[2], (NH * D, H), f32) * std, 'k_b': jnp.zeros((NH * D,), f32), 'v_w': jax.random.normal(ks[3], (NH * D, H), f32) * std, 'v_b': jnp.zeros((NH * D,), f32), 'a_w': jax.random.normal(ks[4], (NH, H), f32) * std, 'a_b': jnp.zeros((NH,), f32), 'b_w': jax.random.normal(ks[5], (NH, H), f32) * std, 'b_b': jnp.zeros((NH,), f32), 'og_w': jax.random.normal(ks[6], (NH * D, H), f32) * std, 'o_w': jax.random.normal(ks[7], (H, NH * D), f32) * std, 'o_b': jnp.zeros((H,), f32)}
        return inp
    _L0_attn_in = _L0_attn_setup()

    def _L0_ffn_setup():
        import jax, jax.numpy as jnp
        import numpy as np
        B, S, D, H = (8, 512, 256, 640)

        def ternarize_weight(w):
            abs_mean = jnp.maximum(jnp.mean(jnp.abs(w)), 1e-05)
            thr = 0.7 * abs_mean
            one = jnp.ones((), dtype=w.dtype)
            q = jnp.where(w > thr, one, jnp.where(w < -thr, -one, jnp.zeros((), dtype=w.dtype)))
            return w + jax.lax.stop_gradient(q * abs_mean - w)
        key = jax.random.key(seed)
        k1, k2, k3 = jax.random.split(key, 3)
        x = jax.random.normal(k1, (B, S, D), dtype=jnp.float32)
        w_fc = jax.random.normal(k2, (H, D), dtype=jnp.float32) / np.sqrt(D).astype(np.float32)
        w_proj = jax.random.normal(k3, (D, H), dtype=jnp.float32) / np.sqrt(H).astype(np.float32)
        return {'x': x, 'w_fc': w_fc, 'w_proj': w_proj}
    _L0_ffn_in = _L0_ffn_setup()
    _d = {'L0_attn_hidden_states': _L0_attn_in['hidden_states'], 'L0_attn_q_w': _L0_attn_in['q_w'], 'L0_attn_q_b': _L0_attn_in['q_b'], 'L0_attn_k_w': _L0_attn_in['k_w'], 'L0_attn_k_b': _L0_attn_in['k_b'], 'L0_attn_v_w': _L0_attn_in['v_w'], 'L0_attn_v_b': _L0_attn_in['v_b'], 'L0_attn_a_w': _L0_attn_in['a_w'], 'L0_attn_a_b': _L0_attn_in['a_b'], 'L0_attn_b_w': _L0_attn_in['b_w'], 'L0_attn_b_b': _L0_attn_in['b_b'], 'L0_attn_og_w': _L0_attn_in['og_w'], 'L0_attn_o_w': _L0_attn_in['o_w'], 'L0_attn_o_b': _L0_attn_in['o_b'], 'L0_ffn_w_fc': _L0_ffn_in['w_fc'], 'L0_ffn_w_proj': _L0_ffn_in['w_proj']}
    _x0 = _d['L0_attn_hidden_states']
    _d['L0_attn_hidden_states'] = jax.random.normal(jax.random.fold_in(jax.random.key(seed), 1), (8, 512, 256), dtype=_x0.dtype)
    del _x0
    return _d

def reference(L0_attn_hidden_states, L0_attn_q_w, L0_attn_q_b, L0_attn_k_w, L0_attn_k_b, L0_attn_v_w, L0_attn_v_b, L0_attn_a_w, L0_attn_a_b, L0_attn_b_w, L0_attn_b_b, L0_attn_og_w, L0_attn_o_w, L0_attn_o_b, L0_ffn_w_fc, L0_ffn_w_proj):

    def _L0_attn_ref(hidden_states, q_w, q_b, k_w, k_b, v_w, v_b, a_w, a_b, b_w, b_b, og_w, o_w, o_b):
        import jax, jax.numpy as jnp
        import numpy as np
        NH = 16
        D = 128
        C = 64
        EPS = 1e-12

        def _l2norm(x):
            n = jnp.linalg.norm(x, axis=-1, keepdims=True)
            return x / jnp.maximum(n, EPS)
        B, L, H = hidden_states.shape
        nh, d, c = (NH, D, C)
        hs = hidden_states
        q = (hs @ q_w.T + q_b).reshape(B, L, nh, d)
        k = (hs @ k_w.T + k_b).reshape(B, L, nh, d)
        v = (hs @ v_w.T + v_b).reshape(B, L, nh, d)
        beta = jax.nn.softplus(hs @ b_w.T + b_b)
        scale = float(d) ** 0.5
        qn = _l2norm(q / scale)
        kn = _l2norm(k / scale)
        gv = beta[..., None] * v
        nchunks = L // c

        def to_chunks(x):
            return x.reshape(B, nchunks, c, nh, d).transpose(0, 1, 3, 2, 4)
        qc, kc, gvc = (to_chunks(qn), to_chunks(kn), to_chunks(gv))
        attn = jnp.einsum('bnhid,bnhjd->bnhij', qc, kc)
        pos = jnp.arange(c, dtype=jnp.float32)
        dist = jnp.clip(pos[None, :] - pos[:, None], 0.0, None)
        decay = jnp.exp(-0.1 * dist)
        causal = pos[None, :] <= pos[:, None]
        mask = jnp.where(causal, decay, 0.0)
        out = jnp.einsum('bnhij,bnhjd->bnhid', attn * mask, gvc)
        out = out.transpose(0, 1, 3, 2, 4).reshape(B, L, nh * d)
        gate = jax.nn.silu(hs @ og_w.T)
        out = out * gate
        return out @ o_w.T + o_b

    def _L0_ffn_ref(x, w_fc, w_proj):
        import jax, jax.numpy as jnp
        import numpy as np
        B, S, D, H = (8, 512, 256, 640)

        def ternarize_weight(w):
            abs_mean = jnp.maximum(jnp.mean(jnp.abs(w)), 1e-05)
            thr = 0.7 * abs_mean
            one = jnp.ones((), dtype=w.dtype)
            q = jnp.where(w > thr, one, jnp.where(w < -thr, -one, jnp.zeros((), dtype=w.dtype)))
            return w + jax.lax.stop_gradient(q * abs_mean - w)
        h = jnp.einsum('bsd,hd->bsh', x, ternarize_weight(w_fc))
        h = jnp.square(jax.nn.relu(h))
        return jnp.einsum('bsh,dh->bsd', h, ternarize_weight(w_proj))
    x = L0_attn_hidden_states
    x = x + _L0_attn_ref(_layernorm(x, axis=-1), L0_attn_q_w, L0_attn_q_b, L0_attn_k_w, L0_attn_k_b, L0_attn_v_w, L0_attn_v_b, L0_attn_a_w, L0_attn_a_b, L0_attn_b_w, L0_attn_b_b, L0_attn_og_w, L0_attn_o_w, L0_attn_o_b)
    x = x + _L0_ffn_ref(_layernorm(x, axis=-1), L0_ffn_w_fc, L0_ffn_w_proj)
    return x

_drawn_inputs = setup_inputs


def setup_inputs(seed=0):
    import zlib

    import numpy as np

    out = dict(_drawn_inputs(seed))
    spreads = {'L0_attn_q_b': (0.0, 0.8),
     'L0_attn_k_b': (0.0, 0.8),
     'L0_attn_v_b': (0.0, 0.8),
     'L0_attn_a_b': (0.0, 0.1),
     'L0_attn_b_b': (0.0, 0.8),
     'L0_attn_o_b': (0.0, 0.304)}
    factors = {'L0_attn_q_w': 3.185,
     'L0_attn_k_w': 3.582,
     'L0_attn_v_w': 3.574,
     'L0_attn_b_w': 8.0,
     'L0_attn_og_w': 3.13,
     'L0_attn_o_w': 3.091}
    for name, (base, spread) in spreads.items():
        noise = np.random.default_rng([zlib.crc32(name.encode()), seed]).standard_normal(out[name].shape)
        drawn = base * np.exp(spread * noise) if base else spread * noise
        out[name] = jnp.asarray(drawn.astype(out[name].dtype))
    for name, factor in factors.items():
        out[name] = (out[name] * factor).astype(out[name].dtype)
    return out
```

```python
from contextlib import ExitStack

import concourse.bass as bass
from concourse import mybir

ALU = mybir.AluOpType
ACT = mybir.ActivationFunctionType
AX_X = mybir.AxisListType.X
F32 = mybir.dt.float32
F16 = mybir.dt.float16
BF16 = mybir.dt.bfloat16
I32 = mybir.dt.int32

P = 128
TOK = 8 * 512
HID = 256
KH = HID // P
HEADS = 16
WIDE = HEADS * P
CHUNK = 64
BLK = 512
TILES = BLK // P
NBLK = TOK // BLK
NTILE = TOK // P
GROUP = 4
GW = GROUP * P
FFN = 640
KF = FFN // P
LN_CHUNK = 8
UNITS = NBLK * HEADS
NORM_STEPS = 14
RSQRT_GUESS = 0x5F3759DF
LN_EPS = 1e-5
L2_EPS = 1e-12

ds = bass.ds


def low(n):
    return isinstance(n, int) and n <= 0


def build(nc, x, wq, wk, wv, wg, wo, wb, bq, bk, bv, bv_row, bb, bo, wfc, wpr, out):
    x_v = x.rearrange("(b t p) h -> b p t h", t=TILES, p=P)
    x_c = x.rearrange("(c t p) h -> c p t h", t=LN_CHUNK, p=P)
    out_v = out.rearrange("(b t p) h -> b p t h", t=TILES, p=P)
    mid = nc.dram_tensor("mid_rows", [NBLK, P, TILES * HID], F32, kind="Internal").ap()

    with ExitStack() as whole:
        def sb(name, shape, dt, ctx=whole):
            return ctx.enter_context(nc.sbuf_tensor(name, shape, dt))

        def pb(name, shape, ctx, dt=F32):
            return ctx.enter_context(nc.psum_tensor(name, shape, dt))

        def sem(name, ctx=whole):
            return ctx.enter_context(nc.semaphore(name))

        wq_s = sb("wq_s", [P, 2, KH * WIDE], F16)
        wk_s = sb("wk_s", [P, 2, KH * WIDE], F16)
        wv_s = sb("wv_s", [P, 2, KH * WIDE], F16)
        wg_s = sb("wg_s", [P, 2, KH * WIDE], F16)
        wo_s = sb("wo_s", [P, 2, HEADS * HID], F16)
        wfc_t = sb("wfc_t", [P, KH * FFN], F16)
        wpr_t = sb("wpr_t", [P, KF * HID], F16)
        xT = sb("xT", [P, 2, KH * TOK], F16)
        beta = sb("beta", [P, NTILE, HEADS], F32)
        bq_c = sb("bq_c", [P, HEADS], F32)
        bk_c = sb("bk_c", [P, HEADS], F32)
        bv_b = sb("bv_b", [P, WIDE], F32)
        bo_b = sb("bo_b", [P, HID], F32)
        ident = sb("ident", [P, P], F32)
        mask = sb("mask", [P, P], F32)
        ones16 = sb("ones16", [P, 2], F16)
        scale = sb("scale", [P, 5], F32)
        unscale = sb("unscale", [P, 5], F32)
        eps_sq = sb("eps_sq", [P, 1], F32)
        gate_k = sb("gate_k", [P, 1], F32)
        out_unscale = sb("out_unscale", [P, 1], F32)
        ffn_unscale = sb("ffn_unscale", [P, 1], F32)

        QK, V, G, O, B = range(5)

        def wcol(w, part, k, start, n):
            return w[:, part, ds(k * WIDE + start, n)]

        with ExitStack() as part:
            raw = sb("raw", [P, 2, KH * WIDE], F32, part)
            xc = sb("xc", [P, 2, LN_CHUNK * HID], F32, part)
            xn = sb("xn", [P, 4, HID], F32, part)
            w_sq = sb("w_sq", [P, KH * WIDE], BF16, part)
            b_sq = sb("b_sq", [P, 5 * HEADS], BF16, part)
            ones_bf = sb("ones_bf", [P, P], BF16, part)
            ones_f = sb("ones_f", [P, P], F32, part)
            wb_raw = sb("wb_raw", [P, KH * HEADS], F32, part)
            wb_s = sb("wb_s", [P, 2, KH * HEADS], F16, part)
            bb_b = sb("bb_b", [P, HEADS], F32, part)
            bv_c = sb("bv_c", [P, HEADS], F32, part)
            wfc_r = sb("wfc_r", [P, KH * FFN], F32, part)
            wpr_r = sb("wpr_r", [P, KF * HID], F32, part)
            wabs = sb("wabs", [P, KH * FFN], BF16, part)
            stats = sb("stats", [P, LN_CHUNK, 6], F32, part)
            mv = sb("mv", [P, LN_CHUNK, 2], F32, part)
            t_ln = sb("t_ln", [P, LN_CHUNK], F32, part)
            a_ln = sb("a_ln", [P, LN_CHUNK], F32, part)
            y_ln = sb("y_ln", [P, LN_CHUNK], F32, part)
            peak = sb("peak", [P, 8], F32, part)
            tiny = sb("tiny", [P, 8], F32, part)
            z = sb("z", [P, NTILE * HEADS], F32, part)
            ez = sb("ez", [P, NTILE * HEADS], F32, part)
            uz = xc[:, 0, 0:NTILE * HEADS]
            lz = xc[:, 1, 0:NTILE * HEADS]
            fsum = sb("fsum", [P, 2], F32, part)
            fmean = sb("fmean", [P, 2], F32, part)
            thr = sb("thr", [P, 2], F32, part)
            nthr = sb("nthr", [P, 2], F32, part)

            ps_t = [pb(f"ps_t{i}", [P, 512], part) for i in range(2)]
            ps_n = pb("ps_n", [P, WIDE], part)
            ps_s = pb("ps_s", [P, 512], part)
            ps_z = pb("ps_z", [P, 512], part)

            s_small = sem("s_small", part)
            s_x = [sem(f"s_x{i}", part) for i in range(2)]
            s_raw = [sem(f"s_raw{i}", part) for i in range(2)]
            s_const = sem("s_const", part)
            s_chain = sem("s_chain", part)
            s_xn = sem("s_xn", part)
            s_xt = sem("s_xt", part)
            s_xhi = sem("s_xhi", part)
            s_xlo = sem("s_xlo", part)
            s_wsq = sem("s_wsq", part)
            s_bsq = sem("s_bsq", part)
            s_bnorm = sem("s_bnorm", part)
            s_wnorm = sem("s_wnorm", part)
            s_peak = sem("s_peak", part)
            s_scale = sem("s_scale", part)
            s_whi = sem("s_whi", part)
            s_wlo = sem("s_wlo", part)
            s_lnx = sem("s_lnx", part)
            s_z = sem("s_z", part)
            s_beta = sem("s_beta", part)
            s_bact = sem("s_bact", part)
            s_bt = sem("s_bt", part)
            s_abs = sem("s_abs", part)
            s_fsum = sem("s_fsum", part)

            RAWS = [(wq, wq_s, QK), (wk, wk_s, QK), (wv, wv_s, V), (wg, wg_s, G), (wo, wo_s, O)]
            NX = NTILE // LN_CHUNK
            PAIRS = NTILE // 2

            block = part.enter_context(nc.Block())

            @block.sync
            def _(sp):
                def load_x(c):
                    if c >= 2:
                        sp.wait_ge(s_lnx, c - 1)
                    sp.dma_start(xc[:, c % 2, :].rearrange("p (t h) -> p t h", h=HID), x_c[c]).then_inc(s_x[c % 2], 16)

                def load_raw(j):
                    if j >= 2:
                        sp.wait_ge(s_whi, j - 1)
                        sp.wait_ge(s_wlo, j - 1)
                    sp.dma_start(raw[:, j % 2, :], RAWS[j][0]).then_inc(s_raw[j % 2], 16)

                load_x(0)
                for dst, src in ((wb_raw[:, :], wb), (bq_c[:, :], bq), (bk_c[:, :], bk), (bv_c[:, :], bv)):
                    sp.dma_start(dst, src).then_inc(s_small, 16)
                load_raw(0)
                load_x(1)
                load_raw(1)
                for dst, src, n in ((bv_b, bv_row, WIDE), (bb_b, bb, HEADS), (bo_b, bo, HID)):
                    sp.dma_start(dst[:, :], bass.AP(src.tensor, 0, [[0, P], [1, n]])).then_inc(s_small, 16)
                sp.dma_start(wfc_r[:, :], wfc).then_inc(s_small, 16)
                sp.dma_start(wpr_r[:, :], wpr).then_inc(s_small, 16)
                load_x(2)
                load_x(3)
                for j in range(2, 5):
                    load_raw(j)

            SMALL = 9 * 16

            @block.gpsimd
            def _(pool):
                pool.memset(ident[:, :], 0.0).then_inc(s_const, 1)
                pool.memset(mask[:, :], 1.0).then_inc(s_const, 1)
                pool.wait_ge(s_const, 2)
                pool.affine_select(out=ident[:, :], in_=ident[:, :], compare_op=ALU.not_equal, fill=1.0, base=0,
                                   pattern=[[-1, P]], channel_multiplier=1).then_inc(s_const, 1)
                pool.affine_select(out=mask[:, :], in_=mask[:, :], compare_op=ALU.is_ge, fill=0.0, base=0,
                                   pattern=[[1, P]], channel_multiplier=-1).then_inc(s_const, 1)
                pool.wait_ge(s_const, 4)
                pool.memset(mask[0:CHUNK, CHUNK:P], 0.0).then_inc(s_const, 1)
                pool.memset(ones16[:, :], 1.0).then_inc(s_const, 1)
                pool.memset(ones_bf[:, :], 1.0).then_inc(s_const, 1)
                pool.memset(ones_f[:, :], 1.0).then_inc(s_const, 1)

            @block.scalar
            def _(act):
                def square_small():
                    act.wait_ge(s_small, SMALL)
                    for i, b in enumerate((bq_c, bk_c, bv_c)):
                        act.activation(b_sq[:, i * HEADS:(i + 1) * HEADS], b[:, :], ACT.Square,
                                       scale=1.0 / 16).then_inc(s_bsq, 1)
                    act.activation(b_sq[:, 3 * HEADS:5 * HEADS], wb_raw[:, :], ACT.Square).then_inc(s_bsq, 1)

                def square(j):
                    act.wait_ge(s_raw[j % 2], 16 * (j // 2 + 1))
                    if j:
                        act.wait_ge(s_wnorm, j)
                    act.activation(w_sq[:, :], raw[:, j % 2, :], ACT.Square).then_inc(s_wsq, 1)

                def split_hi(j):
                    _, dst, which = RAWS[j]
                    act.wait_ge(s_scale, which + 1)
                    act.activation(dst[:, 0, :], raw[:, j % 2, :], ACT.Copy, scale=scale[:, which:which + 1]).then_inc(s_whi, 1)

                def x_hi(first, last):
                    for m in range(first, last):
                        act.wait_ge(s_xt, m + 1)
                        act.activation(xT[:, 0, :].rearrange("p (k n) -> p k n", k=KH)[:, :, m * 256:(m + 1) * 256],
                                       ps_t[m % 2][:, :].rearrange("p (k n) -> p k n", k=KH), ACT.Copy).then_inc(s_xhi, 1)

                x_hi(0, 4)
                square_small()
                square(0)
                square(1)
                x_hi(4, 8)
                split_hi(0)
                split_hi(1)
                x_hi(8, 12)
                square(2)
                split_hi(2)
                x_hi(12, 16)
                square(3)
                split_hi(3)
                square(4)
                split_hi(4)
                for i, (w, n) in enumerate(((wfc_r, KH * FFN), (wpr_r, KF * HID))):
                    if i:
                        act.wait_ge(s_abs, 1)
                    act.activation(wabs[:, 0:n], w[:, :], ACT.Abs, accum_out=fsum[:, i:i + 1]).then_inc(s_abs, 1)
                act.wait_ge(s_beta, 1)
                act.activation(lz, z[:, :], ACT.Abs).then_inc(s_bact, 1)
                act.wait_ge(s_bact, 1)
                act.activation(ez[:, :], lz, ACT.Exp, scale=-1.0).then_inc(s_bact, 1)
                act.wait_ge(s_beta, 2)
                act.activation(lz, uz, ACT.Ln).then_inc(s_bact, 1)

            @block.vector
            def _(dve):
                chain = [0]

                def link(ins):
                    chain[0] += 1
                    ins.then_inc(s_chain, 1)
                    dve.wait_ge(s_chain, chain[0])

                def rsqrt(y, a, t, rounds=3):
                    link(dve.tensor_scalar(a.bitcast(I32), t.bitcast(I32), 1, None, ALU.logical_shift_right))
                    link(dve.tensor_scalar(y.bitcast(I32), a.bitcast(I32), -1, RSQRT_GUESS, ALU.mult, ALU.add))
                    for _ in range(rounds):
                        link(dve.scalar_tensor_tensor(out=a, in0=y, scalar=-0.5, in1=y, op0=ALU.mult, op1=ALU.mult))
                        link(dve.tensor_tensor(a, a, t, ALU.mult))
                        link(dve.scalar_tensor_tensor(out=y, in0=a, scalar=1.5, in1=y, op0=ALU.add, op1=ALU.mult))

                def power(dst, src, which):
                    a = tiny[:, 0:1].bitcast(I32)
                    link(dve.tensor_scalar(a, src.bitcast(I32), 23, None, ALU.logical_shift_right))
                    link(dve.tensor_scalar(a, a, 131, None, ALU.add))
                    link(dve.tensor_scalar(a, a, 1, None, ALU.logical_shift_right))
                    b = tiny[:, 1:2].bitcast(I32)
                    link(dve.tensor_scalar(b, a, -1, 259, ALU.mult, ALU.add))
                    link(dve.tensor_scalar(dst.bitcast(I32), b, 23, None, ALU.logical_shift_left))
                    link(dve.tensor_scalar(a, a, -5, None, ALU.add))
                    link(dve.tensor_scalar(unscale[:, which:which + 1].bitcast(I32), a, 23, None, ALU.logical_shift_left))

                def normalise(c):
                    dve.wait_ge(s_x[c % 2], 16 * (c // 2 + 1))
                    rows = xc[:, c % 2, :].rearrange("p (t h) -> p t h", h=HID)
                    for t in range(LN_CHUNK):
                        link(dve.bn_stats(stats[:, t, :], rows[:, t, :]))
                    for t in range(LN_CHUNK):
                        link(dve.bn_aggr(mv[:, t, :], stats[:, t, :]))
                    link(dve.tensor_scalar(t_ln[:, :], mv[:, :, 1], LN_EPS, None, ALU.add))
                    rsqrt(y_ln[:, :], a_ln[:, :], t_ln[:, :])
                    for t in range(LN_CHUNK):
                        n = c * LN_CHUNK + t
                        if n >= 4:
                            dve.wait_ge(s_xt, (n - 4) // 2 + 1)
                        last = dve.tensor_scalar(xn[:, n % 4, :], rows[:, t, :], mv[:, t, 0:1], y_ln[:, t:t + 1],
                                                 ALU.subtract, ALU.mult).then_inc(s_xn, 1)
                        if t % 2:
                            x_lo(n // 2)
                    dve.wait_ge(s_xn, (c + 1) * LN_CHUNK)
                    dve.nop().then_inc(s_lnx, 1)

                def x_lo(m):
                    dve.wait_ge(s_xhi, m + 1)
                    view = xT[:, :, :].rearrange("p s (k n) -> p s k n", k=KH)
                    dve.tensor_tensor(view[:, 1, :, m * 256:(m + 1) * 256],
                                      ps_t[m % 2][:, :].rearrange("p (k n) -> p k n", k=KH),
                                      view[:, 0, :, m * 256:(m + 1) * 256], ALU.subtract).then_inc(s_xlo, 1)

                def top(j):
                    dve.wait_ge(s_wnorm, j + 1)
                    n = WIDE if j < 4 else 512
                    dve.tensor_reduce(peak[:, j:j + 1], ps_n[:, 0:n], AX_X, ALU.max).then_inc(s_peak, 1)
                    dve.wait_ge(s_peak, j + 1)

                normalise(0)
                dve.wait_ge(s_bnorm, 1)
                link(dve.tensor_reduce(peak[:, 6:7], ps_s[:, 0:2 * HEADS], AX_X, ALU.max))
                link(dve.tensor_reduce(peak[:, 7:8], ps_s[:, 2 * HEADS:3 * HEADS], AX_X, ALU.max))
                top(0)
                top(1)
                link(dve.tensor_tensor(peak[:, 0:1], peak[:, 0:1], peak[:, 1:2], ALU.max))
                link(dve.tensor_tensor(peak[:, 0:1], peak[:, 0:1], peak[:, 6:7], ALU.add))
                link(dve.tensor_scalar(peak[:, 0:1], peak[:, 0:1], 1e-30, None, ALU.max))
                power(scale[:, QK:QK + 1], peak[:, 0:1], QK)
                dve.nop().then_inc(s_scale, 1)
                link(dve.tensor_scalar(tiny[:, 2:3], scale[:, QK:QK + 1], L2_EPS, None, ALU.mult))
                link(dve.tensor_tensor(eps_sq[:, :], tiny[:, 2:3], tiny[:, 2:3], ALU.mult))
                normalise(1)

                def split_lo(j):
                    _, dst, which = RAWS[j]
                    dve.wait_ge(s_whi, j + 1)
                    dve.scalar_tensor_tensor(out=dst[:, 1, :], in0=raw[:, j % 2, :], scalar=scale[:, which:which + 1],
                                             in1=dst[:, 0, :], op0=ALU.mult, op1=ALU.subtract).then_inc(s_wlo, 1)

                split_lo(0)
                split_lo(1)
                normalise(2)
                link(dve.tensor_scalar(bq_c[:, :], bq_c[:, :], scale[:, QK:QK + 1], None, ALU.mult))
                link(dve.tensor_scalar(bk_c[:, :], bk_c[:, :], scale[:, QK:QK + 1], None, ALU.mult))
                for j, which in ((2, V), (3, G), (4, O)):
                    top(j)
                    if which == V:
                        link(dve.tensor_tensor(peak[:, 2:3], peak[:, 2:3], peak[:, 7:8], ALU.add))
                    link(dve.tensor_scalar(peak[:, j:j + 1], peak[:, j:j + 1], 1e-30, None, ALU.max))
                    power(scale[:, which:which + 1], peak[:, j:j + 1], which)
                    dve.nop().then_inc(s_scale, 1)
                    split_lo(j)
                    if which == V:
                        link(dve.tensor_scalar(bv_b[:, :], bv_b[:, :], scale[:, V:V + 1], None, ALU.mult))
                        normalise(3)
                link(dve.tensor_reduce(peak[:, 5:6], ps_s[:, 3 * HEADS:5 * HEADS], AX_X, ALU.max))
                link(dve.tensor_scalar(peak[:, 5:6], peak[:, 5:6], 2.0, 1e-30, ALU.mult, ALU.max))
                power(scale[:, B:B + 1], peak[:, 5:6], B)
                link(dve.tensor_scalar(wb_s[:, 0, :], wb_raw[:, :], scale[:, B:B + 1], None, ALU.mult))
                dve.scalar_tensor_tensor(out=wb_s[:, 1, :], in0=wb_raw[:, :], scalar=scale[:, B:B + 1],
                                         in1=wb_s[:, 0, :], op0=ALU.mult, op1=ALU.subtract).then_inc(s_z, 1)
                dve.wait_ge(s_fsum, 1)
                link(dve.tensor_scalar(fmean[:, :], ps_s[:, 128:130], 1.0 / (FFN * HID), 1e-5, ALU.mult, ALU.max))
                link(dve.tensor_scalar(thr[:, :], fmean[:, :], 0.7, None, ALU.mult))
                link(dve.tensor_scalar(nthr[:, :], thr[:, :], -1.0, None, ALU.mult))
                for i, (w, dst, n) in enumerate(((wfc_r, wfc_t, KH * FFN), (wpr_r, wpr_t, KF * HID))):
                    link(dve.tensor_scalar(w_sq[:, 0:n], w[:, :], nthr[:, i:i + 1], None, ALU.is_lt))
                    link(dve.scalar_tensor_tensor(out=dst[:, :], in0=w[:, :], scalar=thr[:, i:i + 1], in1=w_sq[:, 0:n],
                                                  op0=ALU.is_gt, op1=ALU.subtract))
                link(dve.tensor_scalar(wfc_t[:, :], wfc_t[:, :], 0.25, None, ALU.mult))
                link(dve.scalar_tensor_tensor(out=ffn_unscale[:, :], in0=fmean[:, 0:1], scalar=16.0, in1=fmean[:, 0:1],
                                              op0=ALU.mult, op1=ALU.mult))
                link(dve.tensor_tensor(ffn_unscale[:, :], ffn_unscale[:, :], fmean[:, 1:2], ALU.mult))
                dve.wait_ge(s_z, 2)
                z3 = z[:, :].rearrange("p (t h) -> p t h", h=HEADS)
                bb3 = bb_b[:, :].unsqueeze(1).broadcast_to((P, NTILE, HEADS))
                dve.scalar_tensor_tensor(out=z3, in0=ps_z[:, :].rearrange("p (t h) -> p t h", h=HEADS),
                                         scalar=unscale[:, B:B + 1], in1=bb3, op0=ALU.mult, op1=ALU.add).then_inc(s_beta, 1)
                dve.wait_ge(s_bact, 2)
                dve.tensor_scalar(uz, ez[:, :], 1.0, None, ALU.add).then_inc(s_beta, 1)
                dve.wait_ge(s_bact, 3)
                b2 = beta[:, :, :].rearrange("p t h -> p (t h)")
                dve.wait_ge(s_beta, 2)
                link(dve.tensor_scalar(b2, uz, -1.0, 1e-30, ALU.add, ALU.max))
                link(dve.reciprocal(b2, b2))
                link(dve.tensor_tensor(b2, b2, ez[:, :], ALU.mult))
                link(dve.tensor_tensor(b2, b2, lz, ALU.mult))
                link(dve.tensor_scalar(uz, uz, 1.0, None, ALU.is_equal))
                link(dve.tensor_tensor(uz, uz, ez[:, :], ALU.mult))
                link(dve.tensor_tensor(b2, b2, uz, ALU.add))
                link(dve.scalar_tensor_tensor(out=b2, in0=z[:, :], scalar=0.0, in1=b2, op0=ALU.max, op1=ALU.add))
                dve.tensor_reduce(tiny[:, 3:4], b2, AX_X, ALU.max).then_inc(s_bt, 1)
                dve.wait_ge(s_bt, 2)
                dve.tensor_reduce(tiny[0:1, 4:5], ps_t[0][0:1, 0:P], AX_X, ALU.max).then_inc(s_bt, 1)
                dve.wait_ge(s_bt, 4)
                a = tiny[:, 5:6].bitcast(I32)
                link(dve.tensor_scalar(tiny[:, 6:7], ps_t[1][:, 0:1], 1e-30, None, ALU.max))
                link(dve.tensor_scalar(a, tiny[:, 6:7].bitcast(I32), 23, None, ALU.logical_shift_right))
                link(dve.tensor_scalar(tiny[:, 0:1].bitcast(I32), a, -1, 253, ALU.mult, ALU.add))
                link(dve.tensor_scalar(tiny[:, 1:2].bitcast(I32), tiny[:, 0:1].bitcast(I32), 23, None, ALU.logical_shift_left))
                link(dve.tensor_scalar(b2, b2, tiny[:, 1:2], None, ALU.mult))
                link(dve.tensor_scalar(a, a, 1, None, ALU.add))
                link(dve.tensor_scalar(tiny[:, 2:3].bitcast(I32), a, 23, None, ALU.logical_shift_left))
                link(dve.tensor_scalar(gate_k[:, :], scale[:, G:G + 1], 2.0 ** -15, None, ALU.mult))
                link(dve.scalar_tensor_tensor(out=out_unscale[:, :], in0=unscale[:, V:V + 1], scalar=2.0 ** 8,
                                              in1=unscale[:, G:G + 1], op0=ALU.mult, op1=ALU.mult))
                link(dve.tensor_tensor(out_unscale[:, :], out_unscale[:, :], unscale[:, O:O + 1], ALU.mult))
                link(dve.tensor_tensor(out_unscale[:, :], out_unscale[:, :], tiny[:, 2:3], ALU.mult))

            @block.tensor
            def _(pe):
                pe.wait_ge(s_const, 8)

                def transposes(first, last):
                    for m in range(first, last):
                        pe.wait_ge(s_xn, 2 * m + 2)
                        if m >= 2:
                            pe.wait_ge(s_xhi, m - 1)
                            pe.wait_ge(s_xlo, m - 1)
                        for k in range(KH):
                            for t in range(2):
                                last_t = pe.transpose(ps_t[m % 2][:, k * 256 + t * P:k * 256 + (t + 1) * P],
                                                      xn[:, (2 * m + t) % 4, k * P:(k + 1) * P], ident[:, :])
                        last_t.then_inc(s_xt, 1)

                def norms(j):
                    pe.wait_ge(s_wsq, j + 1)
                    if j:
                        pe.wait_ge(s_peak, j)
                    if j < 4:
                        for n in range(WIDE // 512):
                            for k in range(KH):
                                last = pe.matmul(ps_n[:, n * 512:(n + 1) * 512], ones_bf[:, :],
                                                 w_sq[:, k * WIDE + n * 512:k * WIDE + (n + 1) * 512],
                                                 start=(k == 0), stop=(k == KH - 1))
                    else:
                        for n in range(HEADS // 2):
                            last = pe.matmul(ps_n[:, 0:512], ones_bf[:, :], w_sq[:, n * 512:(n + 1) * 512],
                                             start=(n == 0), stop=(n == HEADS // 2 - 1))
                    last.then_inc(s_wnorm, 1)

                transposes(0, 4)
                pe.wait_ge(s_bsq, 4)
                pe.matmul(ps_s[:, 0:5 * HEADS], ones_bf[:, :], b_sq[:, :], start=True, stop=True).then_inc(s_bnorm, 1)
                norms(0)
                norms(1)
                transposes(4, 12)
                norms(2)
                transposes(12, 16)
                norms(3)
                norms(4)
                pe.wait_ge(s_abs, 2)
                pe.wait_ge(s_z, 1)
                pe.matmul(ps_s[:, 128:130], ones_f[:, :], fsum[:, :], start=True, stop=True).then_inc(s_fsum, 1)
                pe.wait_ge(s_xhi, PAIRS)
                pe.wait_ge(s_xlo, PAIRS)
                for t in range(NTILE):
                    n = 0
                    for k in range(KH):
                        for a, b in ((0, 0), (0, 1), (1, 0)):
                            last = pe.matmul(ps_z[:, t * HEADS:(t + 1) * HEADS],
                                             xT[:, a, k * TOK + t * P:k * TOK + (t + 1) * P],
                                             wb_s[:, b, k * HEADS:(k + 1) * HEADS], start=(n == 0), stop=(n == 5))
                            n += 1
                last.then_inc(s_z, 1)
                pe.wait_ge(s_bt, 1)
                pe.transpose(ps_t[0][0:1, 0:P], tiny[:, 3:4], ident[:, :]).then_inc(s_bt, 1)
                pe.wait_ge(s_bt, 3)
                pe.matmul(ps_t[1][:, 0:1], ones_f[0:1, :], tiny[0:1, 4:5], start=True, stop=True).then_inc(s_bt, 1)

        with ExitStack() as part:
            q_s = sb("q_s", [P, 2, 2, BLK], F16, part)
            k_s = sb("k_s", [P, 2, 2, BLK], F16, part)
            q_sq = sb("q_sq", [P, 2, BLK], F32, part)
            k_sq = sb("k_sq", [P, 2, BLK], F32, part)
            q_sl = sb("q_sl", [P, 2, BLK], F16, part)
            k_sl = sb("k_sl", [P, 2, BLK], F16, part)
            v_f = sb("v_f", [P, 2, GW], F32, part)
            v_s = sb("v_s", [P, 2, 2 * TILES * GW], F16, part)
            gate = sb("gate", [P, 2 * TILES * GW], F32, part)
            pr_f = sb("pr_f", [P, 2, BLK], F32, part)
            pr_s = sb("pr_s", [P, 2, 2, BLK], F16, part)
            og = sb("og", [P, 2, BLK], F32, part)
            ogT = sb("ogT", [P, 2, 2, BLK], F16, part)
            rows = sb("rows", [P, TILES * HID], F32, part)
            t_n = sb("t_n", [P, 8], F32, part)
            a_n = sb("a_n", [P, 8], F32, part)
            y_n = sb("y_n", [P, 8], F32, part)
            c_k = sb("c_k", [P, 2, TILES], F32, part)
            c_q = sb("c_q", [P, 2, TILES], F32, part)

            ps_qv = pb("ps_qv", [P, 512], part)
            ps_kg = pb("ps_kg", [P, 512], part)
            ps_sc = pb("ps_sc", [P, 512], part)
            ps_nm = pb("ps_nm", [P, 512], part)
            ps_pv = pb("ps_pv", [P, 512], part)
            ps_tr = pb("ps_tr", [P, 512], part)
            ps_acc = pb("ps_acc", [P, TILES * HID], part)

            s_q = sem("s_q", part)
            s_k = sem("s_k", part)
            s_v = sem("s_v", part)
            s_g = sem("s_g", part)
            s_score = sem("s_score", part)
            s_norm = sem("s_norm", part)
            s_pv = sem("s_pv", part)
            s_tr = sem("s_tr", part)
            s_acc = sem("s_acc", part)
            s_qhi = sem("s_qhi", part)
            s_khi = sem("s_khi", part)
            s_qsq = sem("s_qsq", part)
            s_ksq = sem("s_ksq", part)
            s_vhi = sem("s_vhi", part)
            s_gate = sem("s_gate", part)
            s_phi = sem("s_phi", part)
            s_ohi = sem("s_ohi", part)
            s_qlo = sem("s_qlo", part)
            s_klo = sem("s_klo", part)
            s_vf = sem("s_vf", part)
            s_newton = sem("s_newton", part)
            s_p = sem("s_p", part)
            s_og = sem("s_og", part)
            s_olo = sem("s_olo", part)
            s_mid = sem("s_mid", part)
            s_qsl = sem("s_qsl", part)
            s_ksl = sem("s_ksl", part)
            s_vlo = sem("s_vlo", part)
            s_plo = sem("s_plo", part)
            s_bias = sem("s_bias", part)
            s_rows = sem("s_rows", part)
            s_kept = sem("s_kept", part)

            PARTS = ((0, 0), (0, 1), (1, 0))

            def where(b, hg, s):
                g = NBLK_GROUPS * b + hg
                return GROUP * g + s, g

            NBLK_GROUPS = HEADS // GROUP

            def group_ahead(b, hg, s):
                if s < 2:
                    return b, hg
                return (b, hg + 1) if hg + 1 < NBLK_GROUPS else (b + 1, 0)

            def back(b, hg, s, lag):
                pos = GROUP * hg + s - lag
                g = NBLK_GROUPS * b + hg
                if pos < 0:
                    return b - 1, pos + HEADS, g - 1, (s - lag) % GROUP
                return b, pos, g if s >= lag else g - 1, (s - lag) % GROUP

            def walk(eng, slot, finish):
                slots = [(hg, s) for hg in range(NBLK_GROUPS) for s in range(GROUP)]
                for hg, s in slots[:GROUP]:
                    slot(0, hg, s)
                with eng.Fori(0, NBLK - 1) as b:
                    for hg, s in slots[GROUP:]:
                        slot(b, hg, s)
                    for hg, s in slots[:GROUP]:
                        slot(b + 1, hg, s)
                for hg, s in slots[GROUP:]:
                    slot(NBLK - 1, hg, s)
                for s in range(3):
                    slot(NBLK, 0, s)
                finish()

            def live(u, lag):
                return not isinstance(u, int) or 0 <= u - lag < UNITS

            block = part.enter_context(nc.Block())

            @block.tensor
            def _(pe):
                def wide_tile(ps, wt, t, blk, hg, done):
                    n = 0
                    for k in range(KH):
                        for a, c in PARTS:
                            last = pe.matmul(ps[:, :], xT[:, a, ds(blk * BLK + (k * TOK + t * P), P)],
                                             wcol(wt, c, k, hg * GW, GW), start=(n == 0), stop=(n == 5))
                            n += 1
                    last.then_inc(done, 1)

                def values(w, t, blk, hg):
                    if not low(w - 1):
                        pe.wait_ge(s_qlo, w - 1)
                        pe.wait_ge(s_qsq, w - 1)
                    if not low(w):
                        pe.wait_ge(s_vf, w)
                    wide_tile(ps_qv, wv_s, t, blk, hg, s_v)

                def gates(w, t, blk, hg):
                    if not low(w - 1):
                        pe.wait_ge(s_klo, w - 1)
                        pe.wait_ge(s_ksq, w - 1)
                    if not low(w):
                        pe.wait_ge(s_gate, w)
                    wide_tile(ps_kg, wg_s, t, blk, hg, s_g)

                def slot(b, hg, s):
                    u, g = where(b, hg, s)
                    par = s % 2
                    if live(u, 0):
                        head = (hg * GROUP + s) * P
                        row = b * BLK
                        for ps, wt, done, freed in ((ps_qv, wq_s, s_q, s_vf), (ps_kg, wk_s, s_k, s_gate)):
                            if live(u, -1):
                                pe.wait_ge(freed, u + 2)
                            else:
                                pe.wait_ge(freed, UNITS)
                            n = 0
                            for k in range(KH):
                                for a, c in PARTS:
                                    last = pe.matmul(ps[:, :], wcol(wt, a, k, head, P),
                                                     xT[:, c, ds(row + k * TOK, BLK)], start=(n == 0), stop=(n == 5))
                                    n += 1
                            last.then_inc(done, 1)
                    if live(u, 1):
                        prev = (s - 1) % 2
                        pe.wait_ge(s_qhi, u)
                        pe.wait_ge(s_khi, u)
                        pe.wait_ge(s_qlo, u)
                        pe.wait_ge(s_klo, u)
                        if not low(u - 1):
                            pe.wait_ge(s_p, u - 1)
                        for t in range(TILES):
                            for n, (a, c) in enumerate(PARTS):
                                last = pe.matmul(ps_sc[:, t * P:(t + 1) * P], k_s[:, prev, a, t * P:(t + 1) * P],
                                                 q_s[:, prev, c, t * P:(t + 1) * P], start=(n == 0), stop=(n == 2))
                        last.then_inc(s_score, 1)
                        pe.wait_ge(s_qsl, u)
                        pe.wait_ge(s_ksl, u)
                        if not low(u - 1):
                            pe.wait_ge(s_newton, NORM_STEPS * (u - 1))
                        for i, (sq, sl) in enumerate(((q_sq, q_sl), (k_sq, k_sl))):
                            for t in range(TILES):
                                o = ps_nm[:, i * TILES + t:i * TILES + t + 1]
                                pe.matmul(o, sq[:, prev, t * P:(t + 1) * P].bitcast(BF16)[:, 1::2], ones16[:, 0:1],
                                          start=True, stop=False)
                                last = pe.matmul(o, sl[:, prev, t * P:(t + 1) * P], ones16[:, 0:1],
                                                 start=False, stop=True)
                        last.then_inc(s_norm, 1)
                    if live(u, -2):
                        values(u + 2, (s + 2) % TILES, *group_ahead(b, hg, s))
                    if live(u, 2):
                        _, head, grp, hh = back(b, hg, s, 2)
                        pe.wait_ge(s_phi, u - 1)
                        pe.wait_ge(s_plo, u - 1)
                        pe.wait_ge(s_vhi, GROUP * grp + GROUP)
                        pe.wait_ge(s_vlo, GROUP * grp + GROUP)
                        if not low(u - 2):
                            pe.wait_ge(s_og, u - 2)
                        at = (head // GROUP % 2) * (TILES * GW)
                        for t in range(TILES):
                            for n, (a, c) in enumerate(PARTS):
                                last = pe.matmul(ps_pv[:, t * P:(t + 1) * P], pr_s[:, par, a, t * P:(t + 1) * P],
                                                 v_s[:, c, ds(at + (t * GW + hh * P), P)], start=(n == 0), stop=(n == 2))
                        last.then_inc(s_pv, 1)
                    if live(u, -2):
                        gates(u + 2, (s + 2) % TILES, *group_ahead(b, hg, s))
                    if live(u, 3):
                        blk, head, _, _ = back(b, hg, s, 3)
                        pe.wait_ge(s_ohi, u - 2)
                        pe.wait_ge(s_olo, u - 2)
                        first = head == 0
                        final = head == HEADS - 1
                        if first and not low(blk):
                            pe.wait_ge(s_mid, blk)
                        prev = (s - 3) % 2
                        for t in range(TILES):
                            for n, (a, c) in enumerate(PARTS):
                                last = pe.matmul(ps_acc[:, t * HID:(t + 1) * HID], ogT[:, prev, a, t * P:(t + 1) * P],
                                                 wo_s[:, c, ds(head * HID, HID)],
                                                 start=(first and n == 0 and t % 2 == 0), stop=(final and n == 2),
                                                 skip_group_check=True)
                        last.then_inc(s_acc, 1)
                    if live(u, 2):
                        pe.wait_ge(s_og, u - 1)
                        if not low(u - 2):
                            pe.wait_ge(s_olo, u - 2)
                            pe.wait_ge(s_ohi, u - 2)
                        for t in range(TILES):
                            last = pe.transpose(ps_tr[:, t * P:(t + 1) * P], og[:, par, t * P:(t + 1) * P], ident[:, :])
                        last.then_inc(s_tr, 1)

                for t in range(2):
                    values(t, t, 0, 0)
                    gates(t, t, 0, 0)
                walk(pe, slot, lambda: None)

            @block.scalar
            def _(act):
                def values(w, t, blk, hg):
                    at = (hg % 2) * (TILES * GW) + t * GW
                    act.wait_ge(s_vf, w + 1)
                    if not low(w - 4):
                        act.wait_ge(s_pv, w - 4)
                    act.activation(v_s[:, 0, ds(at, GW)], v_f[:, t % 2, :], ACT.Copy).then_inc(s_vhi, 1)
                    act.wait_ge(s_g, w + 1)
                    if not low(w - 4):
                        act.wait_ge(s_og, w - 4)
                    act.activation(gate[:, ds(at, GW)], ps_kg[:, :], ACT.Silu, scale=unscale[:, G:G + 1]).then_inc(s_gate, 1)

                def projection(u, par, head, done, ps, bias, dst, sq, hi, sqd):
                    if not live(u, 0):
                        return
                    act.wait_ge(done, u + 1)
                    if not low(u - 1):
                        act.wait_ge(s_score, u - 1)
                    act.activation(dst[:, par, 0, :], ps[:, :], ACT.Identity, bias=bias[:, head:head + 1]).then_inc(hi, 1)
                    if not low(u - 1):
                        act.wait_ge(s_norm, u - 1)
                    act.activation(sq[:, par, :], ps[:, :], ACT.Square, bias=bias[:, head:head + 1]).then_inc(sqd, 1)

                def slot(b, hg, s):
                    u, g = where(b, hg, s)
                    par = s % 2
                    if live(u, 3):
                        act.wait_ge(s_tr, u - 2)
                        if not low(u - 3):
                            act.wait_ge(s_acc, u - 3)
                        act.activation(ogT[:, (s - 3) % 2, 0, :], ps_tr[:, :], ACT.Copy).then_inc(s_ohi, 1)
                    projection(u, par, hg * GROUP + s, s_q, ps_qv, bq_c, q_s, q_sq, s_qhi, s_qsq)
                    if live(u, 2):
                        act.wait_ge(s_p, u - 1)
                        if not low(u - 3):
                            act.wait_ge(s_pv, u - 3)
                        act.activation(pr_s[:, par, 0, :], pr_f[:, par, :], ACT.Copy).then_inc(s_phi, 1)
                    projection(u, par, hg * GROUP + s, s_k, ps_kg, bk_c, k_s, k_sq, s_khi, s_ksq)
                    if live(u, -2):
                        values(u + 2, (s + 2) % TILES, *group_ahead(b, hg, s))

                values(0, 0, 0, 0)
                values(1, 1, 0, 0)
                walk(act, slot, lambda: None)

            @block.vector
            def _(dve):
                def values(w, t, blk, hg):
                    col = hg * GW
                    dve.wait_ge(s_v, w + 1)
                    if not low(w - 1):
                        dve.wait_ge(s_vhi, w - 1)
                        dve.wait_ge(s_vlo, w - 1)
                    dve.tensor_tensor(v_f[:, t % 2, :], ps_qv[:, :], bv_b[:, ds(col, GW)], ALU.add).then_inc(s_vf, 1)

                def newton(step, u, prev, blk, head):
                    if step == 0:
                        dve.wait_ge(s_norm, u)
                        if not low(u - 1):
                            dve.wait_ge(s_newton, NORM_STEPS * (u - 1))
                        ins = dve.tensor_scalar(t_n[:, :], ps_nm[:, 0:8], 1.0 / P, eps_sq[:, :], ALU.mult, ALU.max)
                    else:
                        dve.wait_ge(s_newton, NORM_STEPS * (u - 1) + step)
                    if step == 1:
                        ins = dve.tensor_scalar(a_n[:, :].bitcast(I32), t_n[:, :].bitcast(I32), 1, None,
                                                ALU.logical_shift_right)
                    if step == 2:
                        ins = dve.tensor_scalar(y_n[:, :].bitcast(I32), a_n[:, :].bitcast(I32), -1, RSQRT_GUESS,
                                                ALU.mult, ALU.add)
                    if step in (3, 6, 9):
                        ins = dve.scalar_tensor_tensor(out=a_n[:, :], in0=y_n[:, :], scalar=-0.5, in1=y_n[:, :],
                                                       op0=ALU.mult, op1=ALU.mult)
                    if step in (4, 7, 10):
                        ins = dve.tensor_tensor(a_n[:, :], a_n[:, :], t_n[:, :], ALU.mult)
                    if step in (5, 8, 11):
                        ins = dve.scalar_tensor_tensor(out=y_n[:, :], in0=a_n[:, :], scalar=1.5, in1=y_n[:, :],
                                                       op0=ALU.add, op1=ALU.mult)
                    if step == 12:
                        ins = dve.tensor_tensor(c_k[:, prev, :].unsqueeze(2), y_n[:, TILES:2 * TILES].unsqueeze(2),
                                                beta[:, ds(blk * TILES, TILES), ds(head, 1)], ALU.mult)
                    if step == 13:
                        ins = dve.tensor_scalar(c_q[:, prev, :], y_n[:, 0:TILES], gate_k[:, :], None, ALU.mult)
                    ins.then_inc(s_newton, 1)

                def output_tile(t, u, par, head):
                    at = (head // GROUP % 2) * (TILES * GW)
                    ins = dve.scalar_tensor_tensor(out=og[:, par, t * P:(t + 1) * P], in0=ps_pv[:, t * P:(t + 1) * P],
                                                   scalar=c_q[:, par, t:t + 1], in1=gate[:, ds(at + t * GW + head % GROUP * P, P)],
                                                   op0=ALU.mult, op1=ALU.mult)
                    if t == TILES - 1:
                        ins.then_inc(s_og, 1)

                def slot(b, hg, s):
                    u, g = where(b, hg, s)
                    par, prev = s % 2, (s - 1) % 2
                    if live(u, 3):
                        dve.wait_ge(s_ohi, u - 2)
                        if not low(u - 3):
                            dve.wait_ge(s_acc, u - 3)
                        o = ogT[:, (s - 3) % 2, :, :]
                        dve.tensor_tensor(o[:, 1, :], ps_tr[:, :], o[:, 0, :], ALU.subtract).then_inc(s_olo, 1)
                    if s == 3 and hg == 0 and not low(u - 3):
                        rows_out(b)
                    if live(u, 0):
                        head = hg * GROUP + s
                        for ps, bias, dst, hi, sqd, done in (
                            (ps_qv, bq_c, q_s, s_qhi, s_qsq, s_qlo), (ps_kg, bk_c, k_s, s_khi, s_ksq, s_klo),
                        ):
                            dve.wait_ge(hi, u + 1)
                            dve.wait_ge(sqd, u + 1)
                            dve.scalar_tensor_tensor(out=dst[:, par, 1, :], in0=ps[:, :], scalar=bias[:, ds(head, 1)],
                                                     in1=dst[:, par, 0, :], op0=ALU.add, op1=ALU.subtract).then_inc(done, 1)
                    if live(u, 1):
                        blk, head, _, _ = back(b, hg, s, 1)
                        for step in range(4):
                            newton(step, u, prev, blk, head)
                    if live(u, -2):
                        values(u + 2, (s + 2) % TILES, *group_ahead(b, hg, s))
                    if live(u, 1):
                        for step in range(4, 5):
                            newton(step, u, prev, blk, head)
                    if live(u, 2):
                        _, out_head, grp, _ = back(b, hg, s, 2)
                        dve.wait_ge(s_pv, u - 1)
                        dve.wait_ge(s_gate, GROUP * grp + GROUP)
                        dve.wait_ge(s_newton, NORM_STEPS * (u - 1))
                        if not low(u - 3):
                            dve.wait_ge(s_tr, u - 3)
                    for t in range(TILES):
                        if live(u, 2):
                            output_tile(t, u, par, out_head)
                        if live(u, 1):
                            for step in range(5 + 1 * t, 5 + 1 * (t + 1)):
                                newton(step, u, prev, blk, head)
                    if live(u, 1):
                        for step in range(5 + 1 * TILES, NORM_STEPS):
                            newton(step, u, prev, blk, head)
                        dve.wait_ge(s_score, u)
                        dve.wait_ge(s_newton, NORM_STEPS * (u - 1) + 13)
                        if not low(u - 2):
                            dve.wait_ge(s_phi, u - 2)
                            dve.wait_ge(s_plo, u - 2)
                        for t in range(TILES):
                            last = dve.scalar_tensor_tensor(out=pr_f[:, prev, t * P:(t + 1) * P],
                                                            in0=ps_sc[:, t * P:(t + 1) * P], scalar=c_k[:, prev, t:t + 1],
                                                            in1=mask[:, :], op0=ALU.mult, op1=ALU.mult)
                        last.then_inc(s_p, 1)

                def rows_out(b):
                    dve.wait_ge(s_acc, HEADS * b)
                    dve.wait_ge(s_bias, b)
                    for i in range(2):
                        half = slice(i * 512, (i + 1) * 512)
                        ins = dve.scalar_tensor_tensor(out=rows[:, half], in0=ps_acc[:, half], scalar=out_unscale[:, :],
                                                       in1=rows[:, half], op0=ALU.mult, op1=ALU.add)
                    ins.then_inc(s_mid, 1)

                values(0, 0, 0, 0)
                values(1, 1, 0, 0)
                walk(dve, slot, lambda: rows_out(NBLK))

            @block.gpsimd
            def _(pool):
                def values(w, t, blk, hg):
                    at = (hg % 2) * (TILES * GW) + t * GW
                    pool.wait_ge(s_vhi, w + 1)
                    if not low(w - 4):
                        pool.wait_ge(s_pv, w - 4)
                    pool.tensor_tensor(v_s[:, 1, ds(at, GW)], v_f[:, t % 2, :], v_s[:, 0, ds(at, GW)],
                                       ALU.subtract).then_inc(s_vlo, 1)

                def slot(b, hg, s):
                    u, g = where(b, hg, s)
                    par = s % 2
                    if live(u, 0):
                        for sq, sl, ready, done in ((q_sq, q_sl, s_qsq, s_qsl), (k_sq, k_sl, s_ksq, s_ksl)):
                            pool.wait_ge(ready, u + 1)
                            if not low(u - 1):
                                pool.wait_ge(s_norm, u - 1)
                            pool.tensor_tensor(sl[:, par, :], sq[:, par, :], sq[:, par, :].bitcast(BF16)[:, 1::2],
                                               ALU.subtract).then_inc(done, 1)
                    if live(u, -2):
                        values(u + 2, (s + 2) % TILES, *group_ahead(b, hg, s))
                    if live(u, 1):
                        prev = (s - 1) % 2
                        pool.wait_ge(s_phi, u)
                        if not low(u - 2):
                            pool.wait_ge(s_pv, u - 2)
                        pool.tensor_tensor(pr_s[:, prev, 1, :], pr_f[:, prev, :], pr_s[:, prev, 0, :],
                                           ALU.subtract).then_inc(s_plo, 1)
                    if s == 0 and hg == 0 and not isinstance(b, int):
                        rows_in(b)

                def rows_in(b):
                    pool.wait_ge(s_rows, 16 * b)
                    pool.tensor_tensor(rows[:, :].rearrange("p (t h) -> p t h", h=HID),
                                       rows[:, :].rearrange("p (t h) -> p t h", h=HID),
                                       bo_b[:, :].unsqueeze(1).broadcast_to((P, TILES, HID)), ALU.add).then_inc(s_bias, 1)

                values(0, 0, 0, 0)
                values(1, 1, 0, 0)
                walk(pool, slot, lambda: rows_in(NBLK))

            @block.sync
            def _(sp):
                rows3 = rows[:, :].rearrange("p (t h) -> p t h", h=HID)

                def load(b):
                    sp.dma_start(rows3, x_v[ds(b, 1), :, :, :].rearrange("b p t h -> (b p) t h")).then_inc(s_rows, 16)

                def keep(b):
                    sp.wait_ge(s_mid, b + 1)
                    sp.dma_start(mid[ds(b, 1), :, :].rearrange("b p n -> (b p) n"), rows[:, :]).then_inc(s_kept, 16)
                    sp.wait_ge(s_kept, 16 * b + 16)

                load(0)
                with sp.Fori(0, NBLK - 1) as b:
                    keep(b)
                    load(b + 1)
                keep(NBLK - 1)

        with ExitStack() as part:
            mrows = sb("mrows", [P, 2, TILES * HID], F32, part)
            mn = sb("mn", [P, 2, TILES * HID], F32, part)
            yT = sb("yT", [P, 2, 2, KH * BLK], F16, part)
            r_f = sb("r_f", [P, 2, BLK], F32, part)
            h_f = sb("h_f", [P, 2, BLK], F32, part)
            h_s = sb("h_s", [P, 2, 2, KF * BLK], F16, part)
            res = sb("res", [P, 2, TILES * HID], F32, part)
            pause = sb("pause", [P, 1], F32, part)
            st2 = sb("st2", [P, TILES, 6], F32, part)
            mv2 = sb("mv2", [P, TILES, 2], F32, part)
            t2 = sb("t2", [P, TILES], F32, part)
            a2 = sb("a2", [P, TILES], F32, part)
            y2 = sb("y2", [P, TILES], F32, part)

            ps_y = pb("ps_y", [P, KH * BLK], part)
            ps_h = pb("ps_h", [P, 4, BLK], part)
            ps_o = pb("ps_o", [P, TILES * HID], part)

            f_rows = [sem(f"f_rows{i}", part) for i in range(2)]
            f_norm = sem("f_norm", part)
            f_chain = sem("f_chain", part)
            f_t = sem("f_t", part)
            f_thi = sem("f_thi", part)
            f_tlo = sem("f_tlo", part)
            f_h = sem("f_h", part)
            f_relu = sem("f_relu", part)
            f_sq = sem("f_sq", part)
            f_hi = sem("f_hi", part)
            f_lo = sem("f_lo", part)
            f_o = sem("f_o", part)
            f_res = sem("f_res", part)
            f_out = [sem(f"f_out{i}", part) for i in range(2)]
            CHAIN = 14

            def hidden_bank(f, par):
                return (f + par) % 4

            def gap(f, par):
                return 2 if par == 0 and f < 2 else 4

            def pipeline(main, ahead):
                def run(eng):
                    ahead(0, 0)
                    main(0, 0, True)
                    main(1, 1, True)
                    with eng.Fori(1, NBLK // 2 - 1) as pair:
                        for i in range(2):
                            main(2 * pair + i, i, True)
                    main(NBLK - 2, 0, True)
                    main(NBLK - 1, 1, False)
                return run

            block = part.enter_context(nc.Block())

            @block.sync
            def _(sp):
                def load(b, par):
                    if not low(b - 1):
                        sp.wait_ge(f_res, b - 1)
                    sp.dma_start(mrows[:, par, :], mid[ds(b, 1), :, :].rearrange("b p n -> (b p) n")).then_inc(f_rows[par], 16)

                def store(b, par):
                    sp.wait_ge(f_res, b + 1)
                    sp.dma_start(out_v[ds(b, 1), :, :, :].rearrange("b p t h -> (b p) t h"),
                                 res[:, par, :].rearrange("p (t h) -> p t h", h=HID)).then_inc(f_out[par], 16)

                load(0, 0)
                load(1, 1)
                with sp.Fori(0, NBLK // 2 - 1) as pair:
                    for i in range(2):
                        store(2 * pair + i, i)
                        load(2 * pair + (2 + i), i)
                store(NBLK - 2, 0)
                store(NBLK - 1, 1)
                for par in range(2):
                    sp.wait_ge(f_out[par], 16 * (NBLK // 2))

            @block.tensor
            def _(pe):
                def ahead(b, par):
                    pe.wait_ge(f_norm, b + 1)
                    if not low(b):
                        pe.wait_ge(f_thi, b)
                        pe.wait_ge(f_tlo, b)
                    for k in range(KH):
                        for t in range(TILES):
                            last = pe.transpose(ps_y[:, k * BLK + t * P:k * BLK + (t + 1) * P],
                                                mn[:, par, t * HID + k * P:t * HID + (k + 1) * P], ident[:, :])
                    last.then_inc(f_t, 1)

                def main(b, par, more):
                    pe.wait_ge(f_thi, b + 1)
                    pe.wait_ge(f_tlo, b + 1)
                    for f in range(KF):
                        n = KF * b + f
                        if not low(n - gap(f, par) + 1):
                            pe.wait_ge(f_sq, n - gap(f, par) + 1)
                        i = 0
                        for k in range(KH):
                            for a in range(2):
                                last = pe.matmul(ps_h[:, hidden_bank(f, par), :],
                                                 wfc_t[:, k * FFN + f * P:k * FFN + (f + 1) * P],
                                                 yT[:, par, a, k * BLK:(k + 1) * BLK], start=(i == 0), stop=(i == 3))
                                i += 1
                        last.then_inc(f_h, 1)
                    if more:
                        ahead(b + 1, 1 - par)
                    if not low(b):
                        pe.wait_ge(f_res, b)
                    pe.wait_ge(f_hi, KF * b + KF)
                    pe.wait_ge(f_lo, KF * b + KF)
                    for t in range(TILES):
                        i = 0
                        for f in range(KF):
                            for a in range(2):
                                last = pe.matmul(ps_o[:, t * HID:(t + 1) * HID],
                                                 h_s[:, par, a, f * BLK + t * P:f * BLK + (t + 1) * P],
                                                 wpr_t[:, f * HID:(f + 1) * HID], start=(i == 0), stop=(i == 2 * KF - 1))
                                i += 1
                    last.then_inc(f_o, 1)

                pipeline(main, ahead)(pe)

            @block.scalar
            def _(act):
                def ahead(b, par):
                    act.wait_ge(f_t, b + 1)
                    if not low(b - 1):
                        act.wait_ge(f_o, b - 1)
                    act.activation(yT[:, par, 0, :], ps_y[:, :], ACT.Copy).then_inc(f_thi, 1)

                def relu(b, par, f):
                    n = KF * b + f
                    act.wait_ge(f_h, n + 1)
                    if not low(n - 1):
                        act.wait_ge(f_sq, n - 1)
                    act.activation(r_f[:, (f + par) % 2, :], ps_h[:, hidden_bank(f, par), :], ACT.Relu).then_inc(f_relu, 1)

                def main(b, par, more):
                    if not low(b - 1):
                        act.wait_ge(f_o, b - 1)
                    relu(b, par, 0)
                    relu(b, par, 1)
                    for f in range(KF):
                        act.wait_ge(f_sq, KF * b + (f + 1))
                        act.activation(h_s[:, par, 0, f * BLK:(f + 1) * BLK], h_f[:, (f + par) % 2, :],
                                       ACT.Copy).then_inc(f_hi, 1)
                        if f + 2 < KF:
                            relu(b, par, f + 2)
                    if more:
                        ahead(b + 1, 1 - par)

                pipeline(main, ahead)(act)

            @block.vector
            def _(dve):
                def norm(b, par):
                    count = [CHAIN * b]

                    def link(ins):
                        count[0] = count[0] + 1
                        ins.then_inc(f_chain, 1)
                        dve.wait_ge(f_chain, count[0])

                    dve.wait_ge(f_rows[par], 16 * ((b - par) // 2 + 1))
                    for t in range(TILES):
                        ins = dve.bn_stats(st2[:, t, :], mrows[:, par, t * HID:(t + 1) * HID])
                    link(ins)
                    dve.memset(pause[:, :], 0.0)
                    for t in range(TILES):
                        ins = dve.bn_aggr(mv2[:, t, :], st2[:, t, :])
                    link(ins)
                    link(dve.tensor_scalar(t2[:, :], mv2[:, :, 1], LN_EPS, None, ALU.add))
                    link(dve.tensor_scalar(a2[:, :].bitcast(I32), t2[:, :].bitcast(I32), 1, None, ALU.logical_shift_right))
                    link(dve.tensor_scalar(y2[:, :].bitcast(I32), a2[:, :].bitcast(I32), -1, RSQRT_GUESS, ALU.mult, ALU.add))
                    for _ in range(3):
                        link(dve.scalar_tensor_tensor(out=a2[:, :], in0=y2[:, :], scalar=-0.5, in1=y2[:, :],
                                                      op0=ALU.mult, op1=ALU.mult))
                        link(dve.tensor_tensor(a2[:, :], a2[:, :], t2[:, :], ALU.mult))
                        link(dve.scalar_tensor_tensor(out=y2[:, :], in0=a2[:, :], scalar=1.5, in1=y2[:, :],
                                                      op0=ALU.add, op1=ALU.mult))
                    if not low(b - 1):
                        dve.wait_ge(f_t, b - 1)
                    for t in range(TILES):
                        ins = dve.tensor_scalar(mn[:, par, t * HID:(t + 1) * HID], mrows[:, par, t * HID:(t + 1) * HID],
                                                mv2[:, t, 0:1], y2[:, t:t + 1], ALU.subtract, ALU.mult)
                    ins.then_inc(f_norm, 1)

                def lower(b, par):
                    dve.wait_ge(f_thi, b + 1)
                    if not low(b - 1):
                        dve.wait_ge(f_o, b - 1)
                    dve.tensor_tensor(yT[:, par, 1, :], ps_y[:, :], yT[:, par, 0, :], ALU.subtract).then_inc(f_tlo, 1)

                def square(b, par, f):
                    n = KF * b + f
                    dve.wait_ge(f_relu, n + 1)
                    if not low(n - 1):
                        dve.wait_ge(f_hi, n - 1)
                        dve.wait_ge(f_lo, n - 1)
                    dve.tensor_tensor(h_f[:, (f + par) % 2, :], ps_h[:, hidden_bank(f, par), :],
                                      r_f[:, (f + par) % 2, :], ALU.mult).then_inc(f_sq, 1)

                def main(b, par, more):
                    for f in range(3):
                        square(b, par, f)
                    if more:
                        norm(b + 1, 1 - par)
                    for f in range(3, KF):
                        square(b, par, f)
                    if more:
                        lower(b + 1, 1 - par)
                    dve.wait_ge(f_o, b + 1)
                    if not low(b - 1):
                        dve.wait_ge(f_out[par], 16 * ((b - par) // 2))
                    for i in range(2):
                        half = slice(i * 512, (i + 1) * 512)
                        ins = dve.scalar_tensor_tensor(out=res[:, par, half], in0=ps_o[:, half], scalar=ffn_unscale[:, :],
                                                       in1=mrows[:, par, half], op0=ALU.mult, op1=ALU.add)
                    ins.then_inc(f_res, 1)

                def ahead(b, par):
                    norm(b, par)
                    lower(b, par)

                pipeline(main, ahead)(dve)

            @block.gpsimd
            def _(pool):
                def ahead(b, par):
                    pass

                def main(b, par, more):
                    if not low(b - 1):
                        pool.wait_ge(f_o, b - 1)
                    for f in range(KF):
                        at = slice(f * BLK, (f + 1) * BLK)
                        pool.wait_ge(f_hi, KF * b + (f + 1))
                        pool.tensor_tensor(h_s[:, par, 1, at], h_f[:, (f + par) % 2, :], h_s[:, par, 0, at],
                                           ALU.subtract).then_inc(f_lo, 1)

                pipeline(main, ahead)(pool)


def kernel(L0_attn_hidden_states, L0_attn_q_w, L0_attn_q_b, L0_attn_k_w, L0_attn_k_b, L0_attn_v_w, L0_attn_v_b,
           L0_attn_a_w, L0_attn_a_b, L0_attn_b_w, L0_attn_b_b, L0_attn_og_w, L0_attn_o_w, L0_attn_o_b,
           L0_ffn_w_fc, L0_ffn_w_proj):
    import numpy as np
    import concourse.bacc as bacc
    from concourse.bass_utils import run_bass_kernel_spmd

    def tiled(w):
        w = np.asarray(w)
        n, c = w.shape
        return np.ascontiguousarray(w.T.reshape(c // P, P, n).transpose(1, 0, 2).reshape(P, c // P * n))

    def columns(b):
        return np.ascontiguousarray(np.asarray(b).reshape(HEADS, P).T)

    shape = L0_attn_hidden_states.shape
    arrays = {
        "x": np.ascontiguousarray(np.asarray(L0_attn_hidden_states).reshape(TOK, HID)),
        "wq": tiled(L0_attn_q_w), "wk": tiled(L0_attn_k_w), "wv": tiled(L0_attn_v_w), "wg": tiled(L0_attn_og_w),
        "wo": tiled(L0_attn_o_w), "wb": tiled(L0_attn_b_w),
        "bq": columns(L0_attn_q_b), "bk": columns(L0_attn_k_b), "bv": columns(L0_attn_v_b),
        "bv_row": np.asarray(L0_attn_v_b), "bb": np.asarray(L0_attn_b_b), "bo": np.asarray(L0_attn_o_b),
        "wfc": tiled(L0_ffn_w_fc), "wpr": tiled(L0_ffn_w_proj),
    }
    nc = bacc.Bacc("TRN2", target_bir_lowering=False, num_devices=1)
    aps = {n: nc.dram_tensor(f"in_{n}", a.shape, mybir.dt.from_np(a.dtype), kind="ExternalInput").ap()
           for n, a in arrays.items()}
    aps["out"] = nc.dram_tensor("out_rows", (TOK, HID), F32, kind="ExternalOutput").ap()
    build(nc, **aps)
    r = run_bass_kernel_spmd(nc, [{f"in_{n}": a for n, a in arrays.items()}], core_ids=[0])
    return r.results[0]["out_rows"].reshape(shape)
```

```python
from contextlib import ExitStack

import concourse.bass as bass
from concourse import mybir

ALU = mybir.AluOpType
ACT = mybir.ActivationFunctionType
AX_X = mybir.AxisListType.X
F32 = mybir.dt.float32
F16 = mybir.dt.float16
BF16 = mybir.dt.bfloat16
I32 = mybir.dt.int32

P = 128
TOK = 8 * 512
HID = 256
KH = HID // P
HEADS = 16
WIDE = HEADS * P
CHUNK = 64
BLK = 512
TILES = BLK // P
NBLK = TOK // BLK
NTILE = TOK // P
GROUP = 4
GW = GROUP * P
FFN = 640
KF = FFN // P
LN_CHUNK = 8
RING = 3
UNITS = NBLK * HEADS
NORM_STEPS = 14
RSQRT_GUESS = 0x5F3759DF
LN_EPS = 1e-5
L2_EPS = 1e-12

ds = bass.ds


def low(n):
    return isinstance(n, int) and n <= 0


def build(nc, x, wq, wk, wv, wg, wo, wb, bq, bk, bv, bv_row, bb, bo, wfc, wpr, out):
    x_v = x.rearrange("(b t p) h -> b p t h", t=TILES, p=P)
    x_c = x.rearrange("(c t p) h -> c p t h", t=LN_CHUNK, p=P)
    out_v = out.rearrange("(b t p) h -> b p t h", t=TILES, p=P)
    mid = nc.dram_tensor("mid_rows", [NBLK, P, TILES * HID], F32, kind="Internal").ap()

    with ExitStack() as whole:
        def sb(name, shape, dt, ctx=whole):
            return ctx.enter_context(nc.sbuf_tensor(name, shape, dt))

        def pb(name, shape, ctx, dt=F32):
            return ctx.enter_context(nc.psum_tensor(name, shape, dt))

        def sem(name, ctx=whole):
            return ctx.enter_context(nc.semaphore(name))

        wq_s = sb("wq_s", [P, 2, KH * WIDE], F16)
        wk_s = sb("wk_s", [P, 2, KH * WIDE], F16)
        wv_s = sb("wv_s", [P, 2, KH * WIDE], F16)
        wg_s = sb("wg_s", [P, 2, KH * WIDE], F16)
        wo_s = sb("wo_s", [P, 2, HEADS * HID], F16)
        wfc_t = sb("wfc_t", [P, KH * FFN], F16)
        wpr_t = sb("wpr_t", [P, KF * HID], F16)
        xT = sb("xT", [P, 2, KH * TOK], F16)
        beta = sb("beta", [P, NTILE, HEADS], F32)
        bq_c = sb("bq_c", [P, HEADS], F32)
        bk_c = sb("bk_c", [P, HEADS], F32)
        bv_b = sb("bv_b", [P, WIDE], F32)
        bo_b = sb("bo_b", [P, HID], F32)
        ident = sb("ident", [P, P], F32)
        mask = sb("mask", [P, P], F32)
        ones16 = sb("ones16", [P, 2], F16)
        scale = sb("scale", [P, 5], F32)
        unscale = sb("unscale", [P, 5], F32)
        eps_sq = sb("eps_sq", [P, 1], F32)
        gate_k = sb("gate_k", [P, 1], F32)
        out_unscale = sb("out_unscale", [P, 1], F32)
        ffn_unscale = sb("ffn_unscale", [P, 1], F32)

        QK, V, G, O, B = range(5)

        def wcol(w, part, k, start, n):
            return w[:, part, ds(k * WIDE + start, n)]

        with ExitStack() as part:
            raw = sb("raw", [P, RING, KH * WIDE], F32, part)
            xc = sb("xc", [P, 2, LN_CHUNK * HID], F32, part)
            xn = sb("xn", [P, 4, HID], F32, part)
            b_sq = sb("b_sq", [P, 5 * HEADS], BF16, part)
            ones_bf = sb("ones_bf", [P, P], BF16, part)
            ones_f = sb("ones_f", [P, P], F32, part)
            wb_raw = sb("wb_raw", [P, KH * HEADS], F32, part)
            wb_s = sb("wb_s", [P, 2, KH * HEADS], F16, part)
            bb_b = sb("bb_b", [P, HEADS], F32, part)
            bv_c = sb("bv_c", [P, HEADS], F32, part)
            wfc_r = sb("wfc_r", [P, KH * FFN], F32, part)
            wpr_r = bv_b[:, 0:KF * HID]
            stats = sb("stats", [P, LN_CHUNK, 6], F32, part)
            mv = sb("mv", [P, LN_CHUNK, 2], F32, part)
            t_ln = sb("t_ln", [P, LN_CHUNK], F32, part)
            a_ln = sb("a_ln", [P, LN_CHUNK], F32, part)
            y_ln = sb("y_ln", [P, LN_CHUNK], F32, part)
            peak = sb("peak", [P, 8], F32, part)
            tiny = sb("tiny", [P, 8], F32, part)
            z = wfc_r[:, 0:NTILE * HEADS]
            ez = wfc_r[:, NTILE * HEADS:2 * NTILE * HEADS]
            uz = xc[:, 0, 0:NTILE * HEADS]
            lz = xc[:, 1, 0:NTILE * HEADS]
            fsum = sb("fsum", [P, 2], F32, part)
            fmean = sb("fmean", [P, 2], F32, part)
            thr = sb("thr", [P, 2], F32, part)
            nthr = sb("nthr", [P, 2], F32, part)

            ps_t = [pb(f"ps_t{i}", [P, 512], part) for i in range(2)]
            ps_n = pb("ps_n", [P, WIDE], part)
            ps_s = pb("ps_s", [P, 512], part)
            ps_z = pb("ps_z", [P, 512], part)

            s_small = sem("s_small", part)
            s_wide = sem("s_wide", part)
            s_bv = sem("s_bv", part)
            s_tern = sem("s_tern", part)
            s_x = [sem(f"s_x{i}", part) for i in range(2)]
            s_raw = [sem(f"s_raw{i}", part) for i in range(5)]
            s_const = sem("s_const", part)
            s_chain = sem("s_chain", part)
            s_xn = sem("s_xn", part)
            s_xt = sem("s_xt", part)
            s_xhi = sem("s_xhi", part)
            s_xlo = sem("s_xlo", part)
            s_wsq = sem("s_wsq", part)
            s_bsq = sem("s_bsq", part)
            s_bnorm = sem("s_bnorm", part)
            s_wnorm = sem("s_wnorm", part)
            s_peak = sem("s_peak", part)
            s_scale = sem("s_scale", part)
            s_whi = sem("s_whi", part)
            s_wpre = sem("s_wpre", part)
            s_wlo = [sem(f"s_wlo{i}", part) for i in range(5)]
            s_bread = sem("s_bread", part)
            s_z = sem("s_z", part)
            s_beta = sem("s_beta", part)
            s_bact = sem("s_bact", part)
            s_bt = sem("s_bt", part)
            s_abs = sem("s_abs", part)
            s_fsum = sem("s_fsum", part)

            RAWS = [(wq, wq_s, QK), (wk, wk_s, QK), (wv, wv_s, V), (wg, wg_s, G), (wo, wo_s, O)]
            NORMS = ((0, 1), (2,), (3,), (4,))
            POOL_LOWER = (1, 2, 3)
            SMALL = 4 * 16
            NWIDE = 4 * 16
            NX = NTILE // LN_CHUNK
            PAIRS = NTILE // 2

            def squares(j):
                return RAWS[j][1][:, 0, :].bitcast(BF16)

            block = part.enter_context(nc.Block())

            @block.sync
            def _(sp):
                def load_x(c):
                    if c >= 2:
                        sp.wait_ge(s_xn, (c - 1) * LN_CHUNK)
                    sp.dma_start(xc[:, c % 2, :].rearrange("p (t h) -> p t h", h=HID), x_c[c]).then_inc(s_x[c % 2], 16)

                def load_raw(j):
                    if j >= RING:
                        sp.wait_ge(s_whi, j - RING + 1)
                        sp.wait_ge(s_wlo[j - RING], 1)
                    sp.dma_start(raw[:, j % RING, :], RAWS[j][0]).then_inc(s_raw[j], 16)

                load_x(0)
                for dst, src in ((wb_raw[:, :], wb), (bq_c[:, :], bq), (bk_c[:, :], bk), (bv_c[:, :], bv)):
                    sp.dma_start(dst, src).then_inc(s_small, 16)
                load_raw(0)
                load_x(1)
                load_raw(1)
                for dst, src, n in ((bb_b, bb, HEADS), (bo_b, bo, HID)):
                    sp.dma_start(dst[:, :], bass.AP(src.tensor, 0, [[0, P], [1, n]])).then_inc(s_wide, 16)
                sp.dma_start(wfc_r[:, :], wfc).then_inc(s_wide, 16)
                sp.dma_start(wpr_r, wpr).then_inc(s_wide, 16)
                load_raw(2)
                load_x(2)
                load_x(3)
                load_raw(3)
                sp.wait_ge(s_tern, 1)
                sp.dma_start(bv_b[:, :], bass.AP(bv_row.tensor, 0, [[0, P], [1, WIDE]])).then_inc(s_bv, 16)
                load_raw(4)

            @block.gpsimd
            def _(pool):
                pool.memset(ident[:, :], 0.0).then_inc(s_const, 1)
                pool.memset(mask[:, :], 1.0).then_inc(s_const, 1)
                pool.wait_ge(s_const, 2)
                pool.affine_select(out=ident[:, :], in_=ident[:, :], compare_op=ALU.not_equal, fill=1.0, base=0,
                                   pattern=[[-1, P]], channel_multiplier=1).then_inc(s_const, 1)
                pool.affine_select(out=mask[:, :], in_=mask[:, :], compare_op=ALU.is_ge, fill=0.0, base=0,
                                   pattern=[[1, P]], channel_multiplier=-1).then_inc(s_const, 1)
                pool.wait_ge(s_const, 4)
                pool.memset(mask[0:CHUNK, CHUNK:P], 0.0).then_inc(s_const, 1)
                pool.memset(ones16[:, :], 1.0).then_inc(s_const, 1)
                pool.memset(ones_bf[:, :], 1.0).then_inc(s_const, 1)
                pool.memset(ones_f[:, :], 1.0).then_inc(s_const, 1)

                for j in POOL_LOWER:
                    pool.wait_ge(s_whi, j + 1)
                    _, dst, _ = RAWS[j]
                    pool.tensor_tensor(dst[:, 1, :], raw[:, j % RING, :], dst[:, 0, :], ALU.subtract).then_inc(s_wlo[j], 1)

            @block.scalar
            def _(act):
                def square_small():
                    act.wait_ge(s_small, SMALL)
                    for i, b in enumerate((bq_c, bk_c, bv_c)):
                        act.activation(b_sq[:, i * HEADS:(i + 1) * HEADS], b[:, :], ACT.Square,
                                       scale=1.0 / 16).then_inc(s_bsq, 1)
                    act.activation(b_sq[:, 3 * HEADS:5 * HEADS], wb_raw[:, :], ACT.Square).then_inc(s_bsq, 1)

                def square(j):
                    act.wait_ge(s_raw[j], 16)
                    act.activation(squares(j), raw[:, j % RING, :], ACT.Square).then_inc(s_wsq, 1)

                def split_hi(j):
                    _, dst, which = RAWS[j]
                    act.wait_ge(s_scale, which + 1)
                    place = raw[:, j % RING, :]
                    if j in POOL_LOWER:
                        act.activation(place, place, ACT.Copy, scale=scale[:, which:which + 1]).then_inc(s_wpre, 1)
                        act.wait_ge(s_wpre, POOL_LOWER.index(j) + 1)
                        act.activation(dst[:, 0, :], place, ACT.Copy).then_inc(s_whi, 1)
                    else:
                        act.activation(dst[:, 0, :], place, ACT.Copy, scale=scale[:, which:which + 1]).then_inc(s_whi, 1)

                def x_hi(first, last):
                    for m in range(first, last):
                        act.wait_ge(s_xt, m + 1)
                        act.activation(xT[:, 0, :].rearrange("p (k n) -> p k n", k=KH)[:, :, m * 256:(m + 1) * 256],
                                       ps_t[m % 2][:, :].rearrange("p (k n) -> p k n", k=KH), ACT.Copy).then_inc(s_xhi, 1)

                square_small()
                square(0)
                x_hi(0, 4)
                square(1)
                x_hi(4, 8)
                act.wait_ge(s_wide, NWIDE)
                for i, (w, w_t) in enumerate(((wfc_r[:, :], wfc_t), (wpr_r, wpr_t))):
                    act.activation(w_t[:, :], w, ACT.Abs, accum_out=fsum[:, i:i + 1]).then_inc(s_abs, 1)
                square(2)
                split_hi(0)
                split_hi(1)
                split_hi(2)
                x_hi(8, 12)
                square(3)
                x_hi(12, 16)
                square(4)
                split_hi(3)
                split_hi(4)
                act.wait_ge(s_beta, 1)
                act.activation(lz, z, ACT.Abs).then_inc(s_bact, 1)
                act.wait_ge(s_bact, 1)
                act.activation(ez, lz, ACT.Exp, scale=-1.0).then_inc(s_bact, 1)
                act.wait_ge(s_beta, 2)
                act.activation(lz, uz, ACT.Ln).then_inc(s_bact, 1)

            @block.vector
            def _(dve):
                chain = [0]

                def link(ins):
                    chain[0] += 1
                    ins.then_inc(s_chain, 1)
                    dve.wait_ge(s_chain, chain[0])

                def rsqrt(y, a, t, rounds=3):
                    link(dve.tensor_scalar(a.bitcast(I32), t.bitcast(I32), 1, None, ALU.logical_shift_right))
                    link(dve.tensor_scalar(y.bitcast(I32), a.bitcast(I32), -1, RSQRT_GUESS, ALU.mult, ALU.add))
                    for _ in range(rounds):
                        link(dve.scalar_tensor_tensor(out=a, in0=y, scalar=-0.5, in1=y, op0=ALU.mult, op1=ALU.mult))
                        link(dve.tensor_tensor(a, a, t, ALU.mult))
                        link(dve.scalar_tensor_tensor(out=y, in0=a, scalar=1.5, in1=y, op0=ALU.add, op1=ALU.mult))

                def power(dst, src, which):
                    a = tiny[:, 0:1].bitcast(I32)
                    link(dve.tensor_scalar(a, src.bitcast(I32), 23, None, ALU.logical_shift_right))
                    link(dve.tensor_scalar(a, a, 131, None, ALU.add))
                    link(dve.tensor_scalar(a, a, 1, None, ALU.logical_shift_right))
                    b = tiny[:, 1:2].bitcast(I32)
                    link(dve.tensor_scalar(b, a, -1, 259, ALU.mult, ALU.add))
                    link(dve.tensor_scalar(dst.bitcast(I32), b, 23, None, ALU.logical_shift_left))
                    link(dve.tensor_scalar(a, a, -5, None, ALU.add))
                    link(dve.tensor_scalar(unscale[:, which:which + 1].bitcast(I32), a, 23, None, ALU.logical_shift_left))

                def normalise(c):
                    dve.wait_ge(s_x[c % 2], 16 * (c // 2 + 1))
                    rows = xc[:, c % 2, :].rearrange("p (t h) -> p t h", h=HID)
                    for t in range(LN_CHUNK):
                        ins = dve.bn_stats(stats[:, t, :], rows[:, t, :])
                    link(ins)
                    for t in range(LN_CHUNK):
                        ins = dve.bn_aggr(mv[:, t, :], stats[:, t, :])
                    link(ins)
                    link(dve.tensor_scalar(t_ln[:, :], mv[:, :, 1], LN_EPS, None, ALU.add))
                    rsqrt(y_ln[:, :], a_ln[:, :], t_ln[:, :])
                    for t in range(LN_CHUNK):
                        n = c * LN_CHUNK + t
                        if n >= 4:
                            dve.wait_ge(s_xt, (n - 4) // 2 + 1)
                        dve.tensor_scalar(xn[:, n % 4, :], rows[:, t, :], mv[:, t, 0:1], y_ln[:, t:t + 1],
                                          ALU.subtract, ALU.mult).then_inc(s_xn, 1)
                        if t % 2 and n > 1:
                            x_lo(n // 2 - 1)

                def x_lo(m):
                    dve.wait_ge(s_xhi, m + 1)
                    view = xT[:, :, :].rearrange("p s (k n) -> p s k n", k=KH)
                    dve.tensor_tensor(view[:, 1, :, m * 256:(m + 1) * 256],
                                      ps_t[m % 2][:, :].rearrange("p (k n) -> p k n", k=KH),
                                      view[:, 0, :, m * 256:(m + 1) * 256], ALU.subtract).then_inc(s_xlo, 1)

                def top(i, which):
                    dve.wait_ge(s_wnorm, i + 1)
                    n = WIDE if which != O else 512
                    dve.tensor_reduce(peak[:, i:i + 1], ps_n[:, 0:n], AX_X, ALU.max).then_inc(s_peak, 1)
                    dve.wait_ge(s_peak, i + 1)
                    if which in (QK, V):
                        bias = peak[:, 6 + which:7 + which]
                        link(dve.tensor_tensor(peak[:, i:i + 1], peak[:, i:i + 1], bias, ALU.add))
                    link(dve.tensor_scalar(peak[:, i:i + 1], peak[:, i:i + 1], 1e-30, None, ALU.max))
                    power(scale[:, which:which + 1], peak[:, i:i + 1], which)
                    dve.nop().then_inc(s_scale, 1)

                def split_lo(j):
                    _, dst, which = RAWS[j]
                    dve.wait_ge(s_whi, j + 1)
                    dve.scalar_tensor_tensor(out=dst[:, 1, :], in0=raw[:, j % RING, :], scalar=scale[:, which:which + 1],
                                             in1=dst[:, 0, :], op0=ALU.mult, op1=ALU.subtract).then_inc(s_wlo[j], 1)

                normalise(0)
                dve.wait_ge(s_bnorm, 1)
                link(dve.tensor_reduce(peak[:, 6:7], ps_s[:, 0:2 * HEADS], AX_X, ALU.max))
                link(dve.tensor_reduce(peak[:, 7:8], ps_s[:, 2 * HEADS:3 * HEADS], AX_X, ALU.max))
                dve.tensor_reduce(peak[:, 5:6], ps_s[:, 3 * HEADS:5 * HEADS], AX_X, ALU.max).then_inc(s_bread, 1)
                dve.wait_ge(s_bread, 1)
                link(dve.tensor_scalar(peak[:, 5:6], peak[:, 5:6], 2.0, 1e-30, ALU.mult, ALU.max))
                power(scale[:, B:B + 1], peak[:, 5:6], B)
                link(dve.tensor_scalar(wb_s[:, 0, :], wb_raw[:, :], scale[:, B:B + 1], None, ALU.mult))
                link(dve.scalar_tensor_tensor(out=wb_s[:, 1, :], in0=wb_raw[:, :], scalar=scale[:, B:B + 1],
                                              in1=wb_s[:, 0, :], op0=ALU.mult, op1=ALU.subtract))
                normalise(1)
                top(0, QK)
                link(dve.tensor_scalar(tiny[:, 2:3], scale[:, QK:QK + 1], L2_EPS, None, ALU.mult))
                link(dve.tensor_tensor(eps_sq[:, :], tiny[:, 2:3], tiny[:, 2:3], ALU.mult))
                link(dve.tensor_scalar(bq_c[:, :], bq_c[:, :], scale[:, QK:QK + 1], None, ALU.mult))
                link(dve.tensor_scalar(bk_c[:, :], bk_c[:, :], scale[:, QK:QK + 1], None, ALU.mult))
                split_lo(0)
                top(1, V)
                dve.wait_ge(s_fsum, 1)
                link(dve.tensor_scalar(fmean[:, :], ps_s[:, 128:130], 1.0 / (FFN * HID), 1e-5, ALU.mult, ALU.max))
                link(dve.tensor_scalar(thr[:, :], fmean[:, :], 0.7, None, ALU.mult))
                link(dve.tensor_scalar(nthr[:, :], thr[:, :], -1.0, None, ALU.mult))
                for i, (w, dst) in enumerate(((wfc_r[:, :], wfc_t), (wpr_r, wpr_t))):
                    link(dve.tensor_scalar(dst[:, :], w, nthr[:, i:i + 1], None, ALU.is_lt))
                    link(dve.scalar_tensor_tensor(out=dst[:, :], in0=w, scalar=thr[:, i:i + 1], in1=dst[:, :],
                                                  op0=ALU.is_gt, op1=ALU.subtract))
                dve.nop().then_inc(s_tern, 1)
                link(dve.tensor_scalar(wfc_t[:, :], wfc_t[:, :], 0.25, None, ALU.mult))
                link(dve.scalar_tensor_tensor(out=ffn_unscale[:, :], in0=fmean[:, 0:1], scalar=16.0, in1=fmean[:, 0:1],
                                              op0=ALU.mult, op1=ALU.mult))
                link(dve.tensor_tensor(ffn_unscale[:, :], ffn_unscale[:, :], fmean[:, 1:2], ALU.mult))
                normalise(2)
                normalise(3)
                x_lo(PAIRS - 1)
                top(2, G)
                dve.wait_ge(s_bv, 16)
                link(dve.tensor_scalar(bv_b[:, :], bv_b[:, :], scale[:, V:V + 1], None, ALU.mult))
                top(3, O)
                split_lo(4)
                dve.wait_ge(s_wide, NWIDE)
                dve.wait_ge(s_z, 1)
                z3 = z.rearrange("p (t h) -> p t h", h=HEADS)
                bb3 = bb_b[:, :].unsqueeze(1).broadcast_to((P, NTILE, HEADS))
                dve.scalar_tensor_tensor(out=z3, in0=ps_z.rearrange("p (t h) -> p t h", h=HEADS),
                                         scalar=unscale[:, B:B + 1], in1=bb3, op0=ALU.mult, op1=ALU.add).then_inc(s_beta, 1)
                dve.wait_ge(s_bact, 2)
                dve.tensor_scalar(uz, ez, 1.0, None, ALU.add).then_inc(s_beta, 1)
                dve.wait_ge(s_bact, 3)
                b2 = beta[:, :, :].rearrange("p t h -> p (t h)")
                dve.wait_ge(s_beta, 2)
                link(dve.tensor_scalar(b2, uz, -1.0, 1e-30, ALU.add, ALU.max))
                link(dve.reciprocal(b2, b2))
                link(dve.tensor_tensor(b2, b2, ez, ALU.mult))
                link(dve.tensor_tensor(b2, b2, lz, ALU.mult))
                link(dve.tensor_scalar(uz, uz, 1.0, None, ALU.is_equal))
                link(dve.tensor_tensor(uz, uz, ez, ALU.mult))
                link(dve.tensor_tensor(b2, b2, uz, ALU.add))
                link(dve.scalar_tensor_tensor(out=b2, in0=z, scalar=0.0, in1=b2, op0=ALU.max, op1=ALU.add))
                dve.tensor_reduce(tiny[:, 3:4], b2, AX_X, ALU.max).then_inc(s_bt, 1)
                dve.wait_ge(s_bt, 2)
                dve.tensor_reduce(tiny[0:1, 4:5], ps_t[0][0:1, 0:P], AX_X, ALU.max).then_inc(s_bt, 1)
                dve.wait_ge(s_bt, 4)
                a = tiny[:, 5:6].bitcast(I32)
                link(dve.tensor_scalar(tiny[:, 6:7], ps_t[1][:, 0:1], 1e-30, None, ALU.max))
                link(dve.tensor_scalar(a, tiny[:, 6:7].bitcast(I32), 23, None, ALU.logical_shift_right))
                link(dve.tensor_scalar(tiny[:, 0:1].bitcast(I32), a, -1, 253, ALU.mult, ALU.add))
                link(dve.tensor_scalar(tiny[:, 1:2].bitcast(I32), tiny[:, 0:1].bitcast(I32), 23, None, ALU.logical_shift_left))
                link(dve.tensor_scalar(b2, b2, tiny[:, 1:2], None, ALU.mult))
                link(dve.tensor_scalar(a, a, 1, None, ALU.add))
                link(dve.tensor_scalar(tiny[:, 2:3].bitcast(I32), a, 23, None, ALU.logical_shift_left))
                link(dve.tensor_scalar(gate_k[:, :], scale[:, G:G + 1], 2.0 ** -15, None, ALU.mult))
                link(dve.scalar_tensor_tensor(out=out_unscale[:, :], in0=unscale[:, V:V + 1], scalar=2.0 ** 8,
                                              in1=unscale[:, G:G + 1], op0=ALU.mult, op1=ALU.mult))
                link(dve.tensor_tensor(out_unscale[:, :], out_unscale[:, :], unscale[:, O:O + 1], ALU.mult))
                link(dve.tensor_tensor(out_unscale[:, :], out_unscale[:, :], tiny[:, 2:3], ALU.mult))

            @block.tensor
            def _(pe):
                pe.wait_ge(s_const, 8)

                def transposes(first, last):
                    for m in range(first, last):
                        pe.wait_ge(s_xn, 2 * m + 2)
                        if m >= 2:
                            pe.wait_ge(s_xhi, m - 1)
                            pe.wait_ge(s_xlo, m - 1)
                        for k in range(KH):
                            for t in range(2):
                                last_t = pe.transpose(ps_t[m % 2][:, k * 256 + t * P:k * 256 + (t + 1) * P],
                                                      xn[:, (2 * m + t) % 4, k * P:(k + 1) * P], ident[:, :])
                        last_t.then_inc(s_xt, 1)

                def norms(i):
                    together = NORMS[i]
                    pe.wait_ge(s_wsq, together[-1] + 1)
                    if i:
                        pe.wait_ge(s_peak, i)
                    if RAWS[together[0]][2] != O:
                        for n in range(WIDE // 512):
                            tiles = [(j, k) for j in together for k in range(KH)]
                            for j, k in tiles:
                                last = pe.matmul(ps_n[:, n * 512:(n + 1) * 512], ones_bf[:, :],
                                                 squares(j)[:, k * WIDE + n * 512:k * WIDE + (n + 1) * 512],
                                                 start=((j, k) == tiles[0]), stop=((j, k) == tiles[-1]))
                    else:
                        for n in range(HEADS // 2):
                            last = pe.matmul(ps_n[:, 0:512], ones_bf[:, :], squares(together[0])[:, n * 512:(n + 1) * 512],
                                             start=(n == 0), stop=(n == HEADS // 2 - 1))
                    last.then_inc(s_wnorm, 1)

                pe.wait_ge(s_bsq, 4)
                pe.matmul(ps_s[:, 0:5 * HEADS], ones_bf[:, :], b_sq[:, :], start=True, stop=True).then_inc(s_bnorm, 1)
                transposes(0, 8)
                norms(0)
                norms(1)
                pe.wait_ge(s_abs, 2)
                pe.wait_ge(s_bread, 1)
                pe.matmul(ps_s[:, 128:130], ones_f[:, :], fsum[:, :], start=True, stop=True).then_inc(s_fsum, 1)
                transposes(8, 12)
                transposes(12, 16)
                norms(2)
                norms(3)
                pe.wait_ge(s_xhi, PAIRS)
                pe.wait_ge(s_xlo, PAIRS)
                for t in range(NTILE):
                    n = 0
                    for k in range(KH):
                        for a, b in ((0, 0), (0, 1), (1, 0)):
                            last = pe.matmul(ps_z[:, t * HEADS:(t + 1) * HEADS],
                                             xT[:, a, k * TOK + t * P:k * TOK + (t + 1) * P],
                                             wb_s[:, b, k * HEADS:(k + 1) * HEADS], start=(n == 0), stop=(n == 5))
                            n += 1
                last.then_inc(s_z, 1)
                pe.wait_ge(s_bt, 1)
                pe.transpose(ps_t[0][0:1, 0:P], tiny[:, 3:4], ident[:, :]).then_inc(s_bt, 1)
                pe.wait_ge(s_bt, 3)
                pe.matmul(ps_t[1][:, 0:1], ones_f[0:1, :], tiny[0:1, 4:5], start=True, stop=True).then_inc(s_bt, 1)

        with ExitStack() as part:
            q_s = sb("q_s", [P, 2, 2, BLK], F16, part)
            k_s = sb("k_s", [P, 2, 2, BLK], F16, part)
            q_sq = sb("q_sq", [P, 2, BLK], F32, part)
            k_sq = sb("k_sq", [P, 2, BLK], F32, part)
            q_sl = sb("q_sl", [P, 2, BLK], F16, part)
            k_sl = sb("k_sl", [P, 2, BLK], F16, part)
            v_f = sb("v_f", [P, 2, GW], F32, part)
            v_s = sb("v_s", [P, 2, 2 * TILES * GW], F16, part)
            gate = sb("gate", [P, 2 * TILES * GW], F32, part)
            pr_f = sb("pr_f", [P, 2, BLK], F32, part)
            pr_s = sb("pr_s", [P, 2, 2, BLK], F16, part)
            og = sb("og", [P, 2, BLK], F32, part)
            ogT = sb("ogT", [P, 2, 2, BLK], F16, part)
            rows = sb("rows", [P, TILES * HID], F32, part)
            t_n = sb("t_n", [P, 8], F32, part)
            a_n = sb("a_n", [P, 8], F32, part)
            y_n = sb("y_n", [P, 8], F32, part)
            c_k = sb("c_k", [P, 2, TILES], F32, part)
            c_q = sb("c_q", [P, 2, TILES], F32, part)

            ps_qv = pb("ps_qv", [P, 512], part)
            ps_kg = pb("ps_kg", [P, 512], part)
            ps_sc = pb("ps_sc", [P, 512], part)
            ps_nm = pb("ps_nm", [P, 512], part)
            ps_pv = pb("ps_pv", [P, 512], part)
            ps_tr = pb("ps_tr", [P, 512], part)
            ps_acc = pb("ps_acc", [P, TILES * HID], part)

            s_q = sem("s_q", part)
            s_k = sem("s_k", part)
            s_v = sem("s_v", part)
            s_g = sem("s_g", part)
            s_score = sem("s_score", part)
            s_norm = sem("s_norm", part)
            s_pv = sem("s_pv", part)
            s_tr = sem("s_tr", part)
            s_acc = sem("s_acc", part)
            s_qhi = sem("s_qhi", part)
            s_khi = sem("s_khi", part)
            s_qsq = sem("s_qsq", part)
            s_ksq = sem("s_ksq", part)
            s_vhi = sem("s_vhi", part)
            s_gate = sem("s_gate", part)
            s_phi = sem("s_phi", part)
            s_ohi = sem("s_ohi", part)
            s_qlo = sem("s_qlo", part)
            s_klo = sem("s_klo", part)
            s_vf = sem("s_vf", part)
            s_newton = sem("s_newton", part)
            s_p = sem("s_p", part)
            s_og = sem("s_og", part)
            s_olo = sem("s_olo", part)
            s_mid = sem("s_mid", part)
            s_qsl = sem("s_qsl", part)
            s_ksl = sem("s_ksl", part)
            s_vlo = sem("s_vlo", part)
            s_plo = sem("s_plo", part)
            s_bias = sem("s_bias", part)
            s_rows = sem("s_rows", part)
            s_kept = sem("s_kept", part)

            PARTS = ((0, 0), (0, 1), (1, 0))

            def where(b, hg, s):
                g = NBLK_GROUPS * b + hg
                return GROUP * g + s, g

            NBLK_GROUPS = HEADS // GROUP

            def group_ahead(b, hg, s):
                if s < 2:
                    return b, hg
                return (b, hg + 1) if hg + 1 < NBLK_GROUPS else (b + 1, 0)

            def back(b, hg, s, lag):
                pos = GROUP * hg + s - lag
                g = NBLK_GROUPS * b + hg
                if pos < 0:
                    return b - 1, pos + HEADS, g - 1, (s - lag) % GROUP
                return b, pos, g if s >= lag else g - 1, (s - lag) % GROUP

            def walk(eng, slot, finish):
                slots = [(hg, s) for hg in range(NBLK_GROUPS) for s in range(GROUP)]
                for hg, s in slots[:GROUP]:
                    slot(0, hg, s)
                with eng.Fori(0, NBLK - 1) as b:
                    for hg, s in slots[GROUP:]:
                        slot(b, hg, s)
                    for hg, s in slots[:GROUP]:
                        slot(b + 1, hg, s)
                for hg, s in slots[GROUP:]:
                    slot(NBLK - 1, hg, s)
                for s in range(3):
                    slot(NBLK, 0, s)
                finish()

            def live(u, lag):
                return not isinstance(u, int) or 0 <= u - lag < UNITS

            block = part.enter_context(nc.Block())

            @block.tensor
            def _(pe):
                def wide_tile(ps, wt, t, blk, hg, done):
                    n = 0
                    for k in range(KH):
                        for a, c in PARTS:
                            last = pe.matmul(ps[:, :], xT[:, a, ds(blk * BLK + (k * TOK + t * P), P)],
                                             wcol(wt, c, k, hg * GW, GW), start=(n == 0), stop=(n == 5))
                            n += 1
                    last.then_inc(done, 1)

                def values(w, t, blk, hg):
                    if not low(w - 1):
                        pe.wait_ge(s_qlo, w - 1)
                        pe.wait_ge(s_qsq, w - 1)
                    if not low(w):
                        pe.wait_ge(s_vf, w)
                    wide_tile(ps_qv, wv_s, t, blk, hg, s_v)

                def gates(w, t, blk, hg):
                    if not low(w - 1):
                        pe.wait_ge(s_klo, w - 1)
                        pe.wait_ge(s_ksq, w - 1)
                    if not low(w):
                        pe.wait_ge(s_gate, w)
                    wide_tile(ps_kg, wg_s, t, blk, hg, s_g)

                def slot(b, hg, s):
                    u, g = where(b, hg, s)
                    par = s % 2
                    if live(u, 0):
                        head = (hg * GROUP + s) * P
                        row = b * BLK
                        for ps, wt, done, freed in ((ps_qv, wq_s, s_q, s_vf), (ps_kg, wk_s, s_k, s_gate)):
                            if live(u, -1):
                                pe.wait_ge(freed, u + 2)
                            else:
                                pe.wait_ge(freed, UNITS)
                            n = 0
                            for k in range(KH):
                                for a, c in PARTS:
                                    last = pe.matmul(ps[:, :], wcol(wt, a, k, head, P),
                                                     xT[:, c, ds(row + k * TOK, BLK)], start=(n == 0), stop=(n == 5))
                                    n += 1
                            last.then_inc(done, 1)
                    if live(u, 1):
                        prev = (s - 1) % 2
                        pe.wait_ge(s_qhi, u)
                        pe.wait_ge(s_khi, u)
                        pe.wait_ge(s_qlo, u)
                        pe.wait_ge(s_klo, u)
                        if not low(u - 1):
                            pe.wait_ge(s_p, u - 1)
                        for t in range(TILES):
                            for n, (a, c) in enumerate(PARTS):
                                last = pe.matmul(ps_sc[:, t * P:(t + 1) * P], k_s[:, prev, a, t * P:(t + 1) * P],
                                                 q_s[:, prev, c, t * P:(t + 1) * P], start=(n == 0), stop=(n == 2))
                        last.then_inc(s_score, 1)
                        pe.wait_ge(s_qsl, u)
                        pe.wait_ge(s_ksl, u)
                        if not low(u - 1):
                            pe.wait_ge(s_newton, NORM_STEPS * (u - 1))
                        for i, (sq, sl) in enumerate(((q_sq, q_sl), (k_sq, k_sl))):
                            for t in range(TILES):
                                o = ps_nm[:, i * TILES + t:i * TILES + t + 1]
                                pe.matmul(o, sq[:, prev, t * P:(t + 1) * P].bitcast(BF16)[:, 1::2], ones16[:, 0:1],
                                          start=True, stop=False)
                                last = pe.matmul(o, sl[:, prev, t * P:(t + 1) * P], ones16[:, 0:1],
                                                 start=False, stop=True)
                        last.then_inc(s_norm, 1)
                    if live(u, -2):
                        values(u + 2, (s + 2) % TILES, *group_ahead(b, hg, s))
                    if live(u, 2):
                        _, head, grp, hh = back(b, hg, s, 2)
                        pe.wait_ge(s_phi, u - 1)
                        pe.wait_ge(s_plo, u - 1)
                        pe.wait_ge(s_vhi, GROUP * grp + GROUP)
                        pe.wait_ge(s_vlo, GROUP * grp + GROUP)
                        if not low(u - 2):
                            pe.wait_ge(s_og, u - 2)
                        at = (head // GROUP % 2) * (TILES * GW)
                        for t in range(TILES):
                            for n, (a, c) in enumerate(PARTS):
                                last = pe.matmul(ps_pv[:, t * P:(t + 1) * P], pr_s[:, par, a, t * P:(t + 1) * P],
                                                 v_s[:, c, ds(at + (t * GW + hh * P), P)], start=(n == 0), stop=(n == 2))
                        last.then_inc(s_pv, 1)
                    if live(u, -2):
                        gates(u + 2, (s + 2) % TILES, *group_ahead(b, hg, s))
                    if live(u, 3):
                        blk, head, _, _ = back(b, hg, s, 3)
                        pe.wait_ge(s_ohi, u - 2)
                        pe.wait_ge(s_olo, u - 2)
                        first = head == 0
                        final = head == HEADS - 1
                        if first and not low(blk):
                            pe.wait_ge(s_mid, blk)
                        prev = (s - 3) % 2
                        for t in range(TILES):
                            for n, (a, c) in enumerate(PARTS):
                                last = pe.matmul(ps_acc[:, t * HID:(t + 1) * HID], ogT[:, prev, a, t * P:(t + 1) * P],
                                                 wo_s[:, c, ds(head * HID, HID)],
                                                 start=(first and n == 0 and t % 2 == 0), stop=(final and n == 2),
                                                 skip_group_check=True)
                        last.then_inc(s_acc, 1)
                    if live(u, 2):
                        pe.wait_ge(s_og, u - 1)
                        if not low(u - 2):
                            pe.wait_ge(s_olo, u - 2)
                            pe.wait_ge(s_ohi, u - 2)
                        for t in range(TILES):
                            last = pe.transpose(ps_tr[:, t * P:(t + 1) * P], og[:, par, t * P:(t + 1) * P], ident[:, :])
                        last.then_inc(s_tr, 1)

                for t in range(2):
                    values(t, t, 0, 0)
                    gates(t, t, 0, 0)
                walk(pe, slot, lambda: None)

            @block.scalar
            def _(act):
                def values(w, t, blk, hg):
                    at = (hg % 2) * (TILES * GW) + t * GW
                    act.wait_ge(s_vf, w + 1)
                    if not low(w - 4):
                        act.wait_ge(s_pv, w - 4)
                    act.activation(v_s[:, 0, ds(at, GW)], v_f[:, t % 2, :], ACT.Copy).then_inc(s_vhi, 1)
                    act.wait_ge(s_g, w + 1)
                    if not low(w - 4):
                        act.wait_ge(s_og, w - 4)
                    act.activation(gate[:, ds(at, GW)], ps_kg[:, :], ACT.Silu, scale=unscale[:, G:G + 1]).then_inc(s_gate, 1)

                def projection(u, par, head, done, ps, bias, dst, sq, hi, sqd):
                    if not live(u, 0):
                        return
                    act.wait_ge(done, u + 1)
                    if not low(u - 1):
                        act.wait_ge(s_score, u - 1)
                    act.activation(dst[:, par, 0, :], ps[:, :], ACT.Identity, bias=bias[:, head:head + 1]).then_inc(hi, 1)
                    if not low(u - 1):
                        act.wait_ge(s_norm, u - 1)
                    act.activation(sq[:, par, :], ps[:, :], ACT.Square, bias=bias[:, head:head + 1]).then_inc(sqd, 1)

                def slot(b, hg, s):
                    u, g = where(b, hg, s)
                    par = s % 2
                    if live(u, 3):
                        act.wait_ge(s_tr, u - 2)
                        if not low(u - 3):
                            act.wait_ge(s_acc, u - 3)
                        act.activation(ogT[:, (s - 3) % 2, 0, :], ps_tr[:, :], ACT.Copy).then_inc(s_ohi, 1)
                    projection(u, par, hg * GROUP + s, s_q, ps_qv, bq_c, q_s, q_sq, s_qhi, s_qsq)
                    if live(u, 2):
                        act.wait_ge(s_p, u - 1)
                        if not low(u - 3):
                            act.wait_ge(s_pv, u - 3)
                        act.activation(pr_s[:, par, 0, :], pr_f[:, par, :], ACT.Copy).then_inc(s_phi, 1)
                    projection(u, par, hg * GROUP + s, s_k, ps_kg, bk_c, k_s, k_sq, s_khi, s_ksq)
                    if live(u, -2):
                        values(u + 2, (s + 2) % TILES, *group_ahead(b, hg, s))

                values(0, 0, 0, 0)
                values(1, 1, 0, 0)
                walk(act, slot, lambda: None)

            @block.vector
            def _(dve):
                def values(w, t, blk, hg):
                    col = hg * GW
                    dve.wait_ge(s_v, w + 1)
                    if not low(w - 1):
                        dve.wait_ge(s_vhi, w - 1)
                        dve.wait_ge(s_vlo, w - 1)
                    dve.tensor_tensor(v_f[:, t % 2, :], ps_qv[:, :], bv_b[:, ds(col, GW)], ALU.add).then_inc(s_vf, 1)

                def newton(step, u, prev, blk, head):
                    if step == 0:
                        dve.wait_ge(s_norm, u)
                        if not low(u - 1):
                            dve.wait_ge(s_newton, NORM_STEPS * (u - 1))
                        ins = dve.tensor_scalar(t_n[:, :], ps_nm[:, 0:8], 1.0 / P, eps_sq[:, :], ALU.mult, ALU.max)
                    else:
                        dve.wait_ge(s_newton, NORM_STEPS * (u - 1) + step)
                    if step == 1:
                        ins = dve.tensor_scalar(a_n[:, :].bitcast(I32), t_n[:, :].bitcast(I32), 1, None,
                                                ALU.logical_shift_right)
                    if step == 2:
                        ins = dve.tensor_scalar(y_n[:, :].bitcast(I32), a_n[:, :].bitcast(I32), -1, RSQRT_GUESS,
                                                ALU.mult, ALU.add)
                    if step in (3, 6, 9):
                        ins = dve.scalar_tensor_tensor(out=a_n[:, :], in0=y_n[:, :], scalar=-0.5, in1=y_n[:, :],
                                                       op0=ALU.mult, op1=ALU.mult)
                    if step in (4, 7, 10):
                        ins = dve.tensor_tensor(a_n[:, :], a_n[:, :], t_n[:, :], ALU.mult)
                    if step in (5, 8, 11):
                        ins = dve.scalar_tensor_tensor(out=y_n[:, :], in0=a_n[:, :], scalar=1.5, in1=y_n[:, :],
                                                       op0=ALU.add, op1=ALU.mult)
                    if step == 12:
                        ins = dve.tensor_tensor(c_k[:, prev, :].unsqueeze(2), y_n[:, TILES:2 * TILES].unsqueeze(2),
                                                beta[:, ds(blk * TILES, TILES), ds(head, 1)], ALU.mult)
                    if step == 13:
                        ins = dve.tensor_scalar(c_q[:, prev, :], y_n[:, 0:TILES], gate_k[:, :], None, ALU.mult)
                    ins.then_inc(s_newton, 1)

                def output_tile(t, u, par, head):
                    at = (head // GROUP % 2) * (TILES * GW)
                    ins = dve.scalar_tensor_tensor(out=og[:, par, t * P:(t + 1) * P], in0=ps_pv[:, t * P:(t + 1) * P],
                                                   scalar=c_q[:, par, t:t + 1], in1=gate[:, ds(at + t * GW + head % GROUP * P, P)],
                                                   op0=ALU.mult, op1=ALU.mult)
                    if t == TILES - 1:
                        ins.then_inc(s_og, 1)

                def slot(b, hg, s):
                    u, g = where(b, hg, s)
                    par, prev = s % 2, (s - 1) % 2
                    if live(u, 3):
                        dve.wait_ge(s_ohi, u - 2)
                        if not low(u - 3):
                            dve.wait_ge(s_acc, u - 3)
                        o = ogT[:, (s - 3) % 2, :, :]
                        dve.tensor_tensor(o[:, 1, :], ps_tr[:, :], o[:, 0, :], ALU.subtract).then_inc(s_olo, 1)
                    if s == 3 and hg == 0 and not low(u - 3):
                        rows_out(b)
                    if live(u, 0):
                        head = hg * GROUP + s
                        for ps, bias, dst, hi, sqd, done in (
                            (ps_qv, bq_c, q_s, s_qhi, s_qsq, s_qlo), (ps_kg, bk_c, k_s, s_khi, s_ksq, s_klo),
                        ):
                            dve.wait_ge(hi, u + 1)
                            dve.wait_ge(sqd, u + 1)
                            dve.scalar_tensor_tensor(out=dst[:, par, 1, :], in0=ps[:, :], scalar=bias[:, ds(head, 1)],
                                                     in1=dst[:, par, 0, :], op0=ALU.add, op1=ALU.subtract).then_inc(done, 1)
                    if live(u, 1):
                        blk, head, _, _ = back(b, hg, s, 1)
                        for step in range(4):
                            newton(step, u, prev, blk, head)
                    if live(u, -2):
                        values(u + 2, (s + 2) % TILES, *group_ahead(b, hg, s))
                    if live(u, 1):
                        for step in range(4, 5):
                            newton(step, u, prev, blk, head)
                    if live(u, 2):
                        _, out_head, grp, _ = back(b, hg, s, 2)
                        dve.wait_ge(s_pv, u - 1)
                        dve.wait_ge(s_gate, GROUP * grp + GROUP)
                        dve.wait_ge(s_newton, NORM_STEPS * (u - 1))
                        if not low(u - 3):
                            dve.wait_ge(s_tr, u - 3)
                    for t in range(TILES):
                        if live(u, 2):
                            output_tile(t, u, par, out_head)
                        if live(u, 1):
                            for step in range(5 + 1 * t, 5 + 1 * (t + 1)):
                                newton(step, u, prev, blk, head)
                    if live(u, 1):
                        for step in range(5 + 1 * TILES, NORM_STEPS):
                            newton(step, u, prev, blk, head)
                        dve.wait_ge(s_score, u)
                        dve.wait_ge(s_newton, NORM_STEPS * (u - 1) + 13)
                        if not low(u - 2):
                            dve.wait_ge(s_phi, u - 2)
                            dve.wait_ge(s_plo, u - 2)
                        for t in range(TILES):
                            last = dve.scalar_tensor_tensor(out=pr_f[:, prev, t * P:(t + 1) * P],
                                                            in0=ps_sc[:, t * P:(t + 1) * P], scalar=c_k[:, prev, t:t + 1],
                                                            in1=mask[:, :], op0=ALU.mult, op1=ALU.mult)
                        last.then_inc(s_p, 1)

                def rows_out(b):
                    dve.wait_ge(s_acc, HEADS * b)
                    dve.wait_ge(s_bias, b)
                    for i in range(2):
                        half = slice(i * 512, (i + 1) * 512)
                        ins = dve.scalar_tensor_tensor(out=rows[:, half], in0=ps_acc[:, half], scalar=out_unscale[:, :],
                                                       in1=rows[:, half], op0=ALU.mult, op1=ALU.add)
                    ins.then_inc(s_mid, 1)

                values(0, 0, 0, 0)
                values(1, 1, 0, 0)
                walk(dve, slot, lambda: rows_out(NBLK))

            @block.gpsimd
            def _(pool):
                def values(w, t, blk, hg):
                    at = (hg % 2) * (TILES * GW) + t * GW
                    pool.wait_ge(s_vhi, w + 1)
                    if not low(w - 4):
                        pool.wait_ge(s_pv, w - 4)
                    pool.tensor_tensor(v_s[:, 1, ds(at, GW)], v_f[:, t % 2, :], v_s[:, 0, ds(at, GW)],
                                       ALU.subtract).then_inc(s_vlo, 1)

                def slot(b, hg, s):
                    u, g = where(b, hg, s)
                    par = s % 2
                    if live(u, 0):
                        for sq, sl, ready, done in ((q_sq, q_sl, s_qsq, s_qsl), (k_sq, k_sl, s_ksq, s_ksl)):
                            pool.wait_ge(ready, u + 1)
                            if not low(u - 1):
                                pool.wait_ge(s_norm, u - 1)
                            pool.tensor_tensor(sl[:, par, :], sq[:, par, :], sq[:, par, :].bitcast(BF16)[:, 1::2],
                                               ALU.subtract).then_inc(done, 1)
                    if live(u, -2):
                        values(u + 2, (s + 2) % TILES, *group_ahead(b, hg, s))
                    if live(u, 1):
                        prev = (s - 1) % 2
                        pool.wait_ge(s_phi, u)
                        if not low(u - 2):
                            pool.wait_ge(s_pv, u - 2)
                        pool.tensor_tensor(pr_s[:, prev, 1, :], pr_f[:, prev, :], pr_s[:, prev, 0, :],
                                           ALU.subtract).then_inc(s_plo, 1)
                    if s == 0 and hg == 0 and not isinstance(b, int):
                        rows_in(b)

                def rows_in(b):
                    pool.wait_ge(s_rows, 16 * b)
                    pool.tensor_tensor(rows[:, :].rearrange("p (t h) -> p t h", h=HID),
                                       rows[:, :].rearrange("p (t h) -> p t h", h=HID),
                                       bo_b[:, :].unsqueeze(1).broadcast_to((P, TILES, HID)), ALU.add).then_inc(s_bias, 1)

                values(0, 0, 0, 0)
                values(1, 1, 0, 0)
                walk(pool, slot, lambda: rows_in(NBLK))

            @block.sync
            def _(sp):
                rows3 = rows[:, :].rearrange("p (t h) -> p t h", h=HID)

                def load(b):
                    sp.dma_start(rows3, x_v[ds(b, 1), :, :, :].rearrange("b p t h -> (b p) t h")).then_inc(s_rows, 16)

                def keep(b):
                    sp.wait_ge(s_mid, b + 1)
                    sp.dma_start(mid[ds(b, 1), :, :].rearrange("b p n -> (b p) n"), rows[:, :]).then_inc(s_kept, 16)
                    sp.wait_ge(s_kept, 16 * b + 16)

                load(0)
                with sp.Fori(0, NBLK - 1) as b:
                    keep(b)
                    load(b + 1)
                keep(NBLK - 1)

        with ExitStack() as part:
            mrows = sb("mrows", [P, 2, TILES * HID], F32, part)
            mn = sb("mn", [P, 2, TILES * HID], F32, part)
            yT = sb("yT", [P, 2, 2, KH * BLK], F16, part)
            r_f = sb("r_f", [P, KF, BLK], F32, part)
            h_f = sb("h_f", [P, 2, BLK], F32, part)
            h_s = sb("h_s", [P, 2, 2, KF * BLK], F16, part)
            res = sb("res", [P, 2, TILES * HID], F32, part)
            pause = sb("pause", [P, 1], F32, part)
            st2 = sb("st2", [P, TILES, 6], F32, part)
            mv2 = sb("mv2", [P, TILES, 2], F32, part)
            t2 = sb("t2", [P, TILES], F32, part)
            a2 = sb("a2", [P, TILES], F32, part)
            y2 = sb("y2", [P, TILES], F32, part)

            ps_y = pb("ps_y", [P, KH * BLK], part)
            ps_h = pb("ps_h", [P, 4, BLK], part)
            ps_o = pb("ps_o", [P, TILES * HID], part)

            f_rows = [sem(f"f_rows{i}", part) for i in range(2)]
            f_back = [sem(f"f_back{i}", part) for i in range(2)]
            f_out = [sem(f"f_out{i}", part) for i in range(2)]
            f_norm = sem("f_norm", part)
            f_chain = sem("f_chain", part)
            f_t = sem("f_t", part)
            f_thi = sem("f_thi", part)
            f_tlo = sem("f_tlo", part)
            f_h = sem("f_h", part)
            f_relu = sem("f_relu", part)
            f_sq = sem("f_sq", part)
            f_hi = sem("f_hi", part)
            f_lo = sem("f_lo", part)
            f_o = sem("f_o", part)
            f_res = sem("f_res", part)

            def hidden_bank(f, par):
                return (f + par) % 4

            def gap(f, par):
                return 2 if par == 0 and f < 2 else 4

            def steps(step):
                def stages(j):
                    return dict(add=j > 1, out=j > 0, turn=j + 1 < NBLK, norm=j + 2 < NBLK)

                def run(eng):
                    for j in range(2):
                        step(j, j % 2, **stages(j))
                    with eng.Fori(1, NBLK // 2 - 1) as pair:
                        for i in range(2):
                            step(2 * pair + i, i, **stages(2))
                    for j in range(NBLK - 2, NBLK):
                        step(j, j % 2, **stages(j))
                return run

            block = part.enter_context(nc.Block())

            @block.sync
            def _(sp):
                def rows_of(b):
                    return mid[ds(b, 1), :, :].rearrange("b p n -> (b p) n")

                def load_norm(b, par):
                    if not low(b - 1):
                        sp.wait_ge(f_norm, b - 1)
                    sp.dma_start(mrows[:, par, :], rows_of(b)).then_inc(f_rows[par], 16)

                def load_back(b, par):
                    sp.dma_start(res[:, par, :], rows_of(b)).then_inc(f_back[par], 16)

                def store(b, par):
                    sp.wait_ge(f_res, b + 1)
                    sp.dma_start(out_v[ds(b, 1), :, :, :].rearrange("b p t h -> (b p) t h"),
                                 res[:, par, :].rearrange("p (t h) -> p t h", h=HID)).then_inc(f_out[par], 16)
                    sp.wait_ge(f_out[par], 16 * ((b - par) // 2 + 1))

                load_norm(0, 0)
                load_norm(1, 1)
                load_back(0, 0)
                load_back(1, 1)
                load_norm(2, 0)
                load_norm(3, 1)
                with sp.Fori(0, NBLK // 2 - 2) as pair:
                    for i in range(2):
                        load_norm(2 * pair + (i + 4), i)
                        store(2 * pair + i, i)
                        load_back(2 * pair + (i + 2), i)
                for b in range(NBLK - 4, NBLK):
                    store(b, b % 2)
                    if b + 2 < NBLK:
                        load_back(b + 2, b % 2)

            @block.tensor
            def _(pe):
                def turn_rows(b, par):
                    pe.wait_ge(f_norm, b + 1)
                    if not low(b):
                        pe.wait_ge(f_thi, b)
                        pe.wait_ge(f_tlo, b)
                    for k in range(KH):
                        for t in range(TILES):
                            last = pe.transpose(ps_y[:, k * BLK + t * P:k * BLK + (t + 1) * P],
                                                mn[:, par, t * HID + k * P:t * HID + (k + 1) * P], ident[:, :])
                    last.then_inc(f_t, 1)

                def hidden(b, par, f):
                    n = KF * b + f
                    if f == 0:
                        pe.wait_ge(f_thi, b + 1)
                        pe.wait_ge(f_tlo, b + 1)
                    if not low(n - gap(f, par) + 1):
                        pe.wait_ge(f_relu, n - gap(f, par) + 1)
                    i = 0
                    for k in range(KH):
                        for a in range(2):
                            last = pe.matmul(ps_h[:, hidden_bank(f, par), :], wfc_t[:, k * FFN + f * P:k * FFN + (f + 1) * P],
                                             yT[:, par, a, k * BLK:(k + 1) * BLK], start=(i == 0), stop=(i == 3))
                            i += 1
                    last.then_inc(f_h, 1)

                def output(b, par):
                    if not low(b):
                        pe.wait_ge(f_res, b)
                    pe.wait_ge(f_hi, KF * b + KF)
                    pe.wait_ge(f_lo, KF * b + KF)
                    for t in range(TILES):
                        i = 0
                        for f in range(KF):
                            for a in range(2):
                                last = pe.matmul(ps_o[:, t * HID:(t + 1) * HID],
                                                 h_s[:, par, a, f * BLK + t * P:f * BLK + (t + 1) * P],
                                                 wpr_t[:, f * HID:(f + 1) * HID], start=(i == 0), stop=(i == 2 * KF - 1))
                                i += 1
                    last.then_inc(f_o, 1)

                def step(j, par, add, out, turn, norm):
                    for f in range(KF):
                        hidden(j, par, f)
                        if turn and f == 2:
                            turn_rows(j + 1, 1 - par)
                    if out:
                        output(j - 1, 1 - par)

                turn_rows(0, 0)
                steps(step)(pe)
                output(NBLK - 1, 1)

            @block.scalar
            def _(act):
                def upper(b, par):
                    act.wait_ge(f_t, b + 1)
                    if not low(b - 1):
                        act.wait_ge(f_h, KF * b - KF)
                    act.activation(yT[:, par, 0, :], ps_y[:, :], ACT.Copy).then_inc(f_thi, 1)

                def relu(b, par, f):
                    n = KF * b + f
                    act.wait_ge(f_h, n + 1)
                    if not low(b):
                        act.wait_ge(f_sq, n - KF + 1)
                    act.activation(r_f[:, f, :], ps_h[:, hidden_bank(f, par), :], ACT.Relu).then_inc(f_relu, 1)

                def square_hi(b, par, f):
                    act.wait_ge(f_relu, KF * b + (f + 1))
                    if f == 0 and not low(b - 1):
                        act.wait_ge(f_o, b - 1)
                    act.activation(h_s[:, par, 0, f * BLK:(f + 1) * BLK], r_f[:, f, :], ACT.Square).then_inc(f_hi, 1)

                def step(j, par, add, out, turn, norm):
                    relu(j, par, 0)
                    for f in range(1, KF):
                        relu(j, par, f)
                        square_hi(j, par, f - 1)
                        if turn and f == 2:
                            upper(j + 1, 1 - par)
                    square_hi(j, par, KF - 1)

                upper(0, 0)
                steps(step)(act)

            @block.vector
            def _(dve):
                LINKS = 13

                def stats(b, par):
                    dve.wait_ge(f_rows[par], 16 * ((b - par) // 2 + 1))
                    for t in range(TILES):
                        ins = dve.bn_stats(st2[:, t, :], mrows[:, par, t * HID:(t + 1) * HID])
                    ins.then_inc(f_chain, 1)

                def link(i, b):
                    dve.wait_ge(f_chain, (LINKS + 1) * b + (i + 1))
                    if i == 0:
                        dve.memset(pause[:, :], 0.0)
                        for t in range(TILES):
                            ins = dve.bn_aggr(mv2[:, t, :], st2[:, t, :])
                    elif i == 1:
                        ins = dve.tensor_scalar(t2[:, :], mv2[:, :, 1], LN_EPS, None, ALU.add)
                    elif i == 2:
                        ins = dve.tensor_scalar(a2[:, :].bitcast(I32), t2[:, :].bitcast(I32), 1, None, ALU.logical_shift_right)
                    elif i == 3:
                        ins = dve.tensor_scalar(y2[:, :].bitcast(I32), a2[:, :].bitcast(I32), -1, RSQRT_GUESS, ALU.mult, ALU.add)
                    elif i % 3 == 1:
                        ins = dve.scalar_tensor_tensor(out=a2[:, :], in0=y2[:, :], scalar=-0.5, in1=y2[:, :],
                                                       op0=ALU.mult, op1=ALU.mult)
                    elif i % 3 == 2:
                        ins = dve.tensor_tensor(a2[:, :], a2[:, :], t2[:, :], ALU.mult)
                    else:
                        ins = dve.scalar_tensor_tensor(out=y2[:, :], in0=a2[:, :], scalar=1.5, in1=y2[:, :],
                                                       op0=ALU.add, op1=ALU.mult)
                    ins.then_inc(f_chain, 1)

                def links(first, last, b):
                    for i in range(first, last):
                        link(i, b)

                def apply(b, par):
                    dve.wait_ge(f_chain, (LINKS + 1) * b + (LINKS + 1))
                    if not low(b - 1):
                        dve.wait_ge(f_t, b - 1)
                    for t in range(TILES):
                        ins = dve.tensor_scalar(mn[:, par, t * HID:(t + 1) * HID], mrows[:, par, t * HID:(t + 1) * HID],
                                                mv2[:, t, 0:1], y2[:, t:t + 1], ALU.subtract, ALU.mult)
                    ins.then_inc(f_norm, 1)

                def lower(b, par, k):
                    dve.wait_ge(f_thi, b + 1)
                    at = slice(k * BLK, (k + 1) * BLK)
                    ins = dve.tensor_tensor(yT[:, par, 1, at], ps_y[:, at], yT[:, par, 0, at], ALU.subtract)
                    if k == KH - 1:
                        ins.then_inc(f_tlo, 1)

                def square(b, par, f):
                    n = KF * b + f
                    dve.wait_ge(f_relu, n + 1)
                    if not low(n - 1):
                        dve.wait_ge(f_lo, n - 1)
                    dve.tensor_tensor(h_f[:, (f + par) % 2, :], r_f[:, f, :], r_f[:, f, :], ALU.mult).then_inc(f_sq, 1)

                def result(b, par, i):
                    if i == 0:
                        dve.wait_ge(f_o, b + 1)
                        dve.wait_ge(f_back[par], 16 * ((b - par) // 2 + 1))
                    half = slice(i * 512, (i + 1) * 512)
                    ins = dve.scalar_tensor_tensor(out=res[:, par, half], in0=ps_o[:, half], scalar=ffn_unscale[:, :],
                                                   in1=res[:, par, half], op0=ALU.mult, op1=ALU.add)
                    if i == 1:
                        ins.then_inc(f_res, 1)

                def step(j, par, add, out, turn, norm):
                    if norm:
                        stats(j + 2, par)
                    for i in range(2):
                        if norm:
                            link(i, j + 2)
                        if add:
                            result(j - 2, par, i)
                    for f in range(KF):
                        if norm:
                            link(2 + f, j + 2)
                        square(j, par, f)
                        if turn and f < KH:
                            lower(j + 1, 1 - par, f)
                    if norm:
                        links(2 + KF, LINKS, j + 2)
                        apply(j + 2, par)

                for b in range(2):
                    stats(b, b)
                    links(0, LINKS, b)
                    apply(b, b)
                    if b == 0:
                        lower(0, 0, 0)
                        lower(0, 0, 1)
                steps(step)(dve)
                for b in (NBLK - 2, NBLK - 1):
                    for i in range(2):
                        result(b, b % 2, i)

            @block.gpsimd
            def _(pool):
                def step(j, par, add, out, turn, norm):
                    if not low(j - 1):
                        pool.wait_ge(f_o, j - 1)
                    for f in range(KF):
                        at = slice(f * BLK, (f + 1) * BLK)
                        pool.wait_ge(f_sq, KF * j + (f + 1))
                        pool.wait_ge(f_hi, KF * j + (f + 1))
                        pool.tensor_tensor(h_s[:, par, 1, at], h_f[:, (f + par) % 2, :], h_s[:, par, 0, at],
                                           ALU.subtract).then_inc(f_lo, 1)

                steps(step)(pool)


def kernel(L0_attn_hidden_states, L0_attn_q_w, L0_attn_q_b, L0_attn_k_w, L0_attn_k_b, L0_attn_v_w, L0_attn_v_b,
           L0_attn_a_w, L0_attn_a_b, L0_attn_b_w, L0_attn_b_b, L0_attn_og_w, L0_attn_o_w, L0_attn_o_b,
           L0_ffn_w_fc, L0_ffn_w_proj):
    import numpy as np
    import concourse.bacc as bacc
    from concourse.bass_utils import run_bass_kernel_spmd

    def tiled(w):
        w = np.asarray(w)
        n, c = w.shape
        return np.ascontiguousarray(w.T.reshape(c // P, P, n).transpose(1, 0, 2).reshape(P, c // P * n))

    def columns(b):
        return np.ascontiguousarray(np.asarray(b).reshape(HEADS, P).T)

    shape = L0_attn_hidden_states.shape
    arrays = {
        "x": np.ascontiguousarray(np.asarray(L0_attn_hidden_states).reshape(TOK, HID)),
        "wq": tiled(L0_attn_q_w), "wk": tiled(L0_attn_k_w), "wv": tiled(L0_attn_v_w), "wg": tiled(L0_attn_og_w),
        "wo": tiled(L0_attn_o_w), "wb": tiled(L0_attn_b_w),
        "bq": columns(L0_attn_q_b), "bk": columns(L0_attn_k_b), "bv": columns(L0_attn_v_b),
        "bv_row": np.asarray(L0_attn_v_b), "bb": np.asarray(L0_attn_b_b), "bo": np.asarray(L0_attn_o_b),
        "wfc": tiled(L0_ffn_w_fc), "wpr": tiled(L0_ffn_w_proj),
    }
    nc = bacc.Bacc("TRN2", target_bir_lowering=False, num_devices=1)
    aps = {n: nc.dram_tensor(f"in_{n}", a.shape, mybir.dt.from_np(a.dtype), kind="ExternalInput").ap()
           for n, a in arrays.items()}
    aps["out"] = nc.dram_tensor("out_rows", (TOK, HID), F32, kind="ExternalOutput").ap()
    build(nc, **aps)
    r = run_bass_kernel_spmd(nc, [{f"in_{n}": a for n, a in arrays.items()}], core_ids=[0])
    return r.results[0]["out_rows"].reshape(shape)
```

```python
from contextlib import ExitStack

import concourse.bass as bass
from concourse import mybir

ALU = mybir.AluOpType
ACT = mybir.ActivationFunctionType
AX_X = mybir.AxisListType.X
F32 = mybir.dt.float32
F16 = mybir.dt.float16
BF16 = mybir.dt.bfloat16
I32 = mybir.dt.int32

P = 128
TOK = 8 * 512
HID = 256
KH = HID // P
HEADS = 16
WIDE = HEADS * P
CHUNK = 64
BLK = 512
TILES = BLK // P
NBLK = TOK // BLK
NTILE = TOK // P
GROUP = 4
GW = GROUP * P
FFN = 640
KF = FFN // P
LN_CHUNK = 8
PAIR = 2 * P
RING = 3
TBANKS = 3
RAW_MATRICES = 5
UNITS = NBLK * HEADS
NORM_STEPS = 14
RSQRT_GUESS = 0x5F3759DF
LN_EPS = 1e-5
L2_EPS = 1e-12

ds = bass.ds


def low(n):
    return isinstance(n, int) and n <= 0


def build(nc, x, wq, wk, wv, wg, wo, wb, bq, bk, bv, bv_row, bb, bo, wfc, wpr, out):
    x_v = x.rearrange("(b t p) h -> b p t h", t=TILES, p=P)
    x_c = x.rearrange("(c t p) h -> c p t h", t=LN_CHUNK, p=P)
    out_v = out.rearrange("(b t p) h -> b p t h", t=TILES, p=P)
    mid = nc.dram_tensor("mid_rows", [NBLK, P, TILES * HID], F32, kind="Internal").ap()
    mid_norm = nc.dram_tensor("mid_norm", [NBLK, P, TILES * HID], F32, kind="Internal").ap()

    with ExitStack() as whole:
        def sb(name, shape, dt, ctx=whole):
            return ctx.enter_context(nc.sbuf_tensor(name, shape, dt))

        def pb(name, shape, ctx, dt=F32):
            return ctx.enter_context(nc.psum_tensor(name, shape, dt))

        def sem(name, ctx=whole):
            return ctx.enter_context(nc.semaphore(name))

        wq_s = sb("wq_s", [P, 2, KH * WIDE], F16)
        wk_s = sb("wk_s", [P, 2, KH * WIDE], F16)
        wv_s = sb("wv_s", [P, 2, KH * WIDE], F16)
        wg_s = sb("wg_s", [P, 2, KH * WIDE], F16)
        wo_s = sb("wo_s", [P, 2, HEADS * HID], F16)
        wfc_t = sb("wfc_t", [P, KH * FFN], F16)
        wpr_t = sb("wpr_t", [P, KF * HID], F16)
        xT = sb("xT", [P, 2, KH * TOK], F16)
        beta = sb("beta", [P, NTILE, HEADS], F32)
        bq_c = sb("bq_c", [P, HEADS], F32)
        bk_c = sb("bk_c", [P, HEADS], F32)
        bv_b = sb("bv_b", [P, WIDE], F32)
        bo_b = sb("bo_b", [P, HID], F32)
        ident = sb("ident", [P, P], F32)
        mask = sb("mask", [P, P], F32)
        ones16 = sb("ones16", [P, 2], F16)
        scale = sb("scale", [P, 5], F32)
        unscale = sb("unscale", [P, 5], F32)
        eps_sq = sb("eps_sq", [P, 1], F32)
        gate_k = sb("gate_k", [P, 1], F32)
        out_unscale = sb("out_unscale", [P, 1], F32)
        ffn_unscale = sb("ffn_unscale", [P, 1], F32)

        QK, V, G, O, B = range(5)

        def wcol(w, part, k, start, n):
            return w[:, part, ds(k * WIDE + start, n)]

        with ExitStack() as part:
            raw = sb("raw", [P, RING, KH * WIDE], F32, part)
            xc = sb("xc", [P, 2, LN_CHUNK * HID], F32, part)
            xn = sb("xn", [P, 2 * TBANKS, HID], F32, part)
            b_sq = sb("b_sq", [P, 5 * HEADS], BF16, part)
            ones_bf = sb("ones_bf", [P, P], BF16, part)
            ones_f = sb("ones_f", [P, P], F32, part)
            wb_raw = sb("wb_raw", [P, KH * HEADS], F32, part)
            wb_s = sb("wb_s", [P, 2, KH * HEADS], F16, part)
            bb_b = sb("bb_b", [P, HEADS], F32, part)
            bv_c = sb("bv_c", [P, HEADS], F32, part)
            wfc_r = sb("wfc_r", [P, KH * FFN], F32, part)
            wpr_r = bv_b[:, 0:KF * HID]
            stats = sb("stats", [P, LN_CHUNK, 6], F32, part)
            mv = sb("mv", [P, LN_CHUNK, 2], F32, part)
            t_ln = sb("t_ln", [P, LN_CHUNK], F32, part)
            a_ln = sb("a_ln", [P, LN_CHUNK], F32, part)
            y_ln = sb("y_ln", [P, LN_CHUNK], F32, part)
            peak = sb("peak", [P, 8], F32, part)
            tiny = sb("tiny", [P, 8], F32, part)
            z = wfc_r[:, 0:NTILE * HEADS]
            ez = wfc_r[:, NTILE * HEADS:2 * NTILE * HEADS]
            uz = xc[:, 0, 0:NTILE * HEADS]
            lz = xc[:, 1, 0:NTILE * HEADS]
            fsum = sb("fsum", [P, 2], F32, part)
            fmean = sb("fmean", [P, 2], F32, part)
            thr = sb("thr", [P, 2], F32, part)
            nthr = sb("nthr", [P, 2], F32, part)

            ps_t = [pb(f"ps_t{i}", [P, 512], part) for i in range(TBANKS)]
            ps_n = pb("ps_n", [P, WIDE], part)
            ps_s = pb("ps_s", [P, 512], part)

            s_small = sem("s_small", part)
            s_wide = sem("s_wide", part)
            s_bv = sem("s_bv", part)
            s_x = [sem(f"s_x{i}", part) for i in range(2)]
            s_raw = [sem(f"s_raw{i}", part) for i in range(RAW_MATRICES)]
            s_const = sem("s_const", part)
            s_wlo = [sem(f"s_wlo{i}", part) for i in range(RAW_MATRICES)]
            s_chain = sem("s_chain", part)
            s_xn = sem("s_xn", part)
            s_xlo = sem("s_xlo", part)
            s_peak = sem("s_peak", part)
            s_scale = sem("s_scale", part)
            s_bread = sem("s_bread", part)
            s_tern = sem("s_tern", part)
            s_xt = sem("s_xt", part)
            s_bnorm = sem("s_bnorm", part)
            s_wnorm = sem("s_wnorm", part)
            s_z = sem("s_z", part)
            s_fsum = sem("s_fsum", part)
            s_xhi = sem("s_xhi", part)
            s_bsq = sem("s_bsq", part)
            s_wsq = sem("s_wsq", part)
            s_wpre = sem("s_wpre", part)
            s_whi = sem("s_whi", part)
            s_abs = sem("s_abs", part)
            s_bvs = sem("s_bvs", part)
            s_beta = sem("s_beta", part)
            s_bact = sem("s_bact", part)
            s_bt = sem("s_bt", part)

            RAWS = [(wq, wq_s, QK), (wk, wk_s, QK), (wv, wv_s, V), (wg, wg_s, G), (wo, wo_s, O)]
            NORMS = ((0, 1), (2,), (3,), (4,))
            POOL_LOWER = (1, 2, 3)
            SMALL = 4 * 16
            NWIDE = 4 * 16
            FSUM_AT = slice(128, 130)
            PAIRS = NTILE // 2

            def squares(j):
                return RAWS[j][1][:, 0, :].bitcast(BF16)

            block = part.enter_context(nc.Block())

            @block.sync
            def _(sp):
                def load_x(c):
                    if c >= 2:
                        sp.wait_ge(s_xn, (c - 1) * LN_CHUNK)
                    sp.dma_start(xc[:, c % 2, :].rearrange("p (t h) -> p t h", h=HID), x_c[c]).then_inc(s_x[c % 2], 16)

                def load_raw(j):
                    if j >= RING:
                        sp.wait_ge(s_whi, j - RING + 1)
                        sp.wait_ge(s_wlo[j - RING], 1)
                    sp.dma_start(raw[:, j % RING, :], RAWS[j][0]).then_inc(s_raw[j], 16)

                load_x(0)
                for dst, src in ((wb_raw[:, :], wb), (bq_c[:, :], bq), (bk_c[:, :], bk), (bv_c[:, :], bv)):
                    sp.dma_start(dst, src).then_inc(s_small, 16)
                load_raw(0)
                load_x(1)
                load_raw(1)
                for dst, src, n in ((bb_b, bb, HEADS), (bo_b, bo, HID)):
                    sp.dma_start(dst[:, :], bass.AP(src.tensor, 0, [[0, P], [1, n]])).then_inc(s_wide, 16)
                sp.dma_start(wfc_r[:, :], wfc).then_inc(s_wide, 16)
                sp.dma_start(wpr_r, wpr).then_inc(s_wide, 16)
                load_raw(2)
                load_x(2)
                load_x(3)
                load_raw(3)
                sp.wait_ge(s_tern, 1)
                sp.dma_start(bv_b[:, :], bass.AP(bv_row.tensor, 0, [[0, P], [1, WIDE]])).then_inc(s_bv, 16)
                load_raw(RAW_MATRICES - 1)

            @block.gpsimd
            def _(pool):
                pool.memset(ident[:, :], 0.0).then_inc(s_const, 1)
                pool.memset(mask[:, :], 1.0).then_inc(s_const, 1)
                pool.wait_ge(s_const, 2)
                pool.affine_select(out=ident[:, :], in_=ident[:, :], compare_op=ALU.not_equal, fill=1.0, base=0,
                                   pattern=[[-1, P]], channel_multiplier=1).then_inc(s_const, 1)
                pool.affine_select(out=mask[:, :], in_=mask[:, :], compare_op=ALU.is_ge, fill=0.0, base=0,
                                   pattern=[[1, P]], channel_multiplier=-1).then_inc(s_const, 1)
                pool.wait_ge(s_const, 4)
                pool.memset(mask[0:CHUNK, CHUNK:P], 0.0).then_inc(s_const, 1)
                pool.memset(ones16[:, :], 1.0).then_inc(s_const, 1)
                pool.memset(ones_bf[:, :], 1.0).then_inc(s_const, 1)
                pool.memset(ones_f[:, :], 1.0).then_inc(s_const, 1)

                for j in POOL_LOWER:
                    pool.wait_ge(s_whi, j + 1)
                    _, dst, _ = RAWS[j]
                    pool.tensor_tensor(dst[:, 1, :], raw[:, j % RING, :], dst[:, 0, :], ALU.subtract).then_inc(s_wlo[j], 1)

            @block.scalar
            def _(act):
                def square_small():
                    act.wait_ge(s_small, SMALL)
                    for i, b in enumerate((bq_c, bk_c, bv_c)):
                        act.activation(b_sq[:, i * HEADS:(i + 1) * HEADS], b[:, :], ACT.Square,
                                       scale=1.0 / 16).then_inc(s_bsq, 1)
                    act.activation(b_sq[:, 3 * HEADS:5 * HEADS], wb_raw[:, :], ACT.Square).then_inc(s_bsq, 1)

                def square(j):
                    act.wait_ge(s_raw[j], 16)
                    act.activation(squares(j), raw[:, j % RING, :], ACT.Square).then_inc(s_wsq, 1)

                def prescale(j):
                    which = RAWS[j][2]
                    act.wait_ge(s_scale, which + 1)
                    place = raw[:, j % RING, :]
                    act.activation(place, place, ACT.Copy, scale=scale[:, which:which + 1]).then_inc(s_wpre, 1)

                def split_hi(j):
                    _, dst, which = RAWS[j]
                    place = raw[:, j % RING, :]
                    if j in POOL_LOWER:
                        act.wait_ge(s_wpre, POOL_LOWER.index(j) + 1)
                        act.activation(dst[:, 0, :], place, ACT.Copy).then_inc(s_whi, 1)
                    else:
                        act.wait_ge(s_scale, which + 1)
                        act.activation(dst[:, 0, :], place, ACT.Copy, scale=scale[:, which:which + 1]).then_inc(s_whi, 1)

                def x_hi(first, last):
                    for m in range(first, last):
                        act.wait_ge(s_xt, m + 1)
                        act.activation(xT[:, 0, :].rearrange("p (k n) -> p k n", k=KH)[:, :, m * PAIR:(m + 1) * PAIR],
                                       ps_t[m % TBANKS][:, :].rearrange("p (k n) -> p k n", k=KH), ACT.Copy).then_inc(s_xhi, 1)

                square_small()
                square(0)
                x_hi(0, 4)
                square(1)
                x_hi(4, 8)
                act.wait_ge(s_wide, NWIDE)
                for i, (w, w_t) in enumerate(((wfc_r[:, :], wfc_t), (wpr_r, wpr_t))):
                    act.activation(w_t[:, :], w, ACT.Abs, accum_out=fsum[:, i:i + 1]).then_inc(s_abs, 1)
                square(2)
                split_hi(0)
                for j in (1, 2):
                    prescale(j)
                    split_hi(j)
                square(3)
                x_hi(8, 12)
                square(4)
                x_hi(12, 16)
                prescale(3)
                split_hi(3)
                act.wait_ge(s_beta, 1)
                act.activation(lz, z, ACT.Abs).then_inc(s_bact, 1)
                act.wait_ge(s_bact, 1)
                act.activation(ez, lz, ACT.Exp, scale=-1.0).then_inc(s_bact, 1)
                split_hi(4)
                act.wait_ge(s_beta, 2)
                act.activation(lz, uz, ACT.Ln).then_inc(s_bact, 1)
                act.wait_ge(s_bv, 16)
                act.activation(bv_b[:, :], bv_b[:, :], ACT.Copy, scale=scale[:, V:V + 1]).then_inc(s_bvs, 1)

            @block.vector
            def _(dve):
                chain = [0]

                def link(ins):
                    chain[0] += 1
                    ins.then_inc(s_chain, 1)
                    dve.wait_ge(s_chain, chain[0])

                def rsqrt(y, a, t, rounds=3):
                    link(dve.tensor_scalar(a.bitcast(I32), t.bitcast(I32), 1, None, ALU.logical_shift_right))
                    link(dve.tensor_scalar(y.bitcast(I32), a.bitcast(I32), -1, RSQRT_GUESS, ALU.mult, ALU.add))
                    for _ in range(rounds):
                        link(dve.scalar_tensor_tensor(out=a, in0=y, scalar=-0.5, in1=y, op0=ALU.mult, op1=ALU.mult))
                        link(dve.tensor_tensor(a, a, t, ALU.mult))
                        link(dve.scalar_tensor_tensor(out=y, in0=a, scalar=1.5, in1=y, op0=ALU.add, op1=ALU.mult))

                def power(dst, src, which):
                    a = tiny[:, 0:1].bitcast(I32)
                    link(dve.tensor_scalar(a, src.bitcast(I32), 23, None, ALU.logical_shift_right))
                    link(dve.tensor_scalar(a, a, 131, None, ALU.add))
                    link(dve.tensor_scalar(a, a, 1, None, ALU.logical_shift_right))
                    b = tiny[:, 1:2].bitcast(I32)
                    link(dve.tensor_scalar(b, a, -1, 259, ALU.mult, ALU.add))
                    link(dve.tensor_scalar(dst.bitcast(I32), b, 23, None, ALU.logical_shift_left))
                    link(dve.tensor_scalar(a, a, -5, None, ALU.add))
                    link(dve.tensor_scalar(unscale[:, which:which + 1].bitcast(I32), a, 23, None, ALU.logical_shift_left))

                def normalise(c, between=None):
                    dve.wait_ge(s_x[c % 2], 16 * (c // 2 + 1))
                    rows = xc[:, c % 2, :].rearrange("p (t h) -> p t h", h=HID)
                    for t in range(LN_CHUNK):
                        ins = dve.bn_stats(stats[:, t, :], rows[:, t, :])
                    link(ins)
                    for t in range(LN_CHUNK):
                        ins = dve.bn_aggr(mv[:, t, :], stats[:, t, :])
                    link(ins)
                    link(dve.tensor_scalar(t_ln[:, :], mv[:, :, 1], LN_EPS, None, ALU.add))
                    rsqrt(y_ln[:, :], a_ln[:, :], t_ln[:, :])
                    if between:
                        between()
                    for t in range(LN_CHUNK):
                        n = c * LN_CHUNK + t
                        if n >= 2 * TBANKS:
                            dve.wait_ge(s_xt, n // 2 - TBANKS + 1)
                        dve.tensor_scalar(xn[:, n % (2 * TBANKS), :], rows[:, t, :], mv[:, t, 0:1], y_ln[:, t:t + 1],
                                          ALU.subtract, ALU.mult).then_inc(s_xn, 1)
                        if t % 2 and n > 3:
                            x_lo(n // 2 - 2)

                def x_lo(m):
                    dve.wait_ge(s_xhi, m + 1)
                    view = xT[:, :, :].rearrange("p s (k n) -> p s k n", k=KH)
                    dve.tensor_tensor(view[:, 1, :, m * PAIR:(m + 1) * PAIR],
                                      ps_t[m % TBANKS][:, :].rearrange("p (k n) -> p k n", k=KH),
                                      view[:, 0, :, m * PAIR:(m + 1) * PAIR], ALU.subtract).then_inc(s_xlo, 1)

                def top(i, which):
                    dve.wait_ge(s_wnorm, i + 1)
                    n = WIDE if which != O else 512
                    dve.tensor_reduce(peak[:, i:i + 1], ps_n[:, 0:n], AX_X, ALU.max).then_inc(s_peak, 1)
                    dve.wait_ge(s_peak, i + 1)
                    if which in (QK, V):
                        bias = peak[:, 6 + which:7 + which]
                        link(dve.tensor_tensor(peak[:, i:i + 1], peak[:, i:i + 1], bias, ALU.add))
                    link(dve.tensor_scalar(peak[:, i:i + 1], peak[:, i:i + 1], 1e-30, None, ALU.max))
                    power(scale[:, which:which + 1], peak[:, i:i + 1], which)
                    dve.nop().then_inc(s_scale, 1)

                def split_lo(j):
                    _, dst, which = RAWS[j]
                    dve.wait_ge(s_whi, j + 1)
                    dve.scalar_tensor_tensor(out=dst[:, 1, :], in0=raw[:, j % RING, :], scalar=scale[:, which:which + 1],
                                             in1=dst[:, 0, :], op0=ALU.mult, op1=ALU.subtract).then_inc(s_wlo[j], 1)

                normalise(0)
                dve.wait_ge(s_bnorm, 1)
                link(dve.tensor_reduce(peak[:, 6:7], ps_s[:, 0:2 * HEADS], AX_X, ALU.max))
                link(dve.tensor_reduce(peak[:, 7:8], ps_s[:, 2 * HEADS:3 * HEADS], AX_X, ALU.max))
                dve.tensor_reduce(peak[:, 5:6], ps_s[:, 3 * HEADS:5 * HEADS], AX_X, ALU.max).then_inc(s_bread, 1)
                dve.wait_ge(s_bread, 1)
                link(dve.tensor_scalar(peak[:, 5:6], peak[:, 5:6], 2.0, 1e-30, ALU.mult, ALU.max))
                power(scale[:, B:B + 1], peak[:, 5:6], B)
                link(dve.tensor_scalar(wb_s[:, 0, :], wb_raw[:, :], scale[:, B:B + 1], None, ALU.mult))
                link(dve.scalar_tensor_tensor(out=wb_s[:, 1, :], in0=wb_raw[:, :], scalar=scale[:, B:B + 1],
                                              in1=wb_s[:, 0, :], op0=ALU.mult, op1=ALU.subtract))
                normalise(1)
                top(0, QK)
                link(dve.tensor_scalar(tiny[:, 2:3], scale[:, QK:QK + 1], L2_EPS, None, ALU.mult))
                link(dve.tensor_tensor(eps_sq[:, :], tiny[:, 2:3], tiny[:, 2:3], ALU.mult))
                link(dve.tensor_scalar(bq_c[:, :], bq_c[:, :], scale[:, QK:QK + 1], None, ALU.mult))
                link(dve.tensor_scalar(bk_c[:, :], bk_c[:, :], scale[:, QK:QK + 1], None, ALU.mult))
                dve.wait_ge(s_fsum, 1)
                link(dve.tensor_scalar(fmean[:, :], ps_s[:, FSUM_AT], 1.0 / (FFN * HID), 1e-5, ALU.mult, ALU.max))
                link(dve.tensor_scalar(thr[:, :], fmean[:, :], 0.7, None, ALU.mult))
                link(dve.tensor_scalar(nthr[:, :], thr[:, :], -1.0, None, ALU.mult))
                for i, (w, dst) in enumerate(((wfc_r[:, :], wfc_t), (wpr_r, wpr_t))):
                    link(dve.tensor_scalar(dst[:, :], w, nthr[:, i:i + 1], None, ALU.is_lt))
                    link(dve.scalar_tensor_tensor(out=dst[:, :], in0=w, scalar=thr[:, i:i + 1], in1=dst[:, :],
                                                  op0=ALU.is_gt, op1=ALU.subtract))
                dve.nop().then_inc(s_tern, 1)
                link(dve.tensor_scalar(wfc_t[:, :], wfc_t[:, :], 0.25, None, ALU.mult))
                link(dve.scalar_tensor_tensor(out=ffn_unscale[:, :], in0=fmean[:, 0:1], scalar=16.0, in1=fmean[:, 0:1],
                                              op0=ALU.mult, op1=ALU.mult))
                link(dve.tensor_tensor(ffn_unscale[:, :], ffn_unscale[:, :], fmean[:, 1:2], ALU.mult))
                top(1, V)
                split_lo(0)
                normalise(2)
                normalise(3, lambda: top(2, G))
                x_lo(PAIRS - 2)
                x_lo(PAIRS - 1)
                top(3, O)
                dve.wait_ge(s_wide, NWIDE)
                dve.wait_ge(s_z, 1)
                z3 = z.rearrange("p (t h) -> p t h", h=HEADS)
                bb3 = bb_b[:, :].unsqueeze(1).broadcast_to((P, NTILE, HEADS))
                dve.scalar_tensor_tensor(out=z3, in0=ps_s.rearrange("p (t h) -> p t h", h=HEADS),
                                         scalar=unscale[:, B:B + 1], in1=bb3, op0=ALU.mult, op1=ALU.add).then_inc(s_beta, 1)
                dve.wait_ge(s_bact, 2)
                dve.tensor_scalar(uz, ez, 1.0, None, ALU.add).then_inc(s_beta, 1)
                b2 = beta[:, :, :].rearrange("p t h -> p (t h)")
                dve.wait_ge(s_beta, 2)
                link(dve.tensor_scalar(b2, uz, -1.0, 1e-30, ALU.add, ALU.max))
                link(dve.reciprocal(b2, b2))
                link(dve.tensor_tensor(b2, b2, ez, ALU.mult))
                split_lo(RAW_MATRICES - 1)
                dve.wait_ge(s_bact, 3)
                link(dve.tensor_tensor(b2, b2, lz, ALU.mult))
                link(dve.tensor_scalar(uz, uz, 1.0, None, ALU.is_equal))
                link(dve.tensor_tensor(uz, uz, ez, ALU.mult))
                link(dve.tensor_tensor(b2, b2, uz, ALU.add))
                link(dve.scalar_tensor_tensor(out=b2, in0=z, scalar=0.0, in1=b2, op0=ALU.max, op1=ALU.add))
                dve.tensor_reduce(tiny[:, 3:4], b2, AX_X, ALU.max).then_inc(s_bt, 1)
                dve.wait_ge(s_bt, 2)
                dve.tensor_reduce(tiny[0:1, 4:5], ps_t[0][0:1, 0:P], AX_X, ALU.max).then_inc(s_bt, 1)
                dve.wait_ge(s_bt, 4)
                a = tiny[:, 5:6].bitcast(I32)
                link(dve.tensor_scalar(tiny[:, 6:7], ps_t[1][:, 0:1], 1e-30, None, ALU.max))
                link(dve.tensor_scalar(a, tiny[:, 6:7].bitcast(I32), 23, None, ALU.logical_shift_right))
                link(dve.tensor_scalar(tiny[:, 0:1].bitcast(I32), a, -1, 253, ALU.mult, ALU.add))
                link(dve.tensor_scalar(tiny[:, 1:2].bitcast(I32), tiny[:, 0:1].bitcast(I32), 23, None, ALU.logical_shift_left))
                link(dve.tensor_scalar(b2, b2, tiny[:, 1:2], None, ALU.mult))
                link(dve.tensor_scalar(a, a, 1, None, ALU.add))
                link(dve.tensor_scalar(tiny[:, 2:3].bitcast(I32), a, 23, None, ALU.logical_shift_left))
                link(dve.tensor_scalar(gate_k[:, :], scale[:, G:G + 1], 2.0 ** -15, None, ALU.mult))
                link(dve.scalar_tensor_tensor(out=out_unscale[:, :], in0=unscale[:, V:V + 1], scalar=2.0 ** 8,
                                              in1=unscale[:, G:G + 1], op0=ALU.mult, op1=ALU.mult))
                link(dve.tensor_tensor(out_unscale[:, :], out_unscale[:, :], unscale[:, O:O + 1], ALU.mult))
                link(dve.tensor_tensor(out_unscale[:, :], out_unscale[:, :], tiny[:, 2:3], ALU.mult))

            @block.tensor
            def _(pe):
                pe.wait_ge(s_const, 8)

                def transposes(first, last):
                    for m in range(first, last):
                        pe.wait_ge(s_xn, 2 * m + 2)
                        if m >= TBANKS:
                            pe.wait_ge(s_xhi, m - TBANKS + 1)
                            pe.wait_ge(s_xlo, m - TBANKS + 1)
                        for k in range(KH):
                            for t in range(2):
                                last_t = pe.transpose(ps_t[m % TBANKS][:, k * PAIR + t * P:k * PAIR + (t + 1) * P],
                                                      xn[:, (2 * m + t) % (2 * TBANKS), k * P:(k + 1) * P], ident[:, :])
                        last_t.then_inc(s_xt, 1)

                def norms(i):
                    together = NORMS[i]
                    pe.wait_ge(s_wsq, together[-1] + 1)
                    if i:
                        pe.wait_ge(s_peak, i)
                    if RAWS[together[0]][2] != O:
                        for n in range(WIDE // 512):
                            tiles = [(j, k) for j in together for k in range(KH)]
                            for j, k in tiles:
                                last = pe.matmul(ps_n[:, n * 512:(n + 1) * 512], ones_bf[:, :],
                                                 squares(j)[:, k * WIDE + n * 512:k * WIDE + (n + 1) * 512],
                                                 start=((j, k) == tiles[0]), stop=((j, k) == tiles[-1]))
                    else:
                        for n in range(HEADS // 2):
                            last = pe.matmul(ps_n[:, 0:512], ones_bf[:, :], squares(together[0])[:, n * 512:(n + 1) * 512],
                                             start=(n == 0), stop=(n == HEADS // 2 - 1))
                    last.then_inc(s_wnorm, 1)

                def beta_rows(first, last):
                    pe.wait_ge(s_xhi, last // 2)
                    pe.wait_ge(s_xlo, last // 2)
                    pe.wait_ge(s_tern, 1)
                    for t in range(first, last):
                        n = 0
                        for k in range(KH):
                            for a, b in ((0, 0), (0, 1), (1, 0)):
                                ins = pe.matmul(ps_s[:, t * HEADS:(t + 1) * HEADS],
                                                xT[:, a, k * TOK + t * P:k * TOK + (t + 1) * P],
                                                wb_s[:, b, k * HEADS:(k + 1) * HEADS], start=(n == 0), stop=(n == 5))
                                n += 1
                    if last == NTILE:
                        ins.then_inc(s_z, 1)

                pe.wait_ge(s_bsq, 4)
                pe.matmul(ps_s[:, 0:5 * HEADS], ones_bf[:, :], b_sq[:, :], start=True, stop=True).then_inc(s_bnorm, 1)
                transposes(0, 4)
                norms(0)
                transposes(4, 8)
                pe.wait_ge(s_abs, 2)
                pe.wait_ge(s_bread, 1)
                pe.matmul(ps_s[:, FSUM_AT], ones_f[:, :], fsum[:, :], start=True, stop=True).then_inc(s_fsum, 1)
                norms(1)
                transposes(8, 12)
                norms(2)
                beta_rows(0, NTILE // 2)
                transposes(12, 16)
                norms(3)
                beta_rows(NTILE // 2, NTILE)
                pe.wait_ge(s_bt, 1)
                pe.transpose(ps_t[0][0:1, 0:P], tiny[:, 3:4], ident[:, :]).then_inc(s_bt, 1)
                pe.wait_ge(s_bt, 3)
                pe.matmul(ps_t[1][:, 0:1], ones_f[0:1, :], tiny[0:1, 4:5], start=True, stop=True).then_inc(s_bt, 1)

        late = whole.enter_context(ExitStack())
        rows = sb("rows", [P, TILES * HID], F32, late)
        normed = sb("normed", [P, TILES * HID], F32, late)
        st2 = sb("st2", [P, TILES, 6], F32, late)
        mv2 = sb("mv2", [P, TILES, 2], F32, late)
        t2 = sb("t2", [P, TILES], F32, late)
        a2 = sb("a2", [P, TILES], F32, late)
        y2 = sb("y2", [P, TILES], F32, late)
        pause = sb("pause", [P, 1], F32, late)
        s_mid = sem("s_mid", late)
        s_ln2 = sem("s_ln2", late)
        s_kept = sem("s_kept", late)
        s_nkept = sem("s_nkept", late)

        STATS, LINKS = TILES, 13
        LN2_STEPS = STATS + LINKS + TILES

        def ln2(dve, step, m):
            i = step - STATS
            if i >= 0:
                dve.wait_ge(s_ln2, LN2_STEPS * m + min(step, STATS + LINKS))
            if i < 0:
                ins = dve.bn_stats(st2[:, step, :], rows[:, step * HID:(step + 1) * HID])
            elif i == 0:
                dve.memset(pause[:, :], 0.0)
                for t in range(TILES):
                    ins = dve.bn_aggr(mv2[:, t, :], st2[:, t, :])
            elif i == 1:
                ins = dve.tensor_scalar(t2[:, :], mv2[:, :, 1], LN_EPS, None, ALU.add)
            elif i == 2:
                ins = dve.tensor_scalar(a2[:, :].bitcast(I32), t2[:, :].bitcast(I32), 1, None, ALU.logical_shift_right)
            elif i == 3:
                ins = dve.tensor_scalar(y2[:, :].bitcast(I32), a2[:, :].bitcast(I32), -1, RSQRT_GUESS, ALU.mult, ALU.add)
            elif i < LINKS and i % 3 == 1:
                ins = dve.scalar_tensor_tensor(out=a2[:, :], in0=y2[:, :], scalar=-0.5, in1=y2[:, :],
                                               op0=ALU.mult, op1=ALU.mult)
            elif i < LINKS and i % 3 == 2:
                ins = dve.tensor_tensor(a2[:, :], a2[:, :], t2[:, :], ALU.mult)
            elif i < LINKS:
                ins = dve.scalar_tensor_tensor(out=y2[:, :], in0=a2[:, :], scalar=1.5, in1=y2[:, :],
                                               op0=ALU.add, op1=ALU.mult)
            else:
                t = i - LINKS
                ins = dve.tensor_scalar(normed[:, t * HID:(t + 1) * HID], rows[:, t * HID:(t + 1) * HID],
                                        mv2[:, t, 0:1], y2[:, t:t + 1], ALU.subtract, ALU.mult)
            ins.then_inc(s_ln2, 1)

        with ExitStack() as part:
            q_s = sb("q_s", [P, 2, 2, BLK], F16, part)
            k_s = sb("k_s", [P, 2, 2, BLK], F16, part)
            q_sq = sb("q_sq", [P, 2, BLK], F32, part)
            k_sq = sb("k_sq", [P, 2, BLK], F32, part)
            q_sl = sb("q_sl", [P, 2, BLK], F16, part)
            k_sl = sb("k_sl", [P, 2, BLK], F16, part)
            v_f = sb("v_f", [P, GW], F32, part)
            v_s = sb("v_s", [P, 2, 2 * TILES * GW], F16, part)
            gate = sb("gate", [P, 2 * TILES * GW], F32, part)
            pr_f = sb("pr_f", [P, BLK], F32, part)
            pr_s = sb("pr_s", [P, 2, 2, BLK], F16, part)
            og = sb("og", [P, BLK], F32, part)
            ogT = sb("ogT", [P, 2, 2, BLK], F16, part)
            t_n = sb("t_n", [P, 8], F32, part)
            a_n = sb("a_n", [P, 8], F32, part)
            y_n = sb("y_n", [P, 8], F32, part)
            c_k = sb("c_k", [P, 2, TILES], F32, part)
            c_q = sb("c_q", [P, 2, TILES], F32, part)

            ps_qv = pb("ps_qv", [P, 512], part)
            ps_kg = pb("ps_kg", [P, 512], part)
            ps_sc = pb("ps_sc", [P, 512], part)
            ps_nm = pb("ps_nm", [P, 512], part)
            ps_pv = pb("ps_pv", [P, 512], part)
            ps_tr = pb("ps_tr", [P, 512], part)
            ps_acc = pb("ps_acc", [P, TILES * HID], part)

            s_q = sem("s_q", part)
            s_k = sem("s_k", part)
            s_v = sem("s_v", part)
            s_g = sem("s_g", part)
            s_score = sem("s_score", part)
            s_norm = sem("s_norm", part)
            s_pv = sem("s_pv", part)
            s_tr = sem("s_tr", part)
            s_acc = sem("s_acc", part)
            s_qhi = sem("s_qhi", part)
            s_khi = sem("s_khi", part)
            s_qsq = sem("s_qsq", part)
            s_ksq = sem("s_ksq", part)
            s_vhi = sem("s_vhi", part)
            s_gate = sem("s_gate", part)
            s_phi = sem("s_phi", part)
            s_ohi = sem("s_ohi", part)
            s_qlo = sem("s_qlo", part)
            s_klo = sem("s_klo", part)
            s_vf = sem("s_vf", part)
            s_newton = sem("s_newton", part)
            s_p = sem("s_p", part)
            s_og = sem("s_og", part)
            s_olo = sem("s_olo", part)
            s_qsl = sem("s_qsl", part)
            s_ksl = sem("s_ksl", part)
            s_vlo = sem("s_vlo", part)
            s_plo = sem("s_plo", part)
            s_bias = sem("s_bias", part)
            s_rows = sem("s_rows", part)

            PARTS = ((0, 0), (0, 1), (1, 0))
            NBLK_GROUPS = HEADS // GROUP

            def where(b, hg, s):
                g = NBLK_GROUPS * b + hg
                return GROUP * g + s, g

            def group_ahead(b, hg, s):
                if s < 2:
                    return b, hg
                return (b, hg + 1) if hg + 1 < NBLK_GROUPS else (b + 1, 0)

            def back(b, hg, s, lag):
                pos = GROUP * hg + s - lag
                g = NBLK_GROUPS * b + hg
                if pos < 0:
                    return b - 1, pos + HEADS, g - 1, (s - lag) % GROUP
                return b, pos, g if s >= lag else g - 1, (s - lag) % GROUP

            def walk(eng, slot, finish):
                slots = [(hg, s) for hg in range(NBLK_GROUPS) for s in range(GROUP)]
                for hg, s in slots:
                    slot(0, hg, s)
                for hg, s in slots[:GROUP]:
                    slot(1, hg, s)
                with eng.Fori(1, NBLK - 1) as b:
                    for hg, s in slots[GROUP:]:
                        slot(b, hg, s)
                    for hg, s in slots[:GROUP]:
                        slot(b + 1, hg, s)
                for hg, s in slots[GROUP:]:
                    slot(NBLK - 1, hg, s)
                for s in range(3):
                    slot(NBLK, 0, s)
                finish()

            def live(u, lag):
                return not isinstance(u, int) or 0 <= u - lag < UNITS

            block = part.enter_context(nc.Block())

            @block.tensor
            def _(pe):
                def wide_tile(ps, wt, t, blk, hg, done):
                    n = 0
                    for k in range(KH):
                        for a, c in PARTS:
                            last = pe.matmul(ps[:, :], xT[:, a, ds(blk * BLK + (k * TOK + t * P), P)],
                                             wcol(wt, c, k, hg * GW, GW), start=(n == 0), stop=(n == 5))
                            n += 1
                    last.then_inc(done, 1)

                def values(w, t, blk, hg):
                    if not low(w - 1):
                        pe.wait_ge(s_qlo, w - 1)
                        pe.wait_ge(s_qsq, w - 1)
                    if not low(w):
                        pe.wait_ge(s_vf, w)
                    wide_tile(ps_qv, wv_s, t, blk, hg, s_v)

                def gates(w, t, blk, hg):
                    if not low(w - 1):
                        pe.wait_ge(s_klo, w - 1)
                        pe.wait_ge(s_ksq, w - 1)
                    if not low(w):
                        pe.wait_ge(s_gate, w)
                    wide_tile(ps_kg, wg_s, t, blk, hg, s_g)

                def slot(b, hg, s):
                    u, g = where(b, hg, s)
                    par = s % 2
                    if live(u, 0):
                        head = (hg * GROUP + s) * P
                        row = b * BLK
                        for ps, wt, done, freed in ((ps_qv, wq_s, s_q, s_vf), (ps_kg, wk_s, s_k, s_gate)):
                            if live(u, -1):
                                pe.wait_ge(freed, u + 2)
                            else:
                                pe.wait_ge(freed, UNITS)
                            n = 0
                            for k in range(KH):
                                for a, c in PARTS:
                                    last = pe.matmul(ps[:, :], wcol(wt, a, k, head, P),
                                                     xT[:, c, ds(row + k * TOK, BLK)], start=(n == 0), stop=(n == 5))
                                    n += 1
                            last.then_inc(done, 1)
                    if live(u, 1):
                        prev = (s - 1) % 2
                        pe.wait_ge(s_qhi, u)
                        pe.wait_ge(s_khi, u)
                        pe.wait_ge(s_qlo, u)
                        pe.wait_ge(s_klo, u)
                        if not low(u - 1):
                            pe.wait_ge(s_p, u - 1)
                        for t in range(TILES):
                            for n, (a, c) in enumerate(PARTS):
                                last = pe.matmul(ps_sc[:, t * P:(t + 1) * P], k_s[:, prev, a, t * P:(t + 1) * P],
                                                 q_s[:, prev, c, t * P:(t + 1) * P], start=(n == 0), stop=(n == 2))
                        last.then_inc(s_score, 1)
                        pe.wait_ge(s_qsl, u)
                        pe.wait_ge(s_ksl, u)
                        if not low(u - 1):
                            pe.wait_ge(s_newton, NORM_STEPS * (u - 1))
                        for i, (sq, sl) in enumerate(((q_sq, q_sl), (k_sq, k_sl))):
                            for t in range(TILES):
                                o = ps_nm[:, i * TILES + t:i * TILES + t + 1]
                                pe.matmul(o, sq[:, prev, t * P:(t + 1) * P].bitcast(BF16)[:, 1::2], ones16[:, 0:1],
                                          start=True, stop=False)
                                last = pe.matmul(o, sl[:, prev, t * P:(t + 1) * P], ones16[:, 0:1],
                                                 start=False, stop=True)
                        last.then_inc(s_norm, 1)
                    if live(u, -2):
                        values(u + 2, (s + 2) % TILES, *group_ahead(b, hg, s))
                    if live(u, 2):
                        _, head, grp, hh = back(b, hg, s, 2)
                        pe.wait_ge(s_phi, u - 1)
                        pe.wait_ge(s_plo, u - 1)
                        pe.wait_ge(s_vhi, GROUP * grp + GROUP)
                        pe.wait_ge(s_vlo, GROUP * grp + GROUP)
                        if not low(u - 2):
                            pe.wait_ge(s_og, u - 2)
                        at = (head // GROUP % 2) * (TILES * GW)
                        for t in range(TILES):
                            for n, (a, c) in enumerate(PARTS):
                                last = pe.matmul(ps_pv[:, t * P:(t + 1) * P], pr_s[:, par, a, t * P:(t + 1) * P],
                                                 v_s[:, c, ds(at + (t * GW + hh * P), P)], start=(n == 0), stop=(n == 2))
                        last.then_inc(s_pv, 1)
                    if live(u, -2):
                        gates(u + 2, (s + 2) % TILES, *group_ahead(b, hg, s))
                    if live(u, 3):
                        blk, head, _, _ = back(b, hg, s, 3)
                        pe.wait_ge(s_ohi, u - 2)
                        pe.wait_ge(s_olo, u - 2)
                        first = head == 0
                        final = head == HEADS - 1
                        if first and not low(blk):
                            pe.wait_ge(s_mid, blk)
                        prev = (s - 3) % 2
                        for t in range(TILES):
                            for n, (a, c) in enumerate(PARTS):
                                last = pe.matmul(ps_acc[:, t * HID:(t + 1) * HID], ogT[:, prev, a, t * P:(t + 1) * P],
                                                 wo_s[:, c, ds(head * HID, HID)],
                                                 start=(first and n == 0 and t % 2 == 0), stop=(final and n == 2),
                                                 skip_group_check=True)
                        last.then_inc(s_acc, 1)
                    if live(u, 2):
                        pe.wait_ge(s_og, u - 1)
                        if not low(u - 2):
                            pe.wait_ge(s_olo, u - 2)
                            pe.wait_ge(s_ohi, u - 2)
                        for t in range(TILES):
                            last = pe.transpose(ps_tr[:, t * P:(t + 1) * P], og[:, t * P:(t + 1) * P], ident[:, :])
                        last.then_inc(s_tr, 1)

                for t in range(2):
                    values(t, t, 0, 0)
                    gates(t, t, 0, 0)
                walk(pe, slot, lambda: None)

            @block.scalar
            def _(act):
                def values(w, t, blk, hg):
                    at = (hg % 2) * (TILES * GW) + t * GW
                    act.wait_ge(s_vf, w + 1)
                    if not low(w - 4):
                        act.wait_ge(s_pv, w - 4)
                    act.activation(v_s[:, 0, ds(at, GW)], v_f[:, :], ACT.Copy).then_inc(s_vhi, 1)
                    act.wait_ge(s_g, w + 1)
                    if not low(w - 4):
                        act.wait_ge(s_og, w - 4)
                    act.activation(gate[:, ds(at, GW)], ps_kg[:, :], ACT.Silu, scale=unscale[:, G:G + 1]).then_inc(s_gate, 1)

                def projection(u, par, head, done, ps, bias, dst, sq, hi, sqd):
                    if not live(u, 0):
                        return
                    act.wait_ge(done, u + 1)
                    if not low(u - 1):
                        act.wait_ge(s_score, u - 1)
                    act.activation(dst[:, par, 0, :], ps[:, :], ACT.Identity, bias=bias[:, head:head + 1]).then_inc(hi, 1)
                    if not low(u - 1):
                        act.wait_ge(s_norm, u - 1)
                    act.activation(sq[:, par, :], ps[:, :], ACT.Square, bias=bias[:, head:head + 1]).then_inc(sqd, 1)

                def slot(b, hg, s):
                    u, g = where(b, hg, s)
                    par = s % 2
                    if live(u, 3):
                        act.wait_ge(s_tr, u - 2)
                        if not low(u - 3):
                            act.wait_ge(s_acc, u - 3)
                        act.activation(ogT[:, (s - 3) % 2, 0, :], ps_tr[:, :], ACT.Copy).then_inc(s_ohi, 1)
                    projection(u, par, hg * GROUP + s, s_q, ps_qv, bq_c, q_s, q_sq, s_qhi, s_qsq)
                    if live(u, 2):
                        act.wait_ge(s_p, u - 1)
                        if not low(u - 3):
                            act.wait_ge(s_pv, u - 3)
                        act.activation(pr_s[:, par, 0, :], pr_f[:, :], ACT.Copy).then_inc(s_phi, 1)
                    projection(u, par, hg * GROUP + s, s_k, ps_kg, bk_c, k_s, k_sq, s_khi, s_ksq)
                    if live(u, -2):
                        values(u + 2, (s + 2) % TILES, *group_ahead(b, hg, s))

                values(0, 0, 0, 0)
                values(1, 1, 0, 0)
                walk(act, slot, lambda: None)

            @block.vector
            def _(dve):
                def values(w, t, blk, hg):
                    col = hg * GW
                    dve.wait_ge(s_v, w + 1)
                    if not low(w):
                        dve.wait_ge(s_vhi, w)
                        dve.wait_ge(s_vlo, w)
                    dve.tensor_tensor(v_f[:, :], ps_qv[:, :], bv_b[:, ds(col, GW)], ALU.add).then_inc(s_vf, 1)

                def newton(step, u, prev, blk, head):
                    if step == 0:
                        dve.wait_ge(s_norm, u)
                        if not low(u - 1):
                            dve.wait_ge(s_newton, NORM_STEPS * (u - 1))
                        ins = dve.tensor_scalar(t_n[:, :], ps_nm[:, 0:8], 1.0 / P, eps_sq[:, :], ALU.mult, ALU.max)
                    else:
                        dve.wait_ge(s_newton, NORM_STEPS * (u - 1) + step)
                    if step == 1:
                        ins = dve.tensor_scalar(a_n[:, :].bitcast(I32), t_n[:, :].bitcast(I32), 1, None,
                                                ALU.logical_shift_right)
                    if step == 2:
                        ins = dve.tensor_scalar(y_n[:, :].bitcast(I32), a_n[:, :].bitcast(I32), -1, RSQRT_GUESS,
                                                ALU.mult, ALU.add)
                    if step in (3, 6, 9):
                        ins = dve.scalar_tensor_tensor(out=a_n[:, :], in0=y_n[:, :], scalar=-0.5, in1=y_n[:, :],
                                                       op0=ALU.mult, op1=ALU.mult)
                    if step in (4, 7, 10):
                        ins = dve.tensor_tensor(a_n[:, :], a_n[:, :], t_n[:, :], ALU.mult)
                    if step in (5, 8, 11):
                        ins = dve.scalar_tensor_tensor(out=y_n[:, :], in0=a_n[:, :], scalar=1.5, in1=y_n[:, :],
                                                       op0=ALU.add, op1=ALU.mult)
                    if step == 12:
                        ins = dve.tensor_tensor(c_k[:, prev, :].unsqueeze(2), y_n[:, TILES:2 * TILES].unsqueeze(2),
                                                beta[:, ds(blk * TILES, TILES), ds(head, 1)], ALU.mult)
                    if step == 13:
                        ins = dve.tensor_scalar(c_q[:, prev, :], y_n[:, 0:TILES], gate_k[:, :], None, ALU.mult)
                    ins.then_inc(s_newton, 1)

                def output_tile(t, u, par, head):
                    at = (head // GROUP % 2) * (TILES * GW)
                    ins = dve.scalar_tensor_tensor(out=og[:, t * P:(t + 1) * P], in0=ps_pv[:, t * P:(t + 1) * P],
                                                   scalar=c_q[:, par, t:t + 1], in1=gate[:, ds(at + t * GW + head % GROUP * P, P)],
                                                   op0=ALU.mult, op1=ALU.mult)
                    if t == TILES - 1:
                        ins.then_inc(s_og, 1)

                def slot(b, hg, s):
                    u, g = where(b, hg, s)
                    par, prev = s % 2, (s - 1) % 2
                    if live(u, 3):
                        dve.wait_ge(s_ohi, u - 2)
                        if not low(u - 3):
                            dve.wait_ge(s_acc, u - 3)
                        o = ogT[:, (s - 3) % 2, :, :]
                        dve.tensor_tensor(o[:, 1, :], ps_tr[:, :], o[:, 0, :], ALU.subtract).then_inc(s_olo, 1)
                    finished = s == 3 and hg == 0 and not low(b)
                    if finished:
                        rows_out(b, 0)
                    if live(u, 0):
                        head = hg * GROUP + s
                        for ps, bias, dst, hi, sqd, done in (
                            (ps_qv, bq_c, q_s, s_qhi, s_qsq, s_qlo), (ps_kg, bk_c, k_s, s_khi, s_ksq, s_klo),
                        ):
                            dve.wait_ge(hi, u + 1)
                            dve.wait_ge(sqd, u + 1)
                            dve.scalar_tensor_tensor(out=dst[:, par, 1, :], in0=ps[:, :], scalar=bias[:, ds(head, 1)],
                                                     in1=dst[:, par, 0, :], op0=ALU.add, op1=ALU.subtract).then_inc(done, 1)
                            if finished and done is s_qlo:
                                rows_out(b, 1)
                    if live(u, 1):
                        blk, head, _, _ = back(b, hg, s, 1)
                        for step in range(BEFORE_VALUES):
                            newton(step, u, prev, blk, head)
                    if live(u, -2):
                        values(u + 2, (s + 2) % TILES, *group_ahead(b, hg, s))
                    if live(u, 1):
                        for step in range(BEFORE_VALUES, BEFORE_OUTPUT):
                            newton(step, u, prev, blk, head)
                    if live(u, 2):
                        _, out_head, grp, _ = back(b, hg, s, 2)
                        dve.wait_ge(s_pv, u - 1)
                        dve.wait_ge(s_gate, GROUP * grp + GROUP)
                        dve.wait_ge(s_newton, NORM_STEPS * (u - 1))
                        if not low(u - 2):
                            dve.wait_ge(s_tr, u - 2)
                    for t in range(TILES):
                        if live(u, 2):
                            output_tile(t, u, par, out_head)
                        if live(u, 1):
                            newton(BEFORE_OUTPUT + t, u, prev, blk, head)
                    if live(u, 1):
                        fill = []
                        if not (isinstance(b, int) and (b == 0 or b == NBLK)):
                            fill = LN2_AT.get(GROUP * hg + s, ())
                        for i, step in enumerate(range(BEFORE_OUTPUT + TILES, NORM_STEPS)):
                            newton(step, u, prev, blk, head)
                            if i < len(fill):
                                ln2(dve, fill[i], b - 1)
                        dve.wait_ge(s_score, u)
                        dve.wait_ge(s_newton, NORM_STEPS * (u - 1) + 13)
                        if not low(u - 1):
                            dve.wait_ge(s_phi, u - 1)
                            dve.wait_ge(s_plo, u - 1)
                        for t in range(TILES):
                            last = dve.scalar_tensor_tensor(out=pr_f[:, t * P:(t + 1) * P],
                                                            in0=ps_sc[:, t * P:(t + 1) * P], scalar=c_k[:, prev, t:t + 1],
                                                            in1=mask[:, :], op0=ALU.mult, op1=ALU.mult)
                        last.then_inc(s_p, 1)

                BEFORE_VALUES, BEFORE_OUTPUT = 4, 5

                LN2_AT = {GROUP + i // 3: range(i, min(i + 3, LN2_STEPS)) for i in range(0, LN2_STEPS, 3)}

                def rows_out(b, i):
                    if i == 0:
                        dve.wait_ge(s_acc, HEADS * b)
                        dve.wait_ge(s_bias, b)
                    half = slice(i * 512, (i + 1) * 512)
                    ins = dve.scalar_tensor_tensor(out=rows[:, half], in0=ps_acc[:, half], scalar=out_unscale[:, :],
                                                   in1=rows[:, half], op0=ALU.mult, op1=ALU.add)
                    if i == 1:
                        ins.then_inc(s_mid, 1)

                def finish():
                    rows_out(NBLK, 0)
                    rows_out(NBLK, 1)

                values(0, 0, 0, 0)
                values(1, 1, 0, 0)
                walk(dve, slot, finish)

            @block.gpsimd
            def _(pool):
                def values(w, t, blk, hg):
                    at = (hg % 2) * (TILES * GW) + t * GW
                    pool.wait_ge(s_vhi, w + 1)
                    if not low(w - 4):
                        pool.wait_ge(s_pv, w - 4)
                    pool.tensor_tensor(v_s[:, 1, ds(at, GW)], v_f[:, :], v_s[:, 0, ds(at, GW)],
                                       ALU.subtract).then_inc(s_vlo, 1)

                def slot(b, hg, s):
                    u, g = where(b, hg, s)
                    par = s % 2
                    if live(u, 0):
                        for sq, sl, ready, done in ((q_sq, q_sl, s_qsq, s_qsl), (k_sq, k_sl, s_ksq, s_ksl)):
                            pool.wait_ge(ready, u + 1)
                            if not low(u - 1):
                                pool.wait_ge(s_norm, u - 1)
                            pool.tensor_tensor(sl[:, par, :], sq[:, par, :], sq[:, par, :].bitcast(BF16)[:, 1::2],
                                               ALU.subtract).then_inc(done, 1)
                    if live(u, -2):
                        values(u + 2, (s + 2) % TILES, *group_ahead(b, hg, s))
                    if live(u, 1):
                        prev = (s - 1) % 2
                        pool.wait_ge(s_phi, u)
                        if not low(u - 2):
                            pool.wait_ge(s_pv, u - 2)
                        pool.tensor_tensor(pr_s[:, prev, 1, :], pr_f[:, :], pr_s[:, prev, 0, :],
                                           ALU.subtract).then_inc(s_plo, 1)
                    if s == 0 and hg == 0 and not low(b) and live(u, 0):
                        rows_in(b)

                def rows_in(b):
                    pool.wait_ge(s_rows, 16 * b)
                    pool.tensor_tensor(rows[:, :].rearrange("p (t h) -> p t h", h=HID),
                                       rows[:, :].rearrange("p (t h) -> p t h", h=HID),
                                       bo_b[:, :].unsqueeze(1).broadcast_to((P, TILES, HID)), ALU.add).then_inc(s_bias, 1)

                values(0, 0, 0, 0)
                values(1, 1, 0, 0)
                walk(pool, slot, lambda: rows_in(NBLK))

            @block.sync
            def _(sp):
                rows3 = rows[:, :].rearrange("p (t h) -> p t h", h=HID)

                def load(b):
                    sp.dma_start(rows3, x_v[ds(b, 1), :, :, :].rearrange("b p t h -> (b p) t h")).then_inc(s_rows, 16)

                def keep(b):
                    sp.wait_ge(s_mid, b + 1)
                    sp.dma_start(mid[ds(b, 1), :, :].rearrange("b p n -> (b p) n"), rows[:, :]).then_inc(s_kept, 16)
                    sp.wait_ge(s_ln2, LN2_STEPS * b + LN2_STEPS)
                    sp.dma_start(mid_norm[ds(b, 1), :, :].rearrange("b p n -> (b p) n"), normed[:, :]).then_inc(s_nkept, 16)
                    sp.wait_ge(s_kept, 16 * b + 16)
                    sp.wait_ge(s_nkept, 16 * b + 16)

                load(0)
                with sp.Fori(0, NBLK - 1) as b:
                    keep(b)
                    load(b + 1)

        with ExitStack() as part:
            mn = sb("mn", [P, 2, TILES * HID], F32, part)
            yT = sb("yT", [P, 2, 2, KH * BLK], F16, part)
            r_f = sb("r_f", [P, KF, BLK], F32, part)
            h_f = sb("h_f", [P, 2, BLK], F32, part)
            h_s = sb("h_s", [P, 2, 2, KF * BLK], F16, part)
            res = sb("res", [P, 2, TILES * HID], F32, part)

            ps_y = pb("ps_y", [P, KH * BLK], part)
            ps_h = pb("ps_h", [P, 4, BLK], part)
            ps_o = pb("ps_o", [P, TILES * HID], part)

            f_rows = [sem(f"f_rows{i}", part) for i in range(2)]
            f_back = [sem(f"f_back{i}", part) for i in range(2)]
            f_out = [sem(f"f_out{i}", part) for i in range(2)]
            f_t = sem("f_t", part)
            f_thi = sem("f_thi", part)
            f_tlo = sem("f_tlo", part)
            f_h = sem("f_h", part)
            f_relu = sem("f_relu", part)
            f_sq = sem("f_sq", part)
            f_hi = sem("f_hi", part)
            f_lo = sem("f_lo", part)
            f_o = sem("f_o", part)
            f_res = sem("f_res", part)

            def hidden_bank(f, par):
                return (f + par) % 4

            def gap(f, par):
                return 2 if par == 0 and f < 2 else 4

            def steps(step):
                def stages(j):
                    return dict(add=j > 1, out=j > 0, turn=j + 1 < NBLK)

                def run(eng):
                    for j in range(2):
                        step(j, j % 2, **stages(j))
                    with eng.Fori(1, NBLK // 2 - 1) as pair:
                        for i in range(2):
                            step(2 * pair + i, i, **stages(2))
                    for j in range(NBLK - 2, NBLK):
                        step(j, j % 2, **stages(j))
                return run

            block = part.enter_context(nc.Block())

            @block.sync
            def _(sp):
                def rows_of(kept, b):
                    return kept[ds(b, 1), :, :].rearrange("b p n -> (b p) n")

                def load_norm(b, par):
                    if not low(b - 1):
                        sp.wait_ge(f_t, b - 1)
                    sp.dma_start(mn[:, par, :], rows_of(mid_norm, b)).then_inc(f_rows[par], 16)

                def load_back(b, par):
                    sp.dma_start(res[:, par, :], rows_of(mid, b)).then_inc(f_back[par], 16)

                def store(b, par):
                    sp.wait_ge(f_res, b + 1)
                    sp.dma_start(out_v[ds(b, 1), :, :, :].rearrange("b p t h -> (b p) t h"),
                                 res[:, par, :].rearrange("p (t h) -> p t h", h=HID)).then_inc(f_out[par], 16)
                    sp.wait_ge(f_out[par], 16 * ((b - par) // 2 + 1))

                load_norm(0, 0)
                load_norm(1, 1)
                load_back(0, 0)
                load_back(1, 1)
                sp.wait_ge(s_mid, NBLK)
                sp.dma_start(rows_of(mid, NBLK - 1), rows[:, :]).then_inc(s_kept, 16)
                load_norm(2, 0)
                load_norm(3, 1)
                sp.wait_ge(s_ln2, LN2_STEPS * NBLK)
                sp.dma_start(rows_of(mid_norm, NBLK - 1), normed[:, :]).then_inc(s_nkept, 16)
                sp.wait_ge(s_kept, 16 * NBLK)
                sp.wait_ge(s_nkept, 16 * NBLK)
                with sp.Fori(0, NBLK // 2 - 2) as pair:
                    for i in range(2):
                        load_norm(2 * pair + (i + 4), i)
                        store(2 * pair + i, i)
                        load_back(2 * pair + (i + 2), i)
                for b in range(NBLK - 4, NBLK):
                    store(b, b % 2)
                    if b + 2 < NBLK:
                        load_back(b + 2, b % 2)

            @block.tensor
            def _(pe):
                def turn_rows(b, par):
                    pe.wait_ge(f_rows[par], 16 * ((b - par) // 2 + 1))
                    if not low(b):
                        pe.wait_ge(f_thi, b)
                        pe.wait_ge(f_tlo, b)
                    for k in range(KH):
                        for t in range(TILES):
                            last = pe.transpose(ps_y[:, k * BLK + t * P:k * BLK + (t + 1) * P],
                                                mn[:, par, t * HID + k * P:t * HID + (k + 1) * P], ident[:, :])
                    last.then_inc(f_t, 1)

                def hidden(b, par, f):
                    n = KF * b + f
                    if f == 0:
                        pe.wait_ge(f_thi, b + 1)
                        pe.wait_ge(f_tlo, b + 1)
                    if not low(n - gap(f, par) + 1):
                        pe.wait_ge(f_relu, n - gap(f, par) + 1)
                    i = 0
                    for k in range(KH):
                        for a in range(2):
                            last = pe.matmul(ps_h[:, hidden_bank(f, par), :], wfc_t[:, k * FFN + f * P:k * FFN + (f + 1) * P],
                                             yT[:, par, a, k * BLK:(k + 1) * BLK], start=(i == 0), stop=(i == 3))
                            i += 1
                    last.then_inc(f_h, 1)

                def output(b, par):
                    if not low(b):
                        pe.wait_ge(f_res, b)
                    pe.wait_ge(f_hi, KF * b + KF)
                    pe.wait_ge(f_lo, KF * b + KF)
                    for t in range(TILES):
                        i = 0
                        for f in range(KF):
                            for a in range(2):
                                last = pe.matmul(ps_o[:, t * HID:(t + 1) * HID],
                                                 h_s[:, par, a, f * BLK + t * P:f * BLK + (t + 1) * P],
                                                 wpr_t[:, f * HID:(f + 1) * HID], start=(i == 0), stop=(i == 2 * KF - 1))
                                i += 1
                    last.then_inc(f_o, 1)

                def step(j, par, add, out, turn):
                    for f in range(KF):
                        hidden(j, par, f)
                        if turn and f == 2:
                            turn_rows(j + 1, 1 - par)
                    if out:
                        output(j - 1, 1 - par)

                turn_rows(0, 0)
                steps(step)(pe)
                output(NBLK - 1, 1)

            @block.scalar
            def _(act):
                def upper(b, par):
                    act.wait_ge(f_t, b + 1)
                    if not low(b - 1):
                        act.wait_ge(f_h, KF * b - KF)
                    act.activation(yT[:, par, 0, :], ps_y[:, :], ACT.Copy).then_inc(f_thi, 1)

                def relu(b, par, f):
                    n = KF * b + f
                    act.wait_ge(f_h, n + 1)
                    if not low(b):
                        act.wait_ge(f_sq, n - KF + 1)
                    act.activation(r_f[:, f, :], ps_h[:, hidden_bank(f, par), :], ACT.Relu).then_inc(f_relu, 1)

                def square_hi(b, par, f):
                    act.wait_ge(f_relu, KF * b + (f + 1))
                    if f == 0 and not low(b - 1):
                        act.wait_ge(f_o, b - 1)
                    act.activation(h_s[:, par, 0, f * BLK:(f + 1) * BLK], r_f[:, f, :], ACT.Square).then_inc(f_hi, 1)

                def step(j, par, add, out, turn):
                    relu(j, par, 0)
                    for f in range(1, KF):
                        relu(j, par, f)
                        square_hi(j, par, f - 1)
                        if turn and f == 2:
                            upper(j + 1, 1 - par)
                    square_hi(j, par, KF - 1)

                upper(0, 0)
                steps(step)(act)

            @block.vector
            def _(dve):
                def lower(b, par, k):
                    dve.wait_ge(f_thi, b + 1)
                    at = slice(k * BLK, (k + 1) * BLK)
                    ins = dve.tensor_tensor(yT[:, par, 1, at], ps_y[:, at], yT[:, par, 0, at], ALU.subtract)
                    if k == KH - 1:
                        ins.then_inc(f_tlo, 1)

                def square(b, par, f):
                    n = KF * b + f
                    dve.wait_ge(f_relu, n + 1)
                    if not low(n - 1):
                        dve.wait_ge(f_lo, n - 1)
                    dve.tensor_tensor(h_f[:, (f + par) % 2, :], r_f[:, f, :], r_f[:, f, :], ALU.mult).then_inc(f_sq, 1)

                def result(b, par, i):
                    if i == 0:
                        dve.wait_ge(f_o, b + 1)
                        dve.wait_ge(f_back[par], 16 * ((b - par) // 2 + 1))
                    half = slice(i * 512, (i + 1) * 512)
                    ins = dve.scalar_tensor_tensor(out=res[:, par, half], in0=ps_o[:, half], scalar=ffn_unscale[:, :],
                                                   in1=res[:, par, half], op0=ALU.mult, op1=ALU.add)
                    if i == 1:
                        ins.then_inc(f_res, 1)

                LN2_IN = (0, 1)
                LN2_EACH = -(-LN2_STEPS // (KF * len(LN2_IN)))

                def step(j, par, add, out, turn):
                    if add:
                        for i in range(2):
                            result(j - 2, par, i)
                    for f in range(KF):
                        square(j, par, f)
                        if turn and f < KH:
                            lower(j + 1, 1 - par, f)
                        if isinstance(j, int) and j in LN2_IN:
                            done = (KF * j + f) * LN2_EACH
                            for i in range(done, min(done + LN2_EACH, LN2_STEPS)):
                                ln2(dve, i, NBLK - 1)

                for k in range(KH):
                    lower(0, 0, k)
                steps(step)(dve)
                for b in (NBLK - 2, NBLK - 1):
                    for i in range(2):
                        result(b, b % 2, i)

            @block.gpsimd
            def _(pool):
                def step(j, par, add, out, turn):
                    if not low(j - 1):
                        pool.wait_ge(f_o, j - 1)
                    for f in range(KF):
                        at = slice(f * BLK, (f + 1) * BLK)
                        pool.wait_ge(f_sq, KF * j + (f + 1))
                        pool.wait_ge(f_hi, KF * j + (f + 1))
                        pool.tensor_tensor(h_s[:, par, 1, at], h_f[:, (f + par) % 2, :], h_s[:, par, 0, at],
                                           ALU.subtract).then_inc(f_lo, 1)

                steps(step)(pool)


def kernel(L0_attn_hidden_states, L0_attn_q_w, L0_attn_q_b, L0_attn_k_w, L0_attn_k_b, L0_attn_v_w, L0_attn_v_b,
           L0_attn_a_w, L0_attn_a_b, L0_attn_b_w, L0_attn_b_b, L0_attn_og_w, L0_attn_o_w, L0_attn_o_b,
           L0_ffn_w_fc, L0_ffn_w_proj):
    import numpy as np
    import concourse.bacc as bacc
    from concourse.bass_utils import run_bass_kernel_spmd

    def tiled(w):
        w = np.asarray(w)
        n, c = w.shape
        return np.ascontiguousarray(w.T.reshape(c // P, P, n).transpose(1, 0, 2).reshape(P, c // P * n))

    def columns(b):
        return np.ascontiguousarray(np.asarray(b).reshape(HEADS, P).T)

    shape = L0_attn_hidden_states.shape
    arrays = {
        "x": np.ascontiguousarray(np.asarray(L0_attn_hidden_states).reshape(TOK, HID)),
        "wq": tiled(L0_attn_q_w), "wk": tiled(L0_attn_k_w), "wv": tiled(L0_attn_v_w), "wg": tiled(L0_attn_og_w),
        "wo": tiled(L0_attn_o_w), "wb": tiled(L0_attn_b_w),
        "bq": columns(L0_attn_q_b), "bk": columns(L0_attn_k_b), "bv": columns(L0_attn_v_b),
        "bv_row": np.asarray(L0_attn_v_b), "bb": np.asarray(L0_attn_b_b), "bo": np.asarray(L0_attn_o_b),
        "wfc": tiled(L0_ffn_w_fc), "wpr": tiled(L0_ffn_w_proj),
    }
    nc = bacc.Bacc("TRN2", target_bir_lowering=False, num_devices=1)
    aps = {n: nc.dram_tensor(f"in_{n}", a.shape, mybir.dt.from_np(a.dtype), kind="ExternalInput").ap()
           for n, a in arrays.items()}
    aps["out"] = nc.dram_tensor("out_rows", (TOK, HID), F32, kind="ExternalOutput").ap()
    build(nc, **aps)
    r = run_bass_kernel_spmd(nc, [{f"in_{n}": a for n, a in arrays.items()}], core_ids=[0])
    return r.results[0]["out_rows"].reshape(shape)
```
